# Optimizing a Trainium2 kernel written in Bass

```python
import numpy as np
import jax
import jax.numpy as jnp

def _softmax(x, axis=-1):
    return jax.nn.softmax(x, axis=axis)

def _gelu(x):
    return jax.nn.gelu(x, approximate=True)

def _silu(x):
    return jax.nn.silu(x)

def _sigmoid(x):
    return jax.nn.sigmoid(x)

def _layernorm(x, axis=-1, eps=1e-05):
    m = jnp.mean(x, axis=axis, keepdims=True)
    v = jnp.var(x, axis=axis, keepdims=True)
    return (x - m) / jnp.sqrt(v + eps)

def _scatter_add(tgt, idx, src, axis=0):
    return tgt.at[idx].add(src)

def _segment_sum(src, seg, n):
    return jax.ops.segment_sum(src, seg, n)
kernel_name = 'mk_adaln_d2_jaxref_r8_344745'

def setup_inputs(seed: int=0):
    np.random.seed(seed)
    _w = jnp.asarray

    def _L0_attn_setup():
        import jax, jax.numpy as jnp
        import numpy as np
        D_MODEL = 128
        NUM_HEADS = 16
        DEPTH = D_MODEL // NUM_HEADS
        B, T = (2, 256)

        def _rope(x):
            H = x.shape[1]
            D = x.shape[-1]
            inv_freq = 1.0 / 10000.0 ** (jnp.arange(0, D, 2, dtype=jnp.float32) / D)
            freqs = jnp.arange(H, dtype=jnp.float32)[:, None] * inv_freq[None, :]
            sin = jnp.sin(freqs)[:, None, :]
            cos = jnp.cos(freqs)[:, None, :]
            x1 = x[..., ::2]
            x2 = x[..., 1::2]
            rot = jnp.stack([x1 * cos - x2 * sin, x1 * sin + x2 * cos], axis=-1)
            return rot.reshape(x.shape)
        key = jax.random.key(seed)
        k_x, k_wq, k_bq, k_wf, k_bf = jax.random.split(key, 5)
        lim_qkv = 1.0 / np.sqrt(D_MODEL)
        lim_fc = 1.0 / np.sqrt(D_MODEL)
        return {'x': jax.random.normal(k_x, (B, T, D_MODEL), dtype=jnp.float32), 'w_qkv': jax.random.uniform(k_wq, (D_MODEL, 3 * D_MODEL), jnp.float32, -lim_qkv, lim_qkv), 'b_qkv': jax.random.uniform(k_bq, (3 * D_MODEL,), jnp.float32, -lim_qkv, lim_qkv), 'w_fc': jax.random.uniform(k_wf, (D_MODEL, D_MODEL), jnp.float32, -lim_fc, lim_fc), 'b_fc': jax.random.uniform(k_bf, (D_MODEL,), jnp.float32, -lim_fc, lim_fc)}
    _L0_attn_in = _L0_attn_setup()

    def _L0_ffn_setup():
        import jax, jax.numpy as jnp
        import numpy as np
        H = 128
        I = 88
        E = 64
        TOP_K = 8
        NG = 8
        TOPK_GROUP = 4
        N_SHARED = 2
        ROUTED_SCALE = 2.5
        S_I = I * N_SHARED

        def _route(x, gate_w, gate_bias):
            T = x.shape[0]
            logits = x @ gate_w.T
            scores = jax.nn.sigmoid(logits)
            scores_for_choice = scores + gate_bias[None, :]
            grp = scores_for_choice.reshape(T, NG, E // NG)
            group_scores = jnp.sum(jax.lax.top_k(grp, 2)[0], axis=-1)
            _, gidx = jax.lax.top_k(group_scores, TOPK_GROUP)
            gmask = jnp.zeros((T, NG), dtype=scores.dtype).at[jnp.arange(T)[:, None], gidx].set(1.0)
            emask = jnp.repeat(gmask, E // NG, axis=1)
            masked = jnp.where(emask > 0, scores_for_choice, 0.0)
            _, topk_idx = jax.lax.top_k(masked, TOP_K)
            topk_w = jnp.take_along_axis(scores, topk_idx, axis=1)
            topk_w = topk_w / (jnp.sum(topk_w, axis=-1, keepdims=True) + 1e-20)
            topk_w = topk_w * ROUTED_SCALE
            rw = jnp.zeros((T, E), dtype=scores.dtype).at[jnp.arange(T)[:, None], topk_idx].add(topk_w)
            return rw

        def _mlp(x, gw, uw, dw):
            return jax.nn.silu(x @ gw.T) * (x @ uw.T) @ dw.T
        key = jax.random.key(seed)
        ks = jax.random.split(key, 10)
        sc = 0.02
        return {'hidden_states': jax.random.normal(ks[0], (1, 128, H), dtype=jnp.float32), 'gate_w': sc * jax.random.normal(ks[1], (E, H), dtype=jnp.float32), 'gate_bias': sc * jax.random.normal(ks[2], (E,), dtype=jnp.float32), 'Wg': sc * jax.random.normal(ks[3], (E, I, H), dtype=jnp.float32), 'Wu': sc * jax.random.normal(ks[4], (E, I, H), dtype=jnp.float32), 'Wd': sc * jax.random.normal(ks[5], (E, H, I), dtype=jnp.float32), 'Sg': sc * jax.random.normal(ks[6], (S_I, H), dtype=jnp.float32), 'Su': sc * jax.random.normal(ks[7], (S_I, H), dtype=jnp.float32), 'Sd': sc * jax.random.normal(ks[8], (H, S_I), dtype=jnp.float32)}
    _L0_ffn_in = _L0_ffn_setup()
    _L0_c = _w((lambda *s: np.random.randn(*s).astype(np.float32) * 0.05)(16, 128))
    _L0_wmod = _w((lambda *s: np.random.randn(*s).astype(np.float32) * 0.05)(128, 6 * 128) * 128 ** (-0.5))

    def _L1_attn_setup():
        import jax, jax.numpy as jnp
        import numpy as np
        HEADS = 16
        NU = 1
        EPS = 1e-06

        def dpfp(k):
            x = jax.nn.relu(jnp.concatenate([k, -k], axis=-1))
            x_rolled = jnp.concatenate([jnp.roll(x, i, axis=-1) for i in range(1, NU + 1)], axis=-1)
            x_repeat = jnp.concatenate([x] * NU, axis=-1)
            phi = x_repeat * x_rolled
            return phi / (jnp.sum(phi, axis=-1, keepdims=True) + EPS)
        key = jax.random.key(seed)
        ks = jax.random.split(key, 7)
        S, B, D, H = (512, 4, 128, HEADS)
        scale = 0.02
        return {'x': jax.random.normal(ks[0], (S, B, D), dtype=jnp.float32), 'Wq': jax.random.normal(ks[1], (D, D), dtype=jnp.float32) * scale, 'Wk': jax.random.normal(ks[2], (D, D), dtype=jnp.float32) * scale, 'Wv': jax.random.normal(ks[3], (D, D), dtype=jnp.float32) * scale, 'Wb': jax.random.normal(ks[4], (D, H), dtype=jnp.float32) * scale, 'Wo': jax.random.normal(ks[5], (D, D), dtype=jnp.float32) * scale, 'bo': jnp.zeros((D,), dtype=jnp.float32)}
    _L1_attn_in = _L1_attn_setup()

    def _L1_ffn_setup():
        import jax, jax.numpy as jnp
        import numpy as np
        TOP_K = 2
        key = jax.random.key(seed)
        ks = jax.random.split(key, 5)
        B, T, D, F, E = (2, 256, 128, 512, 8)
        x = jax.random.normal(ks[0], (B, T, D), dtype=jnp.float32)
        router_w = jax.random.normal(ks[1], (D, E + 1), dtype=jnp.float32) * 0.02
        router_b = jax.random.normal(ks[2], (E + 1,), dtype=jnp.float32) * 0.02
        w1 = jax.random.normal(ks[3], (E, D, F), dtype=jnp.float32) * 0.02
        w2 = jax.random.normal(ks[4], (E, F, D), dtype=jnp.float32) * 0.02
        return {'x': x, 'router_w': router_w, 'router_b': router_b, 'w1': w1, 'w2': w2}
    _L1_ffn_in = _L1_ffn_setup()
    _L1_c = _w((lambda *s: np.random.randn(*s).astype(np.float32) * 0.05)(16, 128))
    _L1_wmod = _w((lambda *s: np.random.randn(*s).astype(np.float32) * 0.05)(128, 6 * 128) * 128 ** (-0.5))
    _d = {'L0_attn_x': _L0_attn_in['x'], 'L0_attn_w_qkv': _L0_attn_in['w_qkv'], 'L0_attn_b_qkv': _L0_attn_in['b_qkv'], 'L0_attn_w_fc': _L0_attn_in['w_fc'], 'L0_attn_b_fc': _L0_attn_in['b_fc'], 'L0_ffn_gate_w': _L0_ffn_in['gate_w'], 'L0_ffn_gate_bias': _L0_ffn_in['gate_bias'], 'L0_ffn_Wg': _L0_ffn_in['Wg'], 'L0_ffn_Wu': _L0_ffn_in['Wu'], 'L0_ffn_Wd': _L0_ffn_in['Wd'], 'L0_ffn_Sg': _L0_ffn_in['Sg'], 'L0_ffn_Su': _L0_ffn_in['Su'], 'L0_ffn_Sd': _L0_ffn_in['Sd'], 'L0_c': _L0_c, 'L0_wmod': _L0_wmod, 'L1_attn_Wq': _L1_attn_in['Wq'], 'L1_attn_Wk': _L1_attn_in['Wk'], 'L1_attn_Wv': _L1_attn_in['Wv'], 'L1_attn_Wb': _L1_attn_in['Wb'], 'L1_attn_Wo': _L1_attn_in['Wo'], 'L1_attn_bo': _L1_attn_in['bo'], 'L1_ffn_router_w': _L1_ffn_in['router_w'], 'L1_ffn_router_b': _L1_ffn_in['router_b'], 'L1_ffn_w1': _L1_ffn_in['w1'], 'L1_ffn_w2': _L1_ffn_in['w2'], 'L1_c': _L1_c, 'L1_wmod': _L1_wmod}
    _x0 = _d['L0_attn_x']
    _d['L0_attn_x'] = jax.random.normal(jax.random.fold_in(jax.random.key(seed), 1), (16, 256, 128), dtype=_x0.dtype)
    del _x0
    return _d

def reference(L0_attn_x, L0_attn_w_qkv, L0_attn_b_qkv, L0_attn_w_fc, L0_attn_b_fc, L0_ffn_gate_w, L0_ffn_gate_bias, L0_ffn_Wg, L0_ffn_Wu, L0_ffn_Wd, L0_ffn_Sg, L0_ffn_Su, L0_ffn_Sd, L0_c, L0_wmod, L1_attn_Wq, L1_attn_Wk, L1_attn_Wv, L1_attn_Wb, L1_attn_Wo, L1_attn_bo, L1_ffn_router_w, L1_ffn_router_b, L1_ffn_w1, L1_ffn_w2, L1_c, L1_wmod):

    def _L0_attn_ref(x, w_qkv, b_qkv, w_fc, b_fc):
        import jax, jax.numpy as jnp
        import numpy as np
        D_MODEL = 128
        NUM_HEADS = 16
        DEPTH = D_MODEL // NUM_HEADS
        B, T = (2, 256)

        def _rope(x):
            H = x.shape[1]
            D = x.shape[-1]
            inv_freq = 1.0 / 10000.0 ** (jnp.arange(0, D, 2, dtype=jnp.float32) / D)
            freqs = jnp.arange(H, dtype=jnp.float32)[:, None] * inv_freq[None, :]
            sin = jnp.sin(freqs)[:, None, :]
            cos = jnp.cos(freqs)[:, None, :]
            x1 = x[..., ::2]
            x2 = x[..., 1::2]
            rot = jnp.stack([x1 * cos - x2 * sin, x1 * sin + x2 * cos], axis=-1)
            return rot.reshape(x.shape)
        Bs, Ts, C = x.shape
        H, D = (NUM_HEADS, DEPTH)
        qkv = x @ w_qkv + b_qkv
        qkv = qkv.reshape(Bs, Ts, 3, H, D)
        qkv = jnp.transpose(qkv, (2, 0, 3, 1, 4))
        q, k, v = (qkv[0], qkv[1], qkv[2])
        q = _rope(q)
        k = _rope(k)
        scores = jnp.einsum('bhtd,bhsd->bhts', q, k) / jnp.sqrt(jnp.float32(D))
        attn = jax.nn.softmax(scores, axis=-1)
        out = jnp.einsum('bhts,bhsd->bhtd', attn, v)
        out = jnp.transpose(out, (0, 2, 1, 3)).reshape(Bs, Ts, C)
        return out @ w_fc + b_fc

    def _L0_ffn_ref(hidden_states, gate_w, gate_bias, Wg, Wu, Wd, Sg, Su, Sd):
        import jax, jax.numpy as jnp
        import numpy as np
        H = 128
        I = 88
        E = 64
        TOP_K = 8
        NG = 8
        TOPK_GROUP = 4
        N_SHARED = 2
        ROUTED_SCALE = 2.5
        S_I = I * N_SHARED

        def _route(x, gate_w, gate_bias):
            T = x.shape[0]
            logits = x @ gate_w.T
            scores = jax.nn.sigmoid(logits)
            scores_for_choice = scores + gate_bias[None, :]
            grp = scores_for_choice.reshape(T, NG, E // NG)
            group_scores = jnp.sum(jax.lax.top_k(grp, 2)[0], axis=-1)
            _, gidx = jax.lax.top_k(group_scores, TOPK_GROUP)
            gmask = jnp.zeros((T, NG), dtype=scores.dtype).at[jnp.arange(T)[:, None], gidx].set(1.0)
            emask = jnp.repeat(gmask, E // NG, axis=1)
            masked = jnp.where(emask > 0, scores_for_choice, 0.0)
            _, topk_idx = jax.lax.top_k(masked, TOP_K)
            topk_w = jnp.take_along_axis(scores, topk_idx, axis=1)
            topk_w = topk_w / (jnp.sum(topk_w, axis=-1, keepdims=True) + 1e-20)
            topk_w = topk_w * ROUTED_SCALE
            rw = jnp.zeros((T, E), dtype=scores.dtype).at[jnp.arange(T)[:, None], topk_idx].add(topk_w)
            return rw

        def _mlp(x, gw, uw, dw):
            return jax.nn.silu(x @ gw.T) * (x @ uw.T) @ dw.T
        B, S, _ = hidden_states.shape
        x = hidden_states.reshape(B * S, H)
        rw = _route(x, gate_w, gate_bias)
        expert_out = jax.vmap(lambda gw_, uw_, dw_: _mlp(x, gw_, uw_, dw_))(Wg, Wu, Wd)
        routed = jnp.einsum('eth,te->th', expert_out, rw)
        shared = _mlp(x, Sg, Su, Sd)
        out = (routed + shared).reshape(B, S, H)
        return out

    def _L1_attn_ref(x, Wq, Wk, Wv, Wb, Wo, bo):
        import jax, jax.numpy as jnp
        import numpy as np
        HEADS = 16
        NU = 1
        EPS = 1e-06

        def dpfp(k):
            x = jax.nn.relu(jnp.concatenate([k, -k], axis=-1))
            x_rolled = jnp.concatenate([jnp.roll(x, i, axis=-1) for i in range(1, NU + 1)], axis=-1)
            x_repeat = jnp.concatenate([x] * NU, axis=-1)
            phi = x_repeat * x_rolled
            return phi / (jnp.sum(phi, axis=-1, keepdims=True) + EPS)
        S, B, D = x.shape
        H = HEADS
        dk = D // H
        d_dot = 2 * dk * NU
        q = dpfp((x @ Wq).reshape(S, B, H, dk))
        k = dpfp((x @ Wk).reshape(S, B, H, dk))
        v = (x @ Wv).reshape(S, B, H, dk)
        beta = jax.nn.sigmoid(x @ Wb).reshape(S, B, H, 1)
        W0 = jnp.zeros((B, H, dk, d_dot), dtype=x.dtype)

        def step(W, inputs):
            k_i, v_i, q_i, b_i = inputs
            v_bar = jnp.einsum('bhvk,bhk->bhv', W, k_i)
            W = W + jnp.einsum('bhv,bhk->bhvk', b_i * (v_i - v_bar), k_i)
            y = jnp.einsum('bhvk,bhk->bhv', W, q_i)
            return (W, y.reshape(B, H * dk))
        _, outputs = jax.lax.scan(step, W0, (k, v, q, beta))
        return outputs @ Wo + bo

    def _L1_ffn_ref(x, router_w, router_b, w1, w2):
        import jax, jax.numpy as jnp
        import numpy as np
        TOP_K = 2
        E = w1.shape[0]
        logits = x @ router_w + router_b
        probs = jax.nn.softmax(logits, axis=-1)
        top_v, top_i = jax.lax.top_k(probs, TOP_K)
        gates = jnp.sum(jax.nn.one_hot(top_i, E + 1, dtype=x.dtype) * top_v[..., None], axis=-2)
        h = jax.nn.gelu(jnp.einsum('btd,edf->ebtf', x, w1), approximate=False)
        y = jnp.einsum('ebtf,efd->ebtd', h, w2)
        out = jnp.einsum('bte,ebtd->btd', gates[..., :E], y) + gates[..., E:] * x
        return out
    x = L0_attn_x
    mod = (_silu(L0_c) @ L0_wmod).reshape(L0_c.shape[0], 6, 1, -1)
    sa, ca, ga, sb, cb, gb = (mod[:, 0], mod[:, 1], mod[:, 2], mod[:, 3], mod[:, 4], mod[:, 5])
    ga = (2 * (ga >= 0) - 1) * jnp.maximum(jnp.abs(ga), 0.25)
    gb = (2 * (gb >= 0) - 1) * jnp.maximum(jnp.abs(gb), 0.25)
    h = _layernorm(x, axis=-1) * (1 + ca) + sa
    x = x + ga * _L0_attn_ref(h, L0_attn_w_qkv, L0_attn_b_qkv, L0_attn_w_fc, L0_attn_b_fc)
    h = _layernorm(x, axis=-1) * (1 + cb) + sb
    x = x + gb * _L0_ffn_ref(h, L0_ffn_gate_w, L0_ffn_gate_bias, L0_ffn_Wg, L0_ffn_Wu, L0_ffn_Wd, L0_ffn_Sg, L0_ffn_Su, L0_ffn_Sd)
    mod = (_silu(L1_c) @ L1_wmod).reshape(L1_c.shape[0], 6, 1, -1)
    sa, ca, ga, sb, cb, gb = (mod[:, 0], mod[:, 1], mod[:, 2], mod[:, 3], mod[:, 4], mod[:, 5])
    ga = (2 * (ga >= 0) - 1) * jnp.maximum(jnp.abs(ga), 0.25)
    gb = (2 * (gb >= 0) - 1) * jnp.maximum(jnp.abs(gb), 0.25)
    h = _layernorm(x, axis=-1) * (1 + ca) + sa
    x = x + ga * _L1_attn_ref(h, L1_attn_Wq, L1_attn_Wk, L1_attn_Wv, L1_attn_Wb, L1_attn_Wo, L1_attn_bo)
    h = _layernorm(x, axis=-1) * (1 + cb) + sb
    x = x + gb * _L1_ffn_ref(h, L1_ffn_router_w, L1_ffn_router_b, L1_ffn_w1, L1_ffn_w2)
    return x

_drawn_inputs = setup_inputs


def setup_inputs(seed=0):
    import zlib

    import numpy as np

    out = dict(_drawn_inputs(seed))
    spreads = {'L1_attn_bo': (0.0, 1.255)}
    factors = {'L0_attn_w_qkv': 8.0,
     'L0_attn_b_qkv': 7.226,
     'L0_attn_w_fc': 5.91,
     'L0_attn_b_fc': 4.292,
     'L0_ffn_gate_w': 8.0,
     'L0_ffn_gate_bias': 8.0,
     'L0_ffn_Wg': 8.0,
     'L0_ffn_Wu': 8.0,
     'L0_ffn_Wd': 8.0,
     'L0_ffn_Sg': 8.0,
     'L0_ffn_Su': 8.0,
     'L0_ffn_Sd': 8.0,
     'L0_c': 3.705,
     'L0_wmod': 3.543,
     'L1_attn_Wq': 8.0,
     'L1_attn_Wk': 8.0,
     'L1_attn_Wv': 8.0,
     'L1_attn_Wb': 8.0,
     'L1_attn_Wo': 8.0,
     'L1_ffn_router_w': 3.577,
     'L1_ffn_router_b': 8.0,
     'L1_ffn_w1': 8.0,
     'L1_ffn_w2': 8.0}
    for name, (base, spread) in spreads.items():
        noise = np.random.default_rng([zlib.crc32(name.encode()), seed]).standard_normal(out[name].shape)
        drawn = base * np.exp(spread * noise) if base else spread * noise
        out[name] = jnp.asarray(drawn.astype(out[name].dtype))
    for name, factor in factors.items():
        out[name] = (out[name] * factor).astype(out[name].dtype)
    return out
```

```python
from contextlib import ExitStack

import numpy as np

import concourse.bass as bass
from concourse import mybir

F32 = mybir.dt.float32
BF16 = mybir.dt.bfloat16
I32 = mybir.dt.int32
ALU = mybir.AluOpType
ACT = mybir.ActivationFunctionType
AX = mybir.AxisListType

P = 128
D = 128
BATCH, SEQ = 16, 256
TOK = BATCH * SEQ
TILES = TOK // P
HEADS, DEPTH = 16, 8
LN_EPS = 1e-5
BANK = 512


def ds(start, size):
    return bass.ds(start, size)


PARTS = 3
PAIRS = PARTS * PARTS
ROWS = PAIRS * DEPTH
ROWS_M = ROWS + PARTS
HALF = HEADS // 2
GROUP = 4
GROUPS = HEADS // GROUP
BUFS = 3
STACK_DMAS = PARTS * PARTS + PARTS
VW = 32


def attention(nc, T, x_fm, x_tm, mod):
    ident = T["ident"]
    w_qk, w_v, w_fc, bq_col, bk_col, bv_col = (T[k] for k in ("w_qk", "w_v", "w_fc", "bq_col", "bk_col", "bv_col"))
    ca1, sa, ga, ga_bfc = mod
    rstd, nmean = T["rstd"], T["mean"]
    with ExitStack() as ctx:
        def sb(name, shape, dt=F32):
            return ctx.enter_context(nc.sbuf_tensor(name, shape, dt))

        def sem(name):
            return ctx.enter_context(nc.semaphore(name))

        xn = sb("at_xn", [P, 2, D])
        hb = sb("at_h", [P, BUFS, SEQ])
        qk = sb("at_qk", [P, 2 * SEQ])
        rest = sb("at_rest", [P, 2 * SEQ])
        rest2 = sb("at_rest2", [P, 2 * SEQ])
        part = sb("at_part", [P, PARTS, 2 * SEQ], BF16)
        qs = sb("at_qs", [P, BUFS, HEADS, SEQ], BF16)
        ks = sb("at_ks", [P, BUFS, HEADS, SEQ], BF16)
        v1 = sb("at_v", [P, BUFS, 2, HEADS, VW])
        negm = sb("at_negm", [P, BUFS, 2, HALF, 2])
        nrow = sb("at_nrow", [HALF, SEQ])
        nrest = sb("at_nrest", [HALF, SEQ])
        nrest2 = sb("at_nrest2", [HALF, SEQ])
        nzero = sb("at_nzero", [HALF, SEQ])
        npart = sb("at_npart", [HALF, PARTS, SEQ], BF16)
        pt = sb("at_p", [P, 2 * GROUP, 2, SEQ])
        osb = sb("at_o", [P, GROUPS, SEQ])
        rden = sb("at_rden", [P, 2, HEADS])
        a_tm = sb("at_a", [P, 2, HEADS, DEPTH])
        a_fm = sb("at_afm", [P, SEQ])
        upd = sb("at_upd", [P, SEQ])
        bounce = nc.dram_tensor("qk_parts", [BUFS, 2, PARTS, DEPTH, HEADS, SEQ], BF16, kind="Internal").ap()
        nbounce = nc.dram_tensor("max_parts", [BUFS, 2, PARTS, HALF, SEQ], BF16, kind="Internal").ap()
        ps = T["psum"]
        P1, P2, OB, M0, M1 = [0, 1], [2, 3], (4, 5), 6, 7
        o_ps = ps[:, 4:6, :].rearrange("p a c -> p (a c)")

        filled = sem("at_filled")
        zero_filled = sem("at_zero_filled")
        xn_ready = sem("at_xn_ready")
        xt_done = sem("at_xt_done")
        h_ready = sem("at_h_ready")
        qk_proj = sem("at_qk_proj")
        qk_ready = sem("at_qk_ready")
        part_ready = sem("at_part_ready")
        rest_ready = sem("at_rest_ready")
        part_out = sem("at_part_out")
        stacked = sem("at_stacked")
        p1_done = sem("at_p1_done")
        max_done = sem("at_max_done")
        nrow_ready = sem("at_nrow_ready")
        nsplit = sem("at_nsplit")
        nrows_out = sem("at_nrows_out")
        nrows_in = [sem(f"at_nrows_in{i}") for i in range(2)]
        vn_done = sem("at_vn_done")
        v_ready = sem("at_v_ready")
        p2_done = sem("at_p2_done")
        exp_done = sem("at_exp_done")
        pv_done = sem("at_pv_done")
        o_ready = sem("at_o_ready")
        ot_done = sem("at_ot_done")
        rden_ready = sem("at_rden_ready")
        a_ready = sem("at_a_ready")
        at_done = sem("at_at_done")
        afm_ready = sem("at_afm_ready")
        fc_done = sem("at_fc_done")
        upd_ready = sem("at_upd_ready")
        x_added = sem("at_x_added")
        block = ctx.enter_context(nc.Block())

        def live(k):
            return {
                "xn": 0 <= k + 2 < BATCH, "proj": 0 <= k + 1 < BATCH, "p1": 0 <= k < BATCH,
                "p2": 0 <= k - 1 < BATCH, "tail": 0 <= k - 2 < BATCH,
            }

        def run(eng, iteration):
            for n in range(-2, 2):
                iteration(n, n)
            with eng.Fori(0, (BATCH - 4) // BUFS) as i:
                for k in range(BUFS):
                    iteration(BUFS * i + 2 + k, 2 + k)
            for n in range(BATCH - 2, BATCH + 2):
                iteration(n, n)

        @block.tensor
        def _(pe):
            def transpose_negm(n, k, half, bank):
                pe.wait_ge(max_done, HEADS * n + HALF * (half + 1))
                for tt in range(2):
                    mm = pe.transpose(ps[0:HALF, bank, SEQ + tt * P:SEQ + (tt + 1) * P], negm[:, k % BUFS, half, :, tt], ident[:])
                return mm

            def scores(n, k, g):
                f = live(k)
                for h in range(GROUP * g, GROUP * (g + 1)):
                    if f["p1"]:
                        if h == 0:
                            pe.wait_ge(stacked, 16 * STACK_DMAS * (n + 1))
                        if k > 0 or h >= 2:
                            pe.wait_ge(max_done, HEADS * n + h - 1)
                        for tt in range(2):
                            mm = pe.matmul(ps[:, P1[h % 2], tt * SEQ:(tt + 1) * SEQ],
                                           qs[0:ROWS, k % BUFS, h, tt * P:(tt + 1) * P], ks[0:ROWS, k % BUFS, h, :],
                                           start=True, stop=True)
                        mm.then_inc(p1_done, 1)
                    if f["p2"]:
                        m, j = n - 1, k - 1
                        if h % HALF == 0:
                            pe.wait_ge(nrows_in[h // HALF], 16 * (m + 1))
                        if j > 0 or h >= 2:
                            pe.wait_ge(exp_done, HEADS * m + h - 1)
                        for st in range(2):
                            mm = pe.matmul(ps[:, P2[h % 2], st * SEQ:(st + 1) * SEQ],
                                           ks[0:ROWS_M, j % BUFS, h, st * P:(st + 1) * P], qs[0:ROWS_M, j % BUFS, h, :],
                                           start=True, stop=True)
                        mm.then_inc(p2_done, 1)

            def pv(m, j, g):
                pe.wait_ge(exp_done, HEADS * m + GROUP * (g + 1))
                if g == 0:
                    pe.wait_ge(v_ready, m + 1)
                    if j > 0:
                        pe.wait_ge(o_ready, m)
                for st in range(2):
                    for c in range(GROUP):
                        h = GROUP * g + c
                        mm = pe.matmul(o_ps[VW * c:VW * (c + 1), g * SEQ:(g + 1) * SEQ],
                                       v1[:, j % BUFS, st, h, :], pt[:, h % (2 * GROUP), st, :],
                                       start=(st == 0), stop=(st == 1), tile_position=(0, VW * c))
                mm.then_inc(pv_done, 1)

            def iteration(n, k):
                f = live(k)
                if f["proj"]:
                    pe.wait_ge(h_ready, n + 2)
                    if live(k - 1)["p1"]:
                        pe.wait_ge(nrow_ready, 2 * n - 1)
                    for c in range(2):
                        mm = pe.matmul(ps[:, M0, c * SEQ:(c + 1) * SEQ], w_qk[:, c * P:(c + 1) * P], hb[:, (k + 1) % BUFS, :],
                                       start=True, stop=True)
                    mm.then_inc(qk_proj, 1)
                scores(n, k, 0)
                if f["tail"]:
                    pv(n - 2, k - 2, GROUPS - 1)
                if f["p1"] or f["p2"]:
                    if f["p1"]:
                        if k >= 3:
                            pe.wait_ge(upd_ready, n - 2)
                        for st in range(2):
                            mm = pe.matmul(ps[:, M1, st * P:(st + 1) * P], hb[:, k % BUFS, st * P:(st + 1) * P], w_v[:],
                                           start=True, stop=True)
                    if f["p2"]:
                        if not f["p1"]:
                            pe.wait_ge(upd_ready, n - 2)
                        mm = transpose_negm(n - 1, k - 1, 1, M1)
                    mm.then_inc(vn_done, 1)
                if f["tail"]:
                    pe.wait_ge(o_ready, n - 1)
                    if k >= 3:
                        pe.wait_ge(a_ready, n - 2)
                        pe.wait_ge(upd_ready, n - 2)
                    if f["proj"]:
                        pe.wait_ge(qk_ready, n + 2)
                    if f["p1"] or f["p2"]:
                        pe.wait_ge(v_ready, n + 1)
                        pe.wait_ge(nrow_ready, 2 * n)
                    for tt in range(2):
                        for g in range(GROUPS):
                            mm = pe.transpose(ps[:, M0 + tt, g * P:(g + 1) * P], osb[:, g, tt * P:(tt + 1) * P], ident[:])
                    mm.then_inc(ot_done, 1)
                scores(n, k, 1)
                if f["p2"]:
                    pv(n - 1, k - 1, 0)
                if f["p1"] or f["xn"]:
                    if f["tail"]:
                        pe.wait_ge(a_ready, n - 1)
                    elif f["proj"] and k >= -1:
                        pe.wait_ge(qk_ready, n + 2)
                    if f["xn"]:
                        pe.wait_ge(xn_ready, n + 3)
                        for tt in range(2):
                            mm = pe.transpose(ps[:, M0, tt * P:(tt + 1) * P], xn[:, tt, :], ident[:])
                    if f["p1"]:
                        mm = transpose_negm(n, k, 0, M0)
                    mm.then_inc(xt_done, 1)
                scores(n, k, 2)
                if f["p2"]:
                    pv(n - 1, k - 1, 1)
                if f["tail"]:
                    pe.wait_ge(a_ready, n - 1)
                    for tt in range(2):
                        mm = pe.transpose(ps[:, M1, tt * P:(tt + 1) * P],
                                          a_tm[:, tt, :, :].rearrange("p h d -> p (h d)"), ident[:])
                    mm.then_inc(at_done, 1)
                scores(n, k, 3)
                if f["p2"]:
                    pv(n - 1, k - 1, 2)
                if f["tail"]:
                    pe.wait_ge(afm_ready, n - 1)
                    pe.matmul(ps[:, M1, 0:SEQ], w_fc[:], a_fm[:], start=True, stop=True).then_inc(fc_done, 1)

            run(pe, iteration)

        @block.vector
        def _(dve):
            def maxima(n, k, g):
                if not live(k)["p1"]:
                    return
                for h in range(GROUP * g, GROUP * (g + 1)):
                    dve.wait_ge(p1_done, HEADS * n + h + 1)
                    if h == 0 and k >= 2:
                        dve.wait_ge(vn_done, n)
                    nc.vector.tensor_reduce(negm[:, k % BUFS, h // HALF, h % HALF, :],
                                            ps[:, P1[h % 2], :].rearrange("p (t s) -> p t s", t=2),
                                            AX.X, ALU.max, negate=True).then_inc(max_done, 1)

            def iteration(n, k):
                f = live(k)
                if f["xn"]:
                    if k >= -1:
                        dve.wait_ge(xt_done, n + 2)
                    for tt in range(2):
                        t = 2 * n + 4 + tt
                        ins = nc.vector.tensor_scalar(xn[:, tt, :], x_tm[:, ds(t * D, D)], nmean[:, ds(t, 1)], rstd[:, ds(t, 1)],
                                                      ALU.subtract, ALU.mult)
                    ins.then_inc(xn_ready, 1)
                if f["proj"]:
                    dve.wait_ge(qk_proj, n + 2)
                    if k >= 0:
                        dve.wait_ge(part_ready, PARTS * (n + 1))
                    nc.vector.tensor_scalar(qk[:, 0:SEQ], ps[:, M0, 0:SEQ], bq_col[:, 0:1], None, ALU.add)
                    nc.vector.tensor_scalar(qk[:, SEQ:2 * SEQ], ps[:, M0, SEQ:2 * SEQ], bk_col[:, 0:1], None, ALU.add)\
                        .then_inc(qk_ready, 1)
                maxima(n, k, 0)
                if f["proj"]:
                    dve.wait_ge(part_ready, PARTS * (n + 1) + 1)
                    nc.vector.tensor_tensor(rest[:], qk[:], part[:, 0, :], ALU.subtract).then_inc(rest_ready, 1)
                maxima(n, k, 1)
                if f["proj"]:
                    dve.wait_ge(part_ready, PARTS * (n + 1) + 2)
                    nc.vector.tensor_tensor(rest2[:], rest[:], part[:, 1, :], ALU.subtract).then_inc(rest_ready, 1)
                if f["tail"]:
                    dve.wait_ge(ot_done, n - 1)
                    ov = ps[:, 6:8, :].rearrange("p t (h c) -> p (t h) c", c=VW)
                    nc.vector.reciprocal(rden[:].rearrange("p t h -> p (t h)"), ov[:, :, DEPTH]).then_inc(rden_ready, 1)
                    dve.wait_ge(rden_ready, n - 1)
                    if k >= 3:
                        dve.wait_ge(at_done, n - 2)
                    nc.vector.tensor_tensor(a_tm[:].rearrange("p t h d -> p (t h) d"), ov[:, :, 0:DEPTH],
                                            rden[:].rearrange("p t h -> p (t h)").unsqueeze(2).broadcast_to([P, 2 * HEADS, DEPTH]),
                                            ALU.mult).then_inc(a_ready, 1)
                maxima(n, k, 2)
                maxima(n, k, 3)

            nc.vector.memset(v1[:], 0.0).then_inc(filled, 1)
            nc.vector.memset(ks[64:ROWS_M, :, :, :], 1.0).then_inc(filled, 1)
            dve.wait_ge(filled, 2)
            nc.vector.memset(v1[:, :, :, :, DEPTH], 1.0).then_inc(filled, 1)
            run(dve, iteration)

        @block.scalar
        def _(act):
            def exps(n, k, g):
                for h in range(GROUP * g, GROUP * (g + 1)):
                    act.wait_ge(p2_done, HEADS * n + h + 1)
                    if h % GROUP == 0 and (k > 0 or g >= 2):
                        act.wait_ge(pv_done, GROUPS * n + g - 1)
                    nc.scalar.activation(pt[:, h % (2 * GROUP), :, :].rearrange("p s t -> p (s t)"), ps[:, P2[h % 2], :],
                                         ACT.Exp, scale=float(1.0 / np.sqrt(np.float32(DEPTH)))).then_inc(exp_done, 1)

            def cut(n, k, i):
                if i == 0:
                    act.wait_ge(qk_ready, n + 2)
                    if k >= 0:
                        act.wait_ge(part_out, 32 * (n + 1))
                else:
                    act.wait_ge(rest_ready, 2 * (n + 1) + i)
                nc.scalar.activation(part[:, i, :], (qk, rest, rest2)[i][:], ACT.Copy).then_inc(part_ready, 1)

            def iteration(n, k):
                f = live(k)
                if f["proj"]:
                    cut(n, k, 0)
                if f["p2"]:
                    exps(n - 1, k - 1, 0)
                if f["tail"]:
                    act.wait_ge(pv_done, GROUPS * (n - 1))
                    if k >= 3:
                        act.wait_ge(ot_done, n - 2)
                    nc.scalar.activation(osb[:].rearrange("p g t -> p (g t)"), o_ps, ACT.Copy).then_inc(o_ready, 1)
                if f["p1"] or f["p2"]:
                    act.wait_ge(vn_done, n + 1)
                if f["p1"]:
                    if k >= 2:
                        act.wait_ge(pv_done, GROUPS * (n - 1))
                    nc.scalar.activation(v1[:, k % BUFS, :, :, 0:DEPTH],
                                         ps[:, M1, 0:SEQ].rearrange("p (s h d) -> p s h d", s=2, d=DEPTH), ACT.Copy)\
                        .then_inc(v_ready, 1)
                if f["p2"]:
                    if not f["p1"]:
                        nc.scalar.sem_inc(v_ready, 1)
                    act.wait_ge(nsplit, 5 * (2 * n - 1))
                    nc.scalar.activation(nrow[:], ps[0:HALF, M1, SEQ:2 * SEQ], ACT.Copy).then_inc(nrow_ready, 1)
                if f["proj"]:
                    cut(n, k, 1)
                if f["p2"]:
                    exps(n - 1, k - 1, 1)
                if f["proj"]:
                    cut(n, k, 2)
                if f["p1"] or f["xn"]:
                    act.wait_ge(xt_done, n + 3)
                    if f["xn"]:
                        b = n + 2
                        nc.scalar.activation(hb[:, (k + 2) % BUFS, :], ps[:, M0, 0:SEQ], ACT.Identity, bias=sa[:, ds(b, 1)],
                                             scale=ca1[:, ds(b, 1)]).then_inc(h_ready, 1)
                    if f["p1"]:
                        if k > 0:
                            act.wait_ge(nsplit, 5 * 2 * n)
                        nc.scalar.activation(nrow[:], ps[0:HALF, M0, SEQ:2 * SEQ], ACT.Copy).then_inc(nrow_ready, 1)
                if f["p2"]:
                    exps(n - 1, k - 1, 2)
                if f["tail"]:
                    act.wait_ge(at_done, n - 1)
                    if k >= 3:
                        act.wait_ge(fc_done, n - 2)
                    nc.scalar.activation(a_fm[:], ps[:, M1, 0:SEQ], ACT.Identity, bias=bv_col[:, 0:1]).then_inc(afm_ready, 1)
                if f["p2"]:
                    exps(n - 1, k - 1, 3)
                if f["tail"]:
                    b = n - 2
                    act.wait_ge(fc_done, n - 1)
                    if k >= 3:
                        act.wait_ge(x_added, n - 2)
                    nc.scalar.activation(upd[:], ps[:, M1, 0:SEQ], ACT.Identity, bias=ga_bfc[:, ds(b, 1)],
                                         scale=ga[:, ds(b, 1)]).then_inc(upd_ready, 1)

            act.wait_ge(filled, 3)
            run(act, iteration)

        @block.gpsimd
        def _(pool):
            def split_rows(n, k, half):
                c = 5 * (2 * n + half)
                pool.wait_ge(nrow_ready, 2 * n + half + 1)
                if k > 0 or half > 0:
                    pool.wait_ge(nrows_out, 16 * (2 * n + half))
                nc.gpsimd.tensor_tensor(npart[:, 0, :], nrow[:], nzero[:], ALU.add).then_inc(nsplit, 1)
                pool.wait_ge(nsplit, c + 1)
                nc.gpsimd.tensor_tensor(nrest[:], nrow[:], npart[:, 0, :], ALU.subtract).then_inc(nsplit, 1)
                pool.wait_ge(nsplit, c + 2)
                nc.gpsimd.tensor_tensor(npart[:, 1, :], nrest[:], nzero[:], ALU.add).then_inc(nsplit, 1)
                pool.wait_ge(nsplit, c + 3)
                nc.gpsimd.tensor_tensor(nrest2[:], nrest[:], npart[:, 1, :], ALU.subtract).then_inc(nsplit, 1)
                pool.wait_ge(nsplit, c + 4)
                nc.gpsimd.tensor_tensor(npart[:, 2, :], nrest2[:], nzero[:], ALU.add).then_inc(nsplit, 1)

            def iteration(n, k):
                f = live(k)
                if f["p2"]:
                    split_rows(n - 1, k - 1, 1)
                if f["p1"]:
                    split_rows(n, k, 0)
                if f["tail"]:
                    b = n - 2
                    pool.wait_ge(upd_ready, n - 1)
                    cols = x_fm[:, ds(b * SEQ, SEQ)]
                    nc.gpsimd.tensor_tensor(cols, cols, upd[:], ALU.add).then_inc(x_added, 1)

            nc.gpsimd.memset(nzero[:], 0.0).then_inc(zero_filled, 1)
            pool.wait_ge(zero_filled, 1)
            run(pool, iteration)

        @block.sync
        def _(sp):
            def held(name, x):
                if isinstance(x, int):
                    return x
                r = sp.alloc_register(name)
                sp.reg_mov(r, x)
                return sp.snap(r)

            def load_stacks(buf):
                for a in range(PARTS):
                    for b in range(PARTS):
                        r = DEPTH * (PARTS * a + b)
                        sp.dma_start(qs[r:r + DEPTH, buf, :, :], bounce[buf, 0, a]).then_inc(stacked, 16)
                    r = DEPTH * PARTS * a
                    sp.dma_start(ks[r:r + DEPTH * PARTS, buf, :, :],
                                 bounce[buf, 1].rearrange("b d h t -> (b d) h t")).then_inc(stacked, 16)

            def load_rows(buf, half, out):
                sp.dma_start(nbounce[buf, half].rearrange("i h t -> h i t"), npart[:]).then_inc(nrows_out, 16)
                sp.wait_ge(nrows_out, out)
                sp.dma_start(qs[ROWS:ROWS_M, buf, HALF * half:HALF * (half + 1), :], nbounce[buf, half]).then_inc(nrows_in[half], 16)

            def iteration(n, k):
                f = live(k)
                buf = (k + 1) % BUFS
                split1 = held(f"split1_{k}", 10 * n)
                split0 = held(f"split0_{k}", 10 * n + 5)
                cut = held(f"cut_{k}", PARTS * (n + 2))
                rows1 = held(f"rows1_{k}", 32 * n)
                rows0 = held(f"rows0_{k}", 32 * n + 16)
                seen = held(f"seen_{k}", HEADS * n + 1)
                out = held(f"out_{k}", 32 * (n + 2))
                if f["p2"]:
                    sp.wait_ge(nsplit, split1)
                    load_rows((k - 1) % BUFS, 1, rows1)
                if f["proj"]:
                    sp.wait_ge(part_ready, cut)
                    for q in range(2):
                        sp.dma_start(bounce[buf, q].rearrange("a d h t -> (d h) a t"), part[:, :, q * SEQ:(q + 1) * SEQ])\
                            .then_inc(part_out, 16)
                    if f["p1"]:
                        sp.wait_ge(p1_done, seen)
                    sp.wait_ge(part_out, out)
                    load_stacks(buf)
                if f["p1"]:
                    sp.wait_ge(nsplit, split0)
                    load_rows(k % BUFS, 0, rows0)

            sp.wait_ge(filled, 3)
            run(sp, iteration)


MODS = 6


def setup(nc, T, A):
    with ExitStack() as ctx:
        def sb(name, shape, dt=F32):
            return ctx.enter_context(nc.sbuf_tensor(name, shape, dt))

        def sem(name):
            return ctx.enter_context(nc.semaphore(name))

        c_fm = sb("su_c", [P, 2, BATCH])
        cs = sb("su_cs", [P, 2, BATCH])
        wmod = sb("su_wmod", [P, 2, MODS * D])
        rot = sb("su_rot", [P, 2, PI_ALL, HEADS])
        w_in = sb("su_w", [P, 2 * D])
        b_in = sb("su_b", [1, 2 * D])
        b_rot = sb("su_brot", [1, 2 * D])
        t0 = sb("su_t0", [P, PI_ALL, HEADS])
        t1 = sb("su_t1", [P, PI_ALL, HEADS])
        u0 = sb("su_u0", [1, PI_ALL, HEADS])
        u1 = sb("su_u1", [1, PI_ALL, HEADS])
        one = sb("su_one", [1, 1])
        stats = sb("su_stats", [P, TILES, 6])
        var = sb("su_var", [P, TILES])
        dm = sb("su_dm", [P, TILES])
        sg = sb("su_sg", [P, 2 * 2, BATCH])
        ab = sb("su_ab", [P, 2 * 2, BATCH])
        ps = T["psum"]
        x_in = sem("su_x_in")
        c_in = sem("su_c_in")
        w_loaded = sem("su_w_loaded")
        silu_done = sem("su_silu_done")
        mod_done = sem("su_mod_done")
        bias_done = sem("su_bias_done")
        var_ready = sem("su_var_ready")
        std_ready = sem("su_std_ready")
        step = sem("su_step")
        rot_ready = sem("su_rot_ready")
        pool_done = sem("su_pool_done")
        block = ctx.enter_context(nc.Block())

        @block.sync
        def _(sp):
            sp.dma_start(T["x_tm"][:], A["x_tm"]).then_inc(x_in, 16)
            sp.dma_start(T["x_fm"][:], A["x_fm"]).then_inc(w_loaded, 16)
            sp.wait_ge(w_loaded, 16 * 10)
            for name in EARLY_LOADS:
                sp.dma_start(T[name][:], A[name]).then_inc(T["ffn0_loaded"], 16)

        @block.gpsimd
        def _(pool):
            pool.memset(one[:], 1.0).then_inc(pool_done, 1)

        @block.scalar
        def _(act):
            act.dma_start(c_fm[:], A["c_fm"]).then_inc(c_in, 16)
            act.dma_start(wmod[:], A["wmod"]).then_inc(c_in, 16)
            for dst, src in ((w_in[:], A["w_qk"]), (b_in[:], A["b_qk"]), (rot[:], A["rot"]), (T["w_v"][:], A["w_v"]),
                             (T["w_fc"][:], A["w_fc"]), (T["bv_col"][:], A["b_v"]), (T["bfc_col"][:], A["b_fc"]),
                             (T["ident"][:], A["ident"]), (T["bo_col"][:], A["b_o"])):
                act.dma_start(dst, src).then_inc(w_loaded, 16)
            act.wait_ge(c_in, 32)
            nc.scalar.activation(cs[:], c_fm[:], ACT.Silu).then_inc(silu_done, 1)
            act.wait_ge(var_ready, 1)
            nc.scalar.activation(dm[:], var[:], ACT.Sqrt).then_inc(std_ready, 1)

        @block.tensor
        def _(pe):
            pe.wait_ge(silu_done, 1)
            for l in range(2):
                for m in range(MODS):
                    at = (l * MODS + m) * BATCH
                    mm = pe.matmul(ps[:, 0, at:at + BATCH], wmod[:, l, m * D:(m + 1) * D], cs[:, l, :], start=True, stop=True)
            mm.then_inc(mod_done, 1)
            pe.wait_ge(rot_ready, 1)
            pe.wait_ge(pool_done, 1)
            for c in range(2):
                mm = pe.matmul(ps[:, 1, c:c + 1], b_rot[:, c * P:(c + 1) * P], one[:], start=True, stop=True)
            mm.then_inc(bias_done, 1)

        @block.vector
        def _(dve):
            n = 0
            dve.wait_ge(x_in, 16)
            for t in range(TILES):
                ins = nc.vector.bn_stats(stats[:, t, :], T["x_tm"][:, t * D:(t + 1) * D])
            ins.then_inc(step, 1)
            dve.wait_ge(step, 1)
            me, mo, ve, vo = (stats[:, :, i] for i in (1, 4, 2, 5))
            nc.vector.tensor_tensor(T["mean"][:], me, mo, ALU.add).then_inc(step, 1)
            nc.vector.tensor_tensor(dm[:], me, mo, ALU.subtract).then_inc(step, 1)
            nc.vector.tensor_tensor(var[:], ve, vo, ALU.add).then_inc(step, 1)
            dve.wait_ge(step, 4)
            nc.vector.tensor_scalar(T["mean"][:], T["mean"][:], 0.5, None, ALU.mult).then_inc(step, 1)
            nc.vector.scalar_tensor_tensor(dm[:], dm[:], 0.25, dm[:], ALU.mult, ALU.mult).then_inc(step, 1)
            nc.vector.tensor_scalar(var[:], var[:], 1.0 / D, LN_EPS, ALU.mult, ALU.add).then_inc(step, 1)
            dve.wait_ge(step, 7)
            nc.vector.tensor_tensor(var[:], var[:], dm[:], ALU.add).then_inc(var_ready, 1)
            dve.wait_ge(w_loaded, 16 * 10)
            for w, out, a, b, q in ((w_in, T["w_qk"], t0, t1, P), (b_in, b_rot, u0, u1, 1)):
                wv = w[:].rearrange("p (i two h) -> p i two h", two=2, h=HEADS)
                ov = out[:].rearrange("p (i two h) -> p i two h", two=2, h=HEADS)
                cos, sin = rot[0:q, 0], rot[0:q, 1]
                for o, (x, y, op) in enumerate(((cos, sin, ALU.subtract), (sin, cos, ALU.add))):
                    nc.vector.tensor_tensor(a[:], wv[:, :, 0, :], x, ALU.mult).then_inc(step, 1)
                    nc.vector.tensor_tensor(b[:], wv[:, :, 1, :], y, ALU.mult).then_inc(step, 1)
                    n += 3
                    dve.wait_ge(step, 7 + n - 1)
                    nc.vector.tensor_tensor(ov[:, :, o, :], a[:], b[:], op).then_inc(step, 1)
                    dve.wait_ge(step, 7 + n)
            nc.vector.sem_inc(rot_ready, 1)
            dve.wait_ge(mod_done, 1)
            m = ps[:, 0, 0:2 * MODS * BATCH].rearrange("p (l k b) -> p l k b", k=3, b=BATCH)
            nc.vector.tensor_copy(T["shift"][:], m[:, :, 0, :])
            nc.vector.tensor_scalar(T["scale1"][:], m[:, :, 1, :], 1.0, None, ALU.add)
            nc.vector.tensor_scalar(sg[:], m[:, :, 2, :], 0.0, 2.0, ALU.is_ge, ALU.mult).then_inc(step, 1)
            dve.wait_ge(step, 8 + n)
            nc.vector.tensor_scalar(sg[:], sg[:], -1.0, None, ALU.add).then_inc(step, 1)
            dve.wait_ge(step, 9 + n)
            nc.vector.tensor_tensor(ab[:], sg[:], m[:, :, 2, :], ALU.mult).then_inc(step, 1)
            dve.wait_ge(step, 10 + n)
            nc.vector.scalar_tensor_tensor(T["gate"][:], ab[:], 0.25, sg[:], ALU.max, ALU.mult).then_inc(step, 1)
            dve.wait_ge(step, 11 + n)
            nc.vector.tensor_scalar(T["ga_bfc"][:], T["gate"][:, 0, :], T["bfc_col"][:, 0:1], None, ALU.mult)
            nc.vector.tensor_scalar(T["ga_bo"][:], T["gate"][:, 2, :], T["bo_col"][:, 0:1], None, ALU.mult)
            dve.wait_ge(bias_done, 1)
            nc.vector.tensor_copy(T["bq_col"][:], ps[:, 1, 0:1])
            nc.vector.tensor_copy(T["bk_col"][:], ps[:, 1, 1:2])
            dve.wait_ge(std_ready, 1)
            nc.vector.reciprocal(T["rstd"][:], dm[:]).then_inc(step, 1)
            dve.wait_ge(step, 12 + n)


CHUNK = 512
CHUNKS = TOK // CHUNK
CT = CHUNK // P
CB = CHUNK // SEQ


class LayerNorm:

    def __init__(self, nc, ctx, name, T, xc, hc, nt, bank, part):
        self.nc, self.T, self.xc, self.hc, self.part = nc, T, xc, hc, part
        self.ps = T["psum"][:, bank, :]
        sb = lambda n, s: ctx.enter_context(nc.sbuf_tensor(f"{name}_{n}", s, F32))
        self.st, self.mv, self.sd, self.rs = sb("st", [P, CT, 6]), sb("mv", [P, CT, 2]), sb("sd", [P, CT]), sb("rs", [P, CT])
        self.nt = nt
        sem = lambda n: ctx.enter_context(nc.semaphore(f"{name}_{n}"))
        self.x_tm = sem("x_tm")
        self.mean = sem("mean")
        self.std = sem("std")
        self.norm = sem("norm")
        self.n_fm = sem("n_fm")
        self.h = sem("h")

    def pe_x(self, pe):
        for t in range(CT):
            mm = pe.transpose(self.ps[:, t * P:(t + 1) * P], self.xc[:, t * P:(t + 1) * P], self.T["ident"][:])
        mm.then_inc(self.x_tm, 1)

    def dve_stats(self, dve, c):
        v = self.nc.vector
        dve.wait_ge(self.x_tm, c + 1)
        for t in range(CT):
            ins = v.bn_stats(self.st[:, t, :], self.ps[:, t * P:(t + 1) * P])
        ins.then_inc(self.mean, 1)
        me, mo, ve, vo = (self.st[:, :, i] for i in (1, 4, 2, 5))
        mean, dif = self.mv[:, :, 0], self.mv[:, :, 1]
        dve.wait_ge(self.mean, 4 * c + 1)
        v.tensor_tensor(mean, me, mo, ALU.add)
        v.tensor_tensor(dif, me, mo, ALU.subtract)
        v.tensor_tensor(self.rs[:], ve, vo, ALU.add).then_inc(self.mean, 1)
        dve.wait_ge(self.mean, 4 * c + 2)
        v.tensor_scalar(mean, mean, 0.5, None, ALU.mult)
        v.scalar_tensor_tensor(dif, dif, 0.25, dif, ALU.mult, ALU.mult)
        v.tensor_scalar(self.rs[:], self.rs[:], 1.0 / D, LN_EPS, ALU.mult, ALU.add).then_inc(self.mean, 1)
        dve.wait_ge(self.mean, 4 * c + 3)
        v.tensor_tensor(self.rs[:], self.rs[:], dif, ALU.add).then_inc(self.mean, 1)

    def act_std(self, act, c):
        act.wait_ge(self.mean, 4 * c + 4)
        self.nc.scalar.activation(self.sd[:], self.rs[:], ACT.Sqrt).then_inc(self.std, 1)

    def dve_norm(self, dve, c):
        v = self.nc.vector
        dve.wait_ge(self.std, c + 1)
        v.reciprocal(self.rs[:], self.sd[:]).then_inc(self.norm, 1)
        dve.wait_ge(self.norm, 2 * c + 1)
        for t in range(CT):
            ins = v.tensor_scalar(self.nt[:, t, :], self.ps[:, t * P:(t + 1) * P], self.mv[:, t, 0:1], self.rs[:, t:t + 1],
                                  ALU.subtract, ALU.mult)
        ins.then_inc(self.norm, 1)

    def pe_n(self, pe, c):
        pe.wait_ge(self.norm, 2 * c + 2)
        for t in range(CT):
            mm = pe.transpose(self.ps[:, t * P:(t + 1) * P], self.nt[:, t, :], self.T["ident"][:])
        mm.then_inc(self.n_fm, 1)

    def act_h(self, act, c):
        act.wait_ge(self.n_fm, c + 1)
        for i in range(CB):
            b = CB * c + i
            ins = self.nc.scalar.activation(self.hc[:, i * SEQ:(i + 1) * SEQ], self.ps[:, i * SEQ:(i + 1) * SEQ], ACT.Identity,
                                            bias=self.T["shift"][:, self.part, ds(b, 1)],
                                            scale=self.T["scale1"][:, self.part, ds(b, 1)])
        ins.then_inc(self.h, 1)


def cols(t, c, size=CHUNK):
    return t[:, ds(c * size, size)]


class Steps:

    def __init__(self, eng, sem):
        self.eng, self.sem, self.n = eng, sem, 0

    def done(self, ins, wait=True):
        ins.then_inc(self.sem, 1)
        self.n += 1
        if wait:
            self.eng.wait_ge(self.sem, self.n)


EXPERTS, HIDDEN = 64, 88
EGROUPS, EPG = 8, 8
TOP_GROUPS = 4
ROUTED_SCALE = 2.5
EHALF = EXPERTS // 2
TAKEN = -1.0e30


def route0(nc, T, A):
    x_fm, h_fm, ps = T["x_fm"], T["h_fm"], T["psum"]
    with ExitStack() as ctx:
        def sb(name, shape, dt=F32):
            return ctx.enter_context(nc.sbuf_tensor(name, shape, dt))

        def sem(name):
            return ctx.enter_context(nc.semaphore(name))

        xc, hc = sb("r0_xc", [P, CHUNK]), sb("r0_hc", [P, CHUNK])
        ln = LayerNorm(nc, ctx, "r0_ln", T, xc, hc, sb("r0_nt", [P, CT, D]), 0, 1)
        N = TILES * EXPERTS
        lg = sb("r0_lg", [P, N])
        sfc = sb("r0_sfc", [P, N])
        w0 = sb("r0_w0", [P, N])
        w1 = sb("r0_w1", [P, N])
        G = TILES * EGROUPS
        hi, lo, th, tl = (sb(f"r0_{n}", [P, G, 4]) for n in ("hi", "lo", "th", "tl"))
        gs, rank = sb("r0_gs", [P, G]), sb("r0_rank", [P, G])
        top = sb("r0_top", [P, TILES, 8])
        den, rden = sb("r0_den", [P, TILES]), sb("r0_rden", [P, TILES])
        parts = sb("r0_parts", [P, TILES, 2, PARTS, EHALF], BF16)
        gate_w, gate_b = sb("r0_gw", [P, EXPERTS]), sb("r0_gb", [P, EXPERTS])
        less = sb("r0_less", [P, EGROUPS, EGROUPS])
        loaded = sem("r0_loaded")
        xc_ready = sem("r0_xc_ready")
        h_kept = sem("r0_h_kept")
        lg_done = sem("r0_lg_done")
        lg_kept = sem("r0_lg_kept")
        scored = sem("r0_scored")
        step = sem("r0_step")
        cut = sem("r0_cut")
        tr_done = sem("r0_tr_done")
        tr_kept = [sem(f"r0_tr_kept{g}") for g in range(2)]
        block = ctx.enter_context(nc.Block())

        @block.sync
        def _(sp):
            sp.dma_start(gate_w[:], A["gate_w"]).then_inc(loaded, 16)
            sp.dma_start(gate_b[:], A["gate_b"]).then_inc(loaded, 16)
            sp.dma_start(less[:], A["less8"]).then_inc(loaded, 16)
            sp.dma_start(T["sel"][:], A["sel"]).then_inc(T["ffn0_loaded"], 16)
            sp.dma_start(T["wd"][:, 0:ROUTED_TILES, :], A["wd"]).then_inc(T["ffn0_loaded"], 16)
            sp.dma_start(T["wd"][0:SHARED_ROWS, ROUTED_TILES:HT, :], A["sd"]).then_inc(T["ffn0_loaded"], 16)

        @block.tensor
        def _(pe):
            pe.wait_ge(loaded, 48)

            def chunk(c, first):
                pe.wait_ge(xc_ready, c + 1)
                ln.pe_x(pe)
                ln.pe_n(pe, c)
                pe.wait_ge(ln.h, c + 1)
                if not first:
                    pe.wait_ge(lg_kept, c)
                for t in range(CT):
                    mm = pe.matmul(ps[:, 1, t * EXPERTS:(t + 1) * EXPERTS], hc[:, t * P:(t + 1) * P], gate_w[:], start=True, stop=True)
                mm.then_inc(lg_done, 1)

            chunk(0, True)
            with pe.Fori(1, CHUNKS) as c:
                chunk(c, False)
            pe.wait_ge(cut, 1)
            pe.wait_ge(T["ffn0_loaded"], 16 * FFN0_LOADS)

            def turn(c, k):
                if k >= 2:
                    for g in range(2):
                        pe.wait_ge(tr_kept[g], c - 1)
                for g in range(2):
                    for t in range(CT):
                        mm = pe.matmul(ps[0:PARTS * EHALF, 2 + 2 * (k % 2) + g, t * P:(t + 1) * P],
                                       parts[:, ds(CT * c + t, 1), g, :, :].rearrange("p o i e -> p (o i e)"), T["ident_bf"][:],
                                       start=True, stop=True)
                mm.then_inc(tr_done, 1)

            turn(0, 0)
            turn(1, 1)
            with pe.Fori(1, CHUNKS // 2) as i:
                turn(2 * i, 2)
                turn(2 * i + 1, 3)

        @block.scalar
        def _(act):
            def chunk(c, first):
                if not first:
                    act.wait_ge(ln.x_tm, c)
                nc.scalar.activation(xc[:], cols(x_fm, c), ACT.Copy).then_inc(xc_ready, 1)
                ln.act_std(act, c)
                if not first:
                    act.wait_ge(lg_done, c)
                    act.wait_ge(h_kept, c)
                ln.act_h(act, c)

            chunk(0, True)
            with act.Fori(1, CHUNKS) as c:
                chunk(c, False)
            act.wait_ge(lg_kept, CHUNKS)
            nc.scalar.activation(lg[:], lg[:], ACT.Sigmoid).then_inc(scored, 1)

            def keep(c, k):
                act.wait_ge(tr_done, c + 1)
                nc.scalar.activation(T["rw"][0:PARTS * EHALF, 0, ds(c * CHUNK, CHUNK)], ps[0:PARTS * EHALF, 2 + 2 * (k % 2), :], ACT.Copy)\
                    .then_inc(tr_kept[0], 1)

            with act.Fori(0, CHUNKS // 2) as i:
                keep(2 * i, 0)
                keep(2 * i + 1, 1)

        @block.vector
        def _(dve):
            v = nc.vector
            dve.wait_ge(loaded, 48)

            def chunk(c):
                ln.dve_stats(dve, c)
                ln.dve_norm(dve, c)
                dve.wait_ge(ln.h, c + 1)
                v.tensor_copy(cols(h_fm, c), hc[:]).then_inc(h_kept, 1)
                dve.wait_ge(lg_done, c + 1)
                v.tensor_copy(lg[:, ds(c * CT * EXPERTS, CT * EXPERTS)], ps[:, 1, 0:CT * EXPERTS]).then_inc(lg_kept, 1)

            with dve.Fori(0, CHUNKS) as c:
                chunk(c)

            s = Steps(dve, step)
            dve.wait_ge(scored, 1)
            per_tile = lambda t: t[:].rearrange("p (t e) -> p t e", e=EXPERTS)
            s.done(v.tensor_tensor(per_tile(sfc), per_tile(lg), gate_b[:].unsqueeze(1).broadcast_to([P, TILES, EXPERTS]), ALU.add))
            q = sfc[:].rearrange("p (g e) -> p g e", e=EPG)
            s.done(v.tensor_tensor(hi[:], q[:, :, 0:4], q[:, :, 4:8], ALU.max), False)
            s.done(v.tensor_tensor(lo[:], q[:, :, 0:4], q[:, :, 4:8], ALU.min))
            for w in (2, 1):
                s.done(v.tensor_tensor(th[:, :, 0:w], hi[:, :, 0:w], hi[:, :, w:2 * w], ALU.min), False)
                s.done(v.tensor_tensor(tl[:, :, 0:w], lo[:, :, 0:w], lo[:, :, w:2 * w], ALU.max))
                s.done(v.tensor_tensor(hi[:, :, 0:w], hi[:, :, 0:w], hi[:, :, w:2 * w], ALU.max), False)
                s.done(v.tensor_tensor(lo[:, :, 0:w], th[:, :, 0:w], tl[:, :, 0:w], ALU.max))
            s.done(v.tensor_tensor(gs[:], hi[:, :, 0], lo[:, :, 0], ALU.add))
            own = gs[:].rearrange("p (t g) -> p t g", g=EGROUPS)
            for t4 in range(4):
                r = slice(8 * t4, 8 * t4 + 8)
                a = own[:, r, :].unsqueeze(2).broadcast_to([P, 8, EGROUPS, EGROUPS])
                b = own[:, r, :].unsqueeze(3).broadcast_to([P, 8, EGROUPS, EGROUPS])
                o0 = w0[:, 512 * t4:512 * t4 + 512].rearrange("p (t g e) -> p t g e", g=EGROUPS, e=EGROUPS)
                o1 = w1[:, 512 * t4:512 * t4 + 512].rearrange("p (t g e) -> p t g e", g=EGROUPS, e=EGROUPS)
                s.done(v.tensor_tensor(o0, a, b, ALU.is_gt), False)
                s.done(v.tensor_tensor(o1, a, b, ALU.is_equal), t4 == 3)
            s.done(v.tensor_tensor(w1[:].rearrange("p (t g) -> p t g", g=64), w1[:].rearrange("p (t g) -> p t g", g=64),
                                   less[:].rearrange("p g e -> p (g e)").unsqueeze(1).broadcast_to([P, TILES, 64]), ALU.mult))
            s.done(v.tensor_tensor(w0[:], w0[:], w1[:], ALU.add))
            s.done(v.tensor_reduce(rank[:], w0[:].rearrange("p (g e) -> p g e", e=EGROUPS), AX.X, ALU.add))
            s.done(v.tensor_scalar(rank[:], rank[:], float(TOP_GROUPS), None, ALU.is_lt))
            s.done(v.tensor_tensor(sfc[:].rearrange("p (g e) -> p g e", e=EPG), q,
                                   rank[:].unsqueeze(2).broadcast_to([P, G, EPG]), ALU.mult))
            for t in range(TILES):
                s.done(v.max(top[:, t, :], per_tile(sfc)[:, t, :]), t == TILES - 1)
            for t in range(TILES):
                s.done(v.match_replace(out=per_tile(w0)[:, t, :], in_to_replace=top[:, t, :], in_values=per_tile(sfc)[:, t, :],
                                       imm_value=TAKEN), t == TILES - 1)
            s.done(v.scalar_tensor_tensor(w1[:], w0[:], TAKEN / 2, lg[:], ALU.is_lt, ALU.mult))
            s.done(v.tensor_reduce(den[:], per_tile(w1), AX.X, ALU.add))
            s.done(v.tensor_scalar(den[:], den[:], 1e-20, None, ALU.add))
            s.done(v.reciprocal(rden[:], den[:]))
            s.done(v.tensor_tensor(per_tile(w1), per_tile(w1), rden[:].unsqueeze(2).broadcast_to([P, TILES, EXPERTS]), ALU.mult))
            s.done(v.tensor_scalar(w1[:], w1[:], ROUTED_SCALE, None, ALU.mult))
            part = lambda i: parts[:, :, :, i, :].rearrange("p t g e -> p (t g) e")
            half = lambda t: t[:].rearrange("p (t e) -> p t e", e=EHALF)
            s.done(v.tensor_copy(part(0), half(w1)))
            s.done(v.tensor_tensor(half(w0), half(w1), part(0), ALU.subtract))
            s.done(v.tensor_copy(part(1), half(w0)))
            s.done(v.tensor_tensor(half(w1), half(w0), part(1), ALU.subtract))
            v.tensor_copy(part(2), half(w1)).then_inc(cut, 1)

            def keep(c, k):
                dve.wait_ge(tr_done, c + 1)
                v.tensor_copy(T["rw"][0:PARTS * EHALF, 1, ds(c * CHUNK, CHUNK)], ps[0:PARTS * EHALF, 3 + 2 * (k % 2), :])\
                    .then_inc(tr_kept[1], 1)

            with dve.Fori(0, CHUNKS // 2) as i:
                keep(2 * i, 0)
                keep(2 * i + 1, 1)


ROUTED_TILES = EXPERTS * HIDDEN // P
SHARED_TILES, SHARED_ROWS = 2, HIDDEN
HT = ROUTED_TILES + SHARED_TILES
HALF_TILES = ROUTED_TILES // 2
KD = 2 * DEPTH
STATE = CB * HEADS * DEPTH * KD
QKV1 = 3 * D + HEADS
DPFP_EPS = 1e-6
E1 = 9
EARLY_LOADS = ("wg", "wu", "wqkv", "wo", "wr", "ident_bf")
FFN0_LOADS = len(EARLY_LOADS) + 3
FFN1_LOADS = 3
LAG = 2


def experts0(nc, T, A):
    x_fm, h_fm, ps, rw, sel = T["x_fm"], T["h_fm"], T["psum"], T["rw"], T["sel"]
    wg, wu, wd, wqkv, wo, wr = (T[k] for k in ("wg", "wu", "wd", "wqkv", "wo", "wr"))
    with ExitStack() as ctx:
        def sb(name, shape, dt=F32):
            return ctx.enter_context(nc.sbuf_tensor(name, shape, dt))

        def sem(name):
            return ctx.enter_context(nc.semaphore(name))

        act_g = gu = sb("e0_gu", [P, 2, CHUNK])
        hm = sb("e0_hm", [P, 2, CHUNK])
        xa = xb = sb("e0_x", [P, CHUNK])
        ha = hb = y_fm = sb("e0_h", [P, CHUNK])
        nt = sb("e0_nt", [P, CT, D])
        upd = sb("e0_upd", [P, CHUNK])
        y_tm = sb("e0_y", [P, CT, D])
        phi = sb("e0_phi", [P, 2, CT * HEADS, KD])
        psum_r = sb("e0_psum", [P, 2 * CT * HEADS])
        prec = sb("e0_prec", [P, 2 * CT * HEADS])
        vv = sb("e0_v", [P, CT, D])
        beta = sb("e0_beta", [P, CT, HEADS])
        state = sb("e0_state", [P, CB * HEADS, DEPTH, KD])
        t1 = sb("e0_t1", [P, CB * HEADS, DEPTH, KD])
        t2 = sb("e0_t2", [P, CB * HEADS, DEPTH, KD])
        vbar = sb("e0_vbar", [P, CB * HEADS, DEPTH])
        u = sb("e0_u", [P, CB * HEADS, DEPTH])
        raw = t1[:].rearrange("p a v k -> p (a v k)")[:, 0:2 * CT * HEADS * KD].rearrange("p (q a k) -> p q a k", q=2, k=KD)
        GB, UB, RB, ACC, SIDE = (0, 1), (2, 3), (4, 5), 6, 7
        side = ps[:, SIDE, :]
        ln_a = LayerNorm(nc, ctx, "e0_lna", T, xa, ha, nt, SIDE, 2)
        ln_b = LayerNorm(nc, ctx, "e0_lnb", T, xb, hb, nt, SIDE, 3)

        gate_done = sem("e0_gate_done")
        ur_done = sem("e0_ur_done")
        silu_done = sem("e0_silu_done")
        gu_done = sem("e0_gu_done")
        hm_done = sem("e0_hm_done")
        acc_done = sem("e0_acc_done")
        x_new = sem("e0_x_new")
        x_kept = sem("e0_x_kept")
        pr_done = sem("e0_pr_done")
        pr_kept = sem("e0_pr_kept")
        beta_done = sem("e0_beta_done")
        pool_step = sem("e0_pool_step")
        phi_sum = sem("e0_phi_sum")
        vbar_done = sem("e0_vbar_done")
        y_done = sem("e0_y_done")
        yt_done = sem("e0_yt_done")
        yfm_done = sem("e0_yfm_done")
        wo_done = sem("e0_wo_done")
        upd_done = sem("e0_upd_done")
        xb_done = sem("e0_xb_done")
        xb_kept = sem("e0_xb_kept")
        h1_kept = sem("e0_h1_kept")
        lg1_done = sem("e0_lg1_done")
        lg1_kept = sem("e0_lg1_kept")
        u_step = sem("e0_u_step")
        state_zero = sem("e0_state_zero")
        block = ctx.enter_context(nc.Block())

        PHI, NORM, PRODUCTS = 2, 3, 4
        POOL_STEPS = NORM + CB * PRODUCTS

        def pool_at(m, step, s, p):
            return POOL_STEPS * m + (step if step else NORM + PRODUCTS * s + p)

        def live(k):
            return {"ffn": 0 <= k < CHUNKS, "a": 0 <= k - 1 < CHUNKS, "b": 0 <= k - 2 < CHUNKS}

        def run(eng, iteration):
            for c in range(3):
                iteration(c, c)
            with eng.Fori(3, CHUNKS) as c:
                iteration(c, 3)
            iteration(CHUNKS, CHUNKS)
            iteration(CHUNKS + 1, CHUNKS + 1)

        def rows(j):
            return P if j < ROUTED_TILES else SHARED_ROWS

        def hid(w, j):
            at = P * j if j < ROUTED_TILES else P * ROUTED_TILES + SHARED_ROWS * (j - ROUTED_TILES)
            return w[:, at:at + rows(j)]

        @block.tensor
        def _(pe):
            pe.wait_ge(T["ffn0_loaded"], 16 * FFN0_LOADS)

            def down(c, j, k):
                if j == 0 and k > 0:
                    pe.wait_ge(x_new, c)
                pe.wait_ge(hm_done, HT * c + j + 1)
                mm = pe.matmul(ps[:, ACC, :], wd[0:rows(j), j, :], hm[0:rows(j), j % 2, :], start=(j == 0), stop=(j == HT - 1))
                if j == HT - 1:
                    mm.then_inc(acc_done, 1)

            def tile(c, j, k):
                r = rows(j)
                g = HT * c + j
                if k > 0 or j >= 2:
                    pe.wait_ge(silu_done, g - 1)
                pe.matmul(ps[0:r, GB[j % 2], :], hid(wg, j), cols(h_fm, c), start=True, stop=True).then_inc(gate_done, 1)
                if j >= LAG:
                    down(c, j - LAG, k)
                elif k > 0:
                    down(c - 1, HT - LAG + j, k)
                if k > 0 or j >= 2:
                    pe.wait_ge(hm_done, g - 1)
                mm = pe.matmul(ps[0:r, UB[j % 2], :], hid(wu, j), cols(h_fm, c), start=True, stop=True)
                if j < ROUTED_TILES:
                    mm = pe.matmul(ps[:, RB[j % 2], :], sel[0:PARTS * EHALF, j % HALF_TILES, :],
                                   rw[0:PARTS * EHALF, j // HALF_TILES, ds(c * CHUNK, CHUNK)], start=True, stop=True)
                mm.then_inc(ur_done, 1)

            def project(m, t):
                if t == 0:
                    pe.wait_ge(ln_a.h, m + 1)
                else:
                    pe.wait_ge(pr_kept, CT * m + t)
                pe.matmul(side[:, 0:QKV1], ha[:, t * P:(t + 1) * P], wqkv[:], start=True, stop=True).then_inc(pr_done, 1)

            def iteration(c, k):
                f = live(k)
                for j in range(HT):
                    if f["a"]:
                        m = c - 1
                        if j == 3:
                            pe.wait_ge(x_new, m + 1)
                            if k > 1:
                                pe.wait_ge(beta_done, m)
                            if k > 2:
                                pe.wait_ge(lg1_kept, m - 1)
                            ln_a.pe_x(pe)
                        if j == 6:
                            ln_a.pe_n(pe, m)
                        if 8 <= j < 8 + CT:
                            project(m, j - 8)
                    if f["b"]:
                        m = c - 2
                        if j == 14:
                            if f["a"]:
                                pe.wait_ge(beta_done, c)
                            else:
                                pe.wait_ge(lg1_kept, m)
                            pe.wait_ge(y_done, 4 * m + 4)
                            for t in range(CT):
                                mm = pe.transpose(side[:, t * P:(t + 1) * P], y_tm[:, t, :], T["ident"][:])
                            mm.then_inc(yt_done, 1)
                        if j == 16:
                            pe.wait_ge(yfm_done, m + 1)
                            pe.matmul(side, wo[:], y_fm[:], start=True, stop=True).then_inc(wo_done, 1)
                        if j == 19:
                            pe.wait_ge(xb_done, m + 1)
                            ln_b.pe_x(pe)
                        if j == 22:
                            ln_b.pe_n(pe, m)
                        if j == 24:
                            pe.wait_ge(ln_b.h, m + 1)
                            for t in range(CT):
                                mm = pe.matmul(side[:, t * E1:(t + 1) * E1], hb[:, t * P:(t + 1) * P], wr[:], start=True, stop=True)
                            mm.then_inc(lg1_done, 1)
                    if f["ffn"]:
                        tile(c, j, k)
                    elif f["a"] and j < LAG:
                        down(c - 1, HT - LAG + j, k)

            run(pe, iteration)

        @block.scalar
        def _(act):
            a = nc.scalar.activation

            def iteration(c, k):
                f = live(k)
                for j in range(HT):
                    if f["ffn"]:
                        r, g = rows(j), HT * c + j
                        act.wait_ge(gate_done, g + 1)
                        if k > 0 or j >= 2:
                            act.wait_ge(hm_done, g - 1)
                        a(act_g[0:r, j % 2, :], ps[0:r, GB[j % 2], :], ACT.Silu).then_inc(silu_done, 1)
                    if f["a"]:
                        m = c - 1
                        if j == 2:
                            act.wait_ge(x_new, m + 1)
                            a(cols(x_fm, m), xa[:], ACT.Copy).then_inc(x_kept, 1)
                        if j == 4:
                            ln_a.act_std(act, m)
                        if j == 6:
                            if k > 2:
                                act.wait_ge(h1_kept, m - 1)
                            ln_a.act_h(act, m)
                        if 8 <= j < 8 + CT:
                            t = j - 8
                            if t == 0 and k > 1:
                                act.wait_ge(vbar_done, 4 * m)
                                act.wait_ge(pool_step, pool_at(m - 1, 0, CB - 1, PRODUCTS))
                            act.wait_ge(pr_done, CT * m + t + 1)
                            qk = side[:, 0:2 * D].rearrange("p (q h d) -> p q h d", q=2, d=DEPTH)
                            a(raw[:, :, HEADS * t:HEADS * (t + 1), 0:DEPTH], qk, ACT.Relu)
                            a(raw[:, :, HEADS * t:HEADS * (t + 1), DEPTH:KD], qk, ACT.Relu, scale=-1.0)
                            a(vv[:, t, :], side[:, 2 * D:3 * D], ACT.Copy)
                            a(beta[:, t, :], side[:, 3 * D:QKV1], ACT.Copy).then_inc(pr_kept, 1)
                            if t == CT - 1:
                                act.wait_ge(pr_kept, CT * m + CT)
                                a(beta[:], beta[:], ACT.Sigmoid).then_inc(beta_done, 1)
                    if f["b"]:
                        m = c - 2
                        if j == 14:
                            act.wait_ge(yt_done, m + 1)
                            a(y_fm[:], side, ACT.Copy).then_inc(yfm_done, 1)
                        if j == 16:
                            act.wait_ge(wo_done, m + 1)
                            for i in range(CB):
                                b = CB * m + i
                                ins = a(upd[:, i * SEQ:(i + 1) * SEQ], side[:, i * SEQ:(i + 1) * SEQ], ACT.Identity,
                                        bias=T["ga_bo"][:, ds(b, 1)], scale=T["gate"][:, 2, ds(b, 1)])
                            ins.then_inc(upd_done, 1)
                        if j == 18:
                            act.wait_ge(xb_done, m + 1)
                            a(cols(x_fm, m), xb[:], ACT.Copy).then_inc(xb_kept, 1)
                        if j == 20:
                            ln_b.act_std(act, m)
                        if j == 22:
                            if k > 2:
                                act.wait_ge(h1_kept, m)
                            ln_b.act_h(act, m)
                        if j == 24:
                            act.wait_ge(lg1_done, m + 1)
                            a(T["lg1"][:, ds(m * CT * E1, CT * E1)], side[:, 0:CT * E1], ACT.Copy).then_inc(lg1_kept, 1)

            run(act, iteration)

        @block.vector
        def _(dve):
            v = nc.vector

            def product_sum(out, src, half):
                o = out.rearrange("p (z a) -> p z a", z=2)[:, half, :]
                s = src[:].rearrange("p (z a) v k -> p z (a v) k", z=2)[:, half]
                return v.tensor_reduce(o, s, AX.X, ALU.add)

            def iteration(c, k):
                f = live(k)
                for j in range(HT):
                    if f["ffn"]:
                        r, g = rows(j), HT * c + j
                        dve.wait_ge(silu_done, g + 1)
                        dve.wait_ge(ur_done, g + 1)
                        out = gu if j < ROUTED_TILES else hm
                        ins = v.tensor_tensor(out[0:r, j % 2, :], ps[0:r, UB[j % 2], :], act_g[0:r, j % 2, :], ALU.mult)
                        if j < ROUTED_TILES:
                            ins.then_inc(gu_done, 1)
                            dve.wait_ge(gu_done, ROUTED_TILES * c + j + 1)
                            v.tensor_tensor(hm[:, j % 2, :], ps[:, RB[j % 2], :], gu[:, j % 2, :], ALU.mult).then_inc(hm_done, 1)
                        else:
                            ins.then_inc(hm_done, 1)
                    if f["a"]:
                        m = c - 1
                        if j == 1:
                            dve.wait_ge(acc_done, m + 1)
                            if k > 1:
                                dve.wait_ge(ln_a.x_tm, m)
                            if k > 2:
                                dve.wait_ge(xb_kept, m - 1)
                            for i in range(CB):
                                b = CB * m + i
                                ins = v.scalar_tensor_tensor(xa[:, i * SEQ:(i + 1) * SEQ], ps[:, ACC, i * SEQ:(i + 1) * SEQ],
                                                             T["gate"][:, 1, ds(b, 1)], cols(x_fm, b, SEQ), ALU.mult, ALU.add)
                            ins.then_inc(x_new, 1)
                        if j == 3:
                            ln_a.dve_stats(dve, m)
                        if j == 4:
                            ln_a.dve_norm(dve, m)
                        if j == 14:
                            dve.wait_ge(pool_step, pool_at(m, PHI, 0, 0))
                            v.tensor_reduce(psum_r[:], phi[:].rearrange("p q a k -> p (q a) k"), AX.X, ALU.add).then_inc(phi_sum, 1)
                            dve.wait_ge(phi_sum, 3 * m + 1)
                            v.tensor_scalar(psum_r[:], psum_r[:], DPFP_EPS, None, ALU.add).then_inc(phi_sum, 1)
                            dve.wait_ge(phi_sum, 3 * m + 2)
                            v.reciprocal(prec[:], psum_r[:]).then_inc(phi_sum, 1)
                        for s in range(CB):
                            for half in range(2):
                                if j == (21, 37)[s] + half:
                                    dve.wait_ge(pool_step, pool_at(m, 0, s, 1))
                                    product_sum(vbar[:].rearrange("p a v -> p (a v)"), t1, half).then_inc(vbar_done, 1)
                                if s == 0 and j == 34 + half:
                                    dve.wait_ge(pool_step, pool_at(m, 0, s, 4))
                                    if k > 1:
                                        dve.wait_ge(yt_done, m)
                                    product_sum(y_tm[:, 0:CB, :].rearrange("p t d -> p (t d)"), t2, half).then_inc(y_done, 1)
                    if f["b"]:
                        m = c - 2
                        if j in (5, 6):
                            dve.wait_ge(pool_step, pool_at(m, 0, CB - 1, 4))
                            product_sum(y_tm[:, CB:CT, :].rearrange("p t d -> p (t d)"), t2, j - 5).then_inc(y_done, 1)
                        if j == 17:
                            dve.wait_ge(upd_done, m + 1)
                            if k > 2:
                                dve.wait_ge(ln_b.x_tm, m)
                            dve.wait_ge(x_kept, m + 2 if f["a"] else CHUNKS)
                            v.tensor_tensor(xb[:], cols(x_fm, m), upd[:], ALU.add).then_inc(xb_done, 1)
                        if j == 19:
                            ln_b.dve_stats(dve, m)
                        if j == 20:
                            ln_b.dve_norm(dve, m)
                        if j == 23:
                            dve.wait_ge(ln_b.h, m + 1)
                            v.tensor_copy(cols(h_fm, m), hb[:]).then_inc(h1_kept, 1)

            run(dve, iteration)

        @block.gpsimd
        def _(pool):
            tt = nc.gpsimd.tensor_tensor
            nc.gpsimd.memset(state[:], 0.0).then_inc(state_zero, 1)
            pool.wait_ge(state_zero, 1)
            F = CB * HEADS
            wide = lambda ap: ap.unsqueeze(3).broadcast_to([P, F, DEPTH, KD])
            tall = lambda ap: ap.unsqueeze(2).broadcast_to([P, F, DEPTH, KD])

            def chunk(m, first):
                base = POOL_STEPS * m
                pool.wait_ge(pr_kept, CT * m + CT)
                flat = lambda t: t.rearrange("p q a k -> p (q a) k")
                r, o = flat(raw), phi[:].rearrange("p q a k -> p (q a) k")
                tt(o[:, :, 1:KD], r[:, :, 1:KD], r[:, :, 0:KD - 1], ALU.mult).then_inc(pool_step, 1)
                tt(o[:, :, 0], r[:, :, 0], r[:, :, KD - 1], ALU.mult).then_inc(pool_step, 1)
                pool.wait_ge(phi_sum, 3 * m + 3)
                tt(o, o, prec[:].unsqueeze(2).broadcast_to([P, 2 * CT * HEADS, KD]), ALU.mult).then_inc(pool_step, 1)
                pool.wait_ge(pool_step, base + NORM)
                pool.wait_ge(beta_done, m + 1)
                for s in range(CB):
                    at = base + NORM + PRODUCTS * s
                    q, key = phi[:, 0, F * s:F * (s + 1), :], phi[:, 1, F * s:F * (s + 1), :]
                    val = vv[:, CB * s:CB * (s + 1), :].rearrange("p t (h v) -> p (t h) v", v=DEPTH)
                    bt = beta[:, CB * s:CB * (s + 1), :].rearrange("p t h -> p (t h)").unsqueeze(2).broadcast_to([P, F, DEPTH])
                    tt(t1[:], state[:], tall(key), ALU.mult).then_inc(pool_step, 1)
                    pool.wait_ge(vbar_done, 4 * m + 2 * s + 2)
                    tt(u[:], val, vbar[:], ALU.subtract).then_inc(u_step, 1)
                    pool.wait_ge(u_step, 2 * (CB * m + s) + 1)
                    tt(u[:], u[:], bt, ALU.mult).then_inc(u_step, 1)
                    pool.wait_ge(u_step, 2 * (CB * m + s) + 2)
                    if not (first and s == 0):
                        pool.wait_ge(y_done, 4 * m + 2 * s)
                    tt(t2[:], wide(u[:]), tall(key), ALU.mult).then_inc(pool_step, 1)
                    pool.wait_ge(pool_step, at + 2)
                    tt(state[:], state[:], t2[:], ALU.add).then_inc(pool_step, 1)
                    pool.wait_ge(pool_step, at + 3)
                    tt(t2[:], state[:], tall(q), ALU.mult).then_inc(pool_step, 1)
                    pool.wait_ge(pool_step, at + 4)

            chunk(0, True)
            with pool.Fori(1, CHUNKS) as m:
                chunk(m, False)


F1 = 512
F1T = F1 // P


def route1(nc, T, A):
    ps = T["psum"]
    with ExitStack() as ctx:
        def sb(name, shape, dt=F32):
            return ctx.enter_context(nc.sbuf_tensor(name, shape, dt))

        def sem(name):
            return ctx.enter_context(nc.semaphore(name))

        rb = sb("r1_b", [P, E1])
        less = sb("r1_less", [P, E1, E1])
        mx, sm, rs = (sb(f"r1_{n}", [P, TILES]) for n in ("mx", "sm", "rs"))
        pr, w0, w1 = (sb(f"r1_{n}", [P, TILES, E1]) for n in ("pr", "w0", "w1"))
        rank = sb("r1_rank", [P, TILES, E1])
        c0, c1 = (sb(f"r1_{n}", [P, TILES, E1 * E1]) for n in ("c0", "c1"))
        parts = sb("r1_parts", [P, TILES, PARTS, E1], BF16)
        loaded = sem("r1_loaded")
        shifted = sem("r1_shifted")
        exp_done = sem("r1_exp_done")
        step = sem("r1_step")
        cut = sem("r1_cut")
        tr_done = sem("r1_tr_done")
        block = ctx.enter_context(nc.Block())

        @block.sync
        def _(sp):
            sp.dma_start(rb[:], A["b_r1"]).then_inc(loaded, 16)
            sp.dma_start(less[:], A["less9"]).then_inc(loaded, 16)
            for name in ("sel1", "w1", "w2"):
                sp.dma_start(T[name][:], A[name]).then_inc(T["ffn1_loaded"], 16)

        @block.tensor
        def _(pe):
            pe.wait_ge(cut, 1)
            for c in range(CHUNKS):
                for t in range(CT):
                    mm = pe.matmul(ps[0:PARTS * E1, c, t * P:(t + 1) * P],
                                   parts[:, CT * c + t, :, :].rearrange("p i e -> p (i e)"), T["ident_bf"][:], start=True, stop=True)
                mm.then_inc(tr_done, 1)

        @block.scalar
        def _(act):
            act.wait_ge(shifted, 1)
            nc.scalar.activation(pr[:], w0[:], ACT.Exp).then_inc(exp_done, 1)
            for c in range(0, CHUNKS, 2):
                act.wait_ge(tr_done, c + 1)
                nc.scalar.activation(T["g1"][0:PARTS * E1, c * CHUNK:(c + 1) * CHUNK], ps[0:PARTS * E1, c, :], ACT.Copy)

        @block.vector
        def _(dve):
            v = nc.vector
            s = Steps(dve, step)
            lg = T["lg1"][:].rearrange("p (t e) -> p t e", e=E1)
            over = lambda ap: ap.unsqueeze(2).broadcast_to([P, TILES, E1])
            dve.wait_ge(loaded, 32)
            s.done(v.tensor_tensor(w1[:], lg, rb[:].unsqueeze(1).broadcast_to([P, TILES, E1]), ALU.add))
            s.done(v.tensor_reduce(mx[:], w1[:], AX.X, ALU.max))
            v.tensor_tensor(w0[:], w1[:], over(mx[:]), ALU.subtract).then_inc(shifted, 1)
            dve.wait_ge(exp_done, 1)
            s.done(v.tensor_reduce(sm[:], pr[:], AX.X, ALU.add))
            s.done(v.reciprocal(rs[:], sm[:]))
            s.done(v.tensor_tensor(pr[:], pr[:], over(rs[:]), ALU.mult))
            for t in range(TILES // 16):
                r = slice(16 * t, 16 * t + 16)
                a = pr[:, r, :].unsqueeze(2).broadcast_to([P, 16, E1, E1])
                b = pr[:, r, :].unsqueeze(3).broadcast_to([P, 16, E1, E1])
                o = lambda c: c[:, r, :].rearrange("p t (g e) -> p t g e", e=E1)
                s.done(v.tensor_tensor(o(c0), a, b, ALU.is_gt), False)
                s.done(v.tensor_tensor(o(c1), a, b, ALU.is_equal))
            s.done(v.tensor_tensor(c1[:], c1[:], less[:].rearrange("p g e -> p (g e)").unsqueeze(1).broadcast_to([P, TILES, E1 * E1]),
                                   ALU.mult))
            s.done(v.tensor_tensor(c0[:], c0[:], c1[:], ALU.add))
            s.done(v.tensor_reduce(rank[:].rearrange("p t e -> p (t e)"), c0[:].rearrange("p t (g e) -> p (t g) e", e=E1), AX.X, ALU.add))
            s.done(v.scalar_tensor_tensor(w0[:], rank[:], 2.0, pr[:], ALU.is_lt, ALU.mult))
            s.done(v.tensor_copy(parts[:, :, 0, :], w0[:]))
            s.done(v.tensor_tensor(w1[:], w0[:], parts[:, :, 0, :], ALU.subtract))
            s.done(v.tensor_copy(parts[:, :, 1, :], w1[:]))
            s.done(v.tensor_tensor(w0[:], w1[:], parts[:, :, 1, :], ALU.subtract))
            v.tensor_copy(parts[:, :, 2, :], w0[:]).then_inc(cut, 1)
            for c in range(1, CHUNKS, 2):
                dve.wait_ge(tr_done, c + 1)
                v.tensor_copy(T["g1"][0:PARTS * E1, c * CHUNK:(c + 1) * CHUNK], ps[0:PARTS * E1, c, :])


NE1 = E1 - 1
T1 = NE1 * F1T
RING = 4


def experts1(nc, T, A, out):
    x_fm, h_fm, ps, g1, sel1, w1, w2 = (T[k] for k in ("x_fm", "h_fm", "psum", "g1", "sel1", "w1", "w2"))
    with ExitStack() as ctx:
        def sb(name, shape, dt=F32):
            return ctx.enter_context(nc.sbuf_tensor(name, shape, dt))

        def sem(name):
            return ctx.enter_context(nc.semaphore(name))

        ge = sb("e1_gelu", [P, 2, CHUNK])
        hm = sb("e1_hm", [P, RING, CHUNK])
        nh = sb("e1_null", [P, CHUNK])
        HB, RB, ACC, NB = (0, 1), (2, 3), 4, 5
        up_done = sem("e1_up_done")
        gelu_done = sem("e1_gelu_done")
        r_done = sem("e1_r_done")
        rn_done = sem("e1_rn_done")
        nh_done = sem("e1_nh_done")
        hm_done = sem("e1_hm_done")
        acc_done = sem("e1_acc_done")
        x_done = sem("e1_x_done")
        stored = sem("e1_stored")
        block = ctx.enter_context(nc.Block())

        @block.tensor
        def _(pe):
            pe.wait_ge(T["ffn1_loaded"], 16 * FFN1_LOADS)

            def spread(c, e):
                return pe.matmul(ps[:, NB if e == NE1 else RB[e % 2], :], sel1[0:PARTS * E1, e, :],
                                 g1[0:PARTS * E1, ds(c * CHUNK, CHUNK)], start=True, stop=True)

            def down(c, j, k):
                if j == 0:
                    if k > 0:
                        pe.wait_ge(x_done, c)
                    pe.wait_ge(nh_done, c + 1)
                    pe.matmul(ps[:, ACC, :], T["ident"][:], nh[:], start=True, stop=False)
                pe.wait_ge(hm_done, T1 * c + j + 1)
                mm = pe.matmul(ps[:, ACC, :], w2[:, j, :], hm[:, j % RING, :], start=False, stop=(j == T1 - 1))
                if j == T1 - 1:
                    mm.then_inc(acc_done, 1)

            def iteration(c, k):
                for j in range(T1):
                    e, g = j // F1T, T1 * c + j
                    if j % F1T == 0 and (k > 0 or e >= 2):
                        pe.wait_ge(hm_done, g - F1T)
                    if k > 0 or j >= 2:
                        pe.wait_ge(gelu_done, g - 1)
                    pe.matmul(ps[:, HB[j % 2], :], w1[:, j, :], cols(h_fm, c), start=True, stop=True).then_inc(up_done, 1)
                    if j >= LAG:
                        down(c, j - LAG, k)
                    elif k > 0:
                        down(c - 1, T1 - LAG + j, k)
                    if j == 0:
                        if k > 0:
                            pe.wait_ge(nh_done, c)
                        spread(c, NE1).then_inc(rn_done, 1)
                    if j % F1T == 0:
                        spread(c, e).then_inc(r_done, 1)

            iteration(0, 0)
            with pe.Fori(1, CHUNKS) as c:
                iteration(c, 1)
            for j in range(T1 - LAG, T1):
                down(CHUNKS - 1, j, 1)

        @block.scalar
        def _(act):
            def iteration(c, k):
                for j in range(T1):
                    g = T1 * c + j
                    act.wait_ge(up_done, g + 1)
                    if k > 0 or j >= 2:
                        act.wait_ge(hm_done, g - 1)
                    nc.scalar.activation(ge[:, j % 2, :], ps[:, HB[j % 2], :], ACT.Gelu).then_inc(gelu_done, 1)

            iteration(0, 0)
            with act.Fori(1, CHUNKS) as c:
                iteration(c, 1)

        @block.vector
        def _(dve):
            v = nc.vector

            def result(m):
                dve.wait_ge(acc_done, m + 1)
                for i in range(CB):
                    b = CB * m + i
                    x = cols(x_fm, b, SEQ)
                    ins = v.scalar_tensor_tensor(x, ps[:, ACC, i * SEQ:(i + 1) * SEQ], T["gate"][:, 3, ds(b, 1)], x, ALU.mult, ALU.add)
                ins.then_inc(x_done, 1)

            def iteration(c, k):
                for j in range(T1):
                    e, g = j // F1T, T1 * c + j
                    if j == 0:
                        dve.wait_ge(rn_done, c + 1)
                        v.tensor_tensor(nh[:], ps[:, NB, :], cols(h_fm, c), ALU.mult).then_inc(nh_done, 1)
                    dve.wait_ge(gelu_done, g + 1)
                    dve.wait_ge(r_done, NE1 * c + e + 1)
                    v.tensor_tensor(hm[:, j % RING, :], ps[:, RB[e % 2], :], ge[:, j % 2, :], ALU.mult).then_inc(hm_done, 1)
                    if k > 0 and j == LAG - 1:
                        result(c - 1)

            iteration(0, 0)
            with dve.Fori(1, CHUNKS) as c:
                iteration(c, 1)
            result(CHUNKS - 1)

        @block.sync
        def _(sp):
            with sp.Fori(0, CHUNKS) as c:
                sp.wait_ge(x_done, c + 1)
                sp.dma_start(cols(out, c), cols(x_fm, c)).then_inc(stored, 16)
            sp.wait_ge(stored, 16 * CHUNKS)


PI_ALL = 2 * DEPTH // 2
NAMES = ("x_fm", "x_tm", "c_fm", "wmod", "w_qk", "b_qk", "w_v", "b_v", "w_fc", "b_fc", "b_o", "ident", "rot", "ident_bf",
         "gate_w", "gate_b", "less8", "wg", "wu", "wd", "sd", "wqkv", "wo", "sel", "wr", "b_r1", "less9", "sel1", "w1", "w2")


def adaln_two_blocks(nc, *args):
    A, out = dict(zip(NAMES, args[:-1])), args[-1]
    with ExitStack() as ctx:
        T = {}

        def sb(name, shape, dt=F32, scope=ctx):
            T[name] = scope.enter_context(nc.sbuf_tensor(name, shape, dt))

        for name, shape in dict(x_fm=[P, TOK], h_fm=[P, TOK], ident=[P, P], bq_col=[P, 1], bk_col=[P, 1], bv_col=[P, 1],
                                bfc_col=[P, 1], bo_col=[P, 1], shift=[P, 4, BATCH], scale1=[P, 4, BATCH], gate=[P, 4, BATCH],
                                ga_bfc=[P, BATCH], ga_bo=[P, BATCH], lg1=[P, TILES * E1]).items():
            sb(name, shape)
        sb("ident_bf", [P, P], BF16)
        T["x_tm"] = T["h_fm"]
        T["psum"] = ctx.enter_context(nc.psum_tensor("psum", [P, 8, BANK], F32))
        for name in ("ffn0_loaded", "ffn1_loaded"):
            T[name] = ctx.enter_context(nc.semaphore(name))
        with ExitStack() as block0:
            hidden = EXPERTS * HIDDEN + SHARED_TILES * SHARED_ROWS
            for name, shape in dict(wg=[P, hidden], wu=[P, hidden], wqkv=[P, QKV1], wo=[P, D], wr=[P, E1]).items():
                sb(name, shape, scope=block0)
            with ExitStack() as first:
                for name, shape in dict(mean=[P, TILES], rstd=[P, TILES], w_qk=[P, 2 * D], w_v=[P, D], w_fc=[P, D]).items():
                    sb(name, shape, scope=first)
                setup(nc, T, A)
                attention(nc, T, T["x_fm"], T["x_tm"],
                          (T["scale1"][:, 0, :], T["shift"][:, 0, :], T["gate"][:, 0, :], T["ga_bfc"][:, :]))
            sb("wd", [P, HT, D], F32, block0)
            sb("sel", [PARTS * EHALF, HALF_TILES, P], BF16, block0)
            sb("rw", [P, 2, TOK], BF16, block0)
            route0(nc, T, A)
            experts0(nc, T, A)
        for name in ("w1", "w2"):
            sb(name, [P, T1, P])
        sb("sel1", [PARTS * E1, E1, P], BF16)
        sb("g1", [PARTS * E1, TOK], BF16)
        route1(nc, T, A)
        experts1(nc, T, A, out)


def layout(i):
    bf16 = mybir.dt.np(BF16)
    f = np.ascontiguousarray
    x = i["L0_attn_x"].reshape(TOK, D)
    w, b = i["L0_attn_w_qkv"], i["L0_attn_b_qkv"]
    a = {}
    a["x_fm"] = f(x.T)
    a["x_tm"] = f(x.reshape(TILES, P, D).transpose(1, 0, 2).reshape(P, TOK))
    a["c_fm"] = f(np.stack([i["L0_c"], i["L1_c"]]).transpose(2, 0, 1))
    a["wmod"] = f(np.stack([i["L0_wmod"], i["L1_wmod"]]).transpose(1, 0, 2))
    a["w_qk"] = f(w[:, :2 * D].reshape(D, 2, HEADS, DEPTH).transpose(0, 1, 3, 2).reshape(D, 2 * D))
    a["b_qk"] = f(b[:2 * D].reshape(2, HEADS, DEPTH).transpose(0, 2, 1).reshape(1, 2 * D))
    a["w_v"] = f(w[:, 2 * D:])
    a["b_v"] = f(b[2 * D:].reshape(D, 1))
    a["w_fc"] = i["L0_attn_w_fc"]
    a["b_fc"] = f(i["L0_attn_b_fc"].reshape(D, 1))
    a["b_o"] = f(i["L1_attn_bo"].reshape(D, 1))
    a["ident"] = np.eye(P, dtype=np.float32)
    inv = (1.0 / 10000.0 ** (np.arange(0, DEPTH, 2, dtype=np.float32) / DEPTH)).astype(np.float32)
    ang = (np.arange(HEADS, dtype=np.float32)[:, None] * inv[None, :]).astype(np.float32).T
    a["rot"] = f(np.broadcast_to(np.stack([np.tile(np.cos(ang), (2, 1)), np.tile(np.sin(ang), (2, 1))]), (P, 2, PI_ALL, HEADS)))
    a["ident_bf"] = np.eye(P).astype(bf16)
    a["gate_w"] = f(i["L0_ffn_gate_w"].T)
    a["gate_b"] = f(np.broadcast_to(i["L0_ffn_gate_bias"], (P, EXPERTS)))
    a["less8"] = f(np.broadcast_to(np.tril(np.ones((8, 8), np.float32), -1), (P, 8, 8)))
    for name, w, s in (("wg", "Wg", "Sg"), ("wu", "Wu", "Su")):
        rows = np.concatenate([i["L0_ffn_" + w].reshape(EXPERTS * HIDDEN, D), i["L0_ffn_" + s]])
        a[name] = f(rows.T)
    a["wd"] = f(i["L0_ffn_Wd"].transpose(0, 2, 1).reshape(ROUTED_TILES, P, D).transpose(1, 0, 2))
    a["sd"] = f(i["L0_ffn_Sd"].T.reshape(SHARED_TILES, SHARED_ROWS, D).transpose(1, 0, 2))
    a["wqkv"] = f(np.concatenate([i["L1_attn_W" + n] for n in "qkvb"], axis=1))
    a["wo"] = i["L1_attn_Wo"]
    owner = (np.arange(HALF_TILES * P) // HIDDEN).reshape(HALF_TILES, P)
    one_hot = (owner[None] == np.arange(EHALF)[:, None, None])
    a["sel"] = f(np.tile(one_hot, (PARTS, 1, 1)).astype(bf16))
    a["wr"] = i["L1_ffn_router_w"]
    a["b_r1"] = f(np.broadcast_to(i["L1_ffn_router_b"], (P, E1)))
    a["less9"] = f(np.broadcast_to(np.tril(np.ones((E1, E1), np.float32), -1), (P, E1, E1)))
    a["sel1"] = f(np.tile(np.broadcast_to(np.eye(E1)[:, :, None], (E1, E1, P)), (PARTS, 1, 1)).astype(bf16))
    a["w1"] = f(i["L1_ffn_w1"].reshape(NE1, D, F1T, P).transpose(1, 0, 2, 3).reshape(D, T1, P))
    a["w2"] = f(i["L1_ffn_w2"].reshape(NE1, F1T, P, D).transpose(2, 0, 1, 3).reshape(P, T1, D))
    return a


def kernel(**inputs):
    import concourse.bacc as bacc
    from concourse.bass_utils import run_bass_kernel_spmd

    nc = bacc.Bacc("TRN2", target_bir_lowering=False, num_devices=1)
    placed = layout({name: np.asarray(a) for name, a in inputs.items()})
    arrays = {f"in_{name}": np.ascontiguousarray(placed[name]) for name in NAMES}
    args = [nc.dram_tensor(f"in_{name}", arrays[f"in_{name}"].shape, mybir.dt.from_np(arrays[f"in_{name}"].dtype),
                           kind="ExternalInput").ap() for name in NAMES]
    args.append(nc.dram_tensor("out", (D, TOK), F32, kind="ExternalOutput").ap())
    adaln_two_blocks(nc, *args)
    r = run_bass_kernel_spmd(nc, [arrays], core_ids=[0])
    return np.ascontiguousarray(np.asarray(r.results[0]["out"]).T).reshape(BATCH, SEQ, D)
```

```python
from contextlib import ExitStack

import numpy as np

import concourse.bass as bass
from concourse import mybir

F32 = mybir.dt.float32
BF16 = mybir.dt.bfloat16
F32R = mybir.dt.float32r
ALU = mybir.AluOpType
ACT = mybir.ActivationFunctionType
AX = mybir.AxisListType

P = 128
D = 128
BATCH, SEQ = 16, 256
TOK = BATCH * SEQ
TILES = TOK // P
HEADS, DEPTH = 16, 8
LN_EPS = 1e-5
BANK = 512


def ds(start, size):
    return bass.ds(start, size)


PARTS = 3
PAIRS = PARTS * PARTS
ROWS = PAIRS * DEPTH
ROWS_M = ROWS + PARTS
HALF = HEADS // 2
GROUP = 4
GROUPS = HEADS // GROUP
BUFS = 3
STACK_DMAS = PARTS * PARTS + PARTS
VW = 32


def attention(nc, T, x_fm, x_tm, mod):
    ident = T["ident"]
    w_qk, w_v, w_fc, bq_col, bk_col, bv_col = (T[k] for k in ("w_qk", "w_v", "w_fc", "bq_col", "bk_col", "bv_col"))
    ca1, sa, ga, ga_bfc = mod
    rstd, nmean = T["rstd"], T["mean"]
    with ExitStack() as ctx:
        def sb(name, shape, dt=F32):
            return ctx.enter_context(nc.sbuf_tensor(name, shape, dt))

        def sem(name):
            return ctx.enter_context(nc.semaphore(name))

        xn = sb("at_xn", [P, 2, D])
        hb = sb("at_h", [P, BUFS, SEQ])
        qk = sb("at_qk", [P, 2 * SEQ])
        rest = sb("at_rest", [P, 2 * SEQ])
        rest2 = sb("at_rest2", [P, 2 * SEQ])
        part = sb("at_part", [P, PARTS, 2 * SEQ], BF16)
        qs = sb("at_qs", [P, BUFS, HEADS, SEQ], BF16)
        ks = sb("at_ks", [P, BUFS, HEADS, SEQ], BF16)
        v1 = sb("at_v", [P, BUFS, 2, HEADS, VW])
        negm = sb("at_negm", [P, BUFS, 2, HALF, 2])
        nrow = sb("at_nrow", [HALF, SEQ])
        nrest = sb("at_nrest", [HALF, SEQ])
        nrest2 = sb("at_nrest2", [HALF, SEQ])
        nzero = sb("at_nzero", [HALF, SEQ])
        npart = sb("at_npart", [HALF, PARTS, SEQ], BF16)
        pt = sb("at_p", [P, 2 * GROUP, 2, SEQ])
        osb = sb("at_o", [P, GROUPS, SEQ])
        rden = sb("at_rden", [P, 2, HEADS])
        a_tm = sb("at_a", [P, 2, HEADS, DEPTH])
        a_fm = sb("at_afm", [P, SEQ])
        upd = sb("at_upd", [P, SEQ])
        bounce = nc.dram_tensor("qk_parts", [BUFS, 2, PARTS, DEPTH, HEADS, SEQ], BF16, kind="Internal").ap()
        nbounce = nc.dram_tensor("max_parts", [BUFS, 2, PARTS, HALF, SEQ], BF16, kind="Internal").ap()
        ps = T["psum"]
        P1, P2, OB, M0, M1 = [0, 1], [2, 3], (4, 5), 6, 7
        o_ps = ps[:, 4:6, :].rearrange("p a c -> p (a c)")

        filled = sem("at_filled")
        zero_filled = sem("at_zero_filled")
        xn_ready = sem("at_xn_ready")
        xt_done = sem("at_xt_done")
        h_ready = sem("at_h_ready")
        qk_proj = sem("at_qk_proj")
        qk_ready = sem("at_qk_ready")
        part_ready = sem("at_part_ready")
        rest_ready = sem("at_rest_ready")
        part_out = sem("at_part_out")
        stacked = sem("at_stacked")
        p1_done = sem("at_p1_done")
        max_done = sem("at_max_done")
        nrow_ready = sem("at_nrow_ready")
        nsplit = sem("at_nsplit")
        nrows_out = sem("at_nrows_out")
        nrows_in = [sem(f"at_nrows_in{i}") for i in range(2)]
        vn_done = sem("at_vn_done")
        v_ready = sem("at_v_ready")
        p2_done = sem("at_p2_done")
        exp_done = sem("at_exp_done")
        pv_done = sem("at_pv_done")
        o_ready = sem("at_o_ready")
        ot_done = sem("at_ot_done")
        rden_ready = sem("at_rden_ready")
        a_ready = sem("at_a_ready")
        at_done = sem("at_at_done")
        afm_ready = sem("at_afm_ready")
        fc_done = sem("at_fc_done")
        upd_ready = sem("at_upd_ready")
        x_added = sem("at_x_added")
        block = ctx.enter_context(nc.Block())

        def live(k):
            return {
                "xn": 0 <= k + 2 < BATCH, "proj": 0 <= k + 1 < BATCH, "p1": 0 <= k < BATCH,
                "p2": 0 <= k - 1 < BATCH, "tail": 0 <= k - 2 < BATCH,
            }

        def run(eng, iteration):
            for n in range(-2, 2):
                iteration(n, n)
            with eng.Fori(0, (BATCH - 4) // BUFS) as i:
                for k in range(BUFS):
                    iteration(BUFS * i + 2 + k, 2 + k)
            for n in range(BATCH - 2, BATCH + 2):
                iteration(n, n)

        @block.tensor
        def _(pe):
            def transpose_negm(n, k, half, bank):
                pe.wait_ge(max_done, HEADS * n + HALF * (half + 1))
                for tt in range(2):
                    mm = pe.transpose(ps[0:HALF, bank, SEQ + tt * P:SEQ + (tt + 1) * P], negm[:, k % BUFS, half, :, tt], ident[:])
                return mm

            def scores(n, k, g):
                f = live(k)
                for h in range(GROUP * g, GROUP * (g + 1)):
                    if f["p1"]:
                        if h == 0:
                            pe.wait_ge(stacked, 16 * STACK_DMAS * (n + 1))
                        if k > 0 or h >= 2:
                            pe.wait_ge(max_done, HEADS * n + h - 1)
                        for tt in range(2):
                            mm = pe.matmul(ps[:, P1[h % 2], tt * SEQ:(tt + 1) * SEQ],
                                           qs[0:ROWS, k % BUFS, h, tt * P:(tt + 1) * P], ks[0:ROWS, k % BUFS, h, :],
                                           start=True, stop=True)
                        mm.then_inc(p1_done, 1)
                    if f["p2"]:
                        m, j = n - 1, k - 1
                        if h % HALF == 0:
                            pe.wait_ge(nrows_in[h // HALF], 16 * (m + 1))
                        if j > 0 or h >= 2:
                            pe.wait_ge(exp_done, HEADS * m + h - 1)
                        for st in range(2):
                            mm = pe.matmul(ps[:, P2[h % 2], st * SEQ:(st + 1) * SEQ],
                                           ks[0:ROWS_M, j % BUFS, h, st * P:(st + 1) * P], qs[0:ROWS_M, j % BUFS, h, :],
                                           start=True, stop=True)
                        mm.then_inc(p2_done, 1)

            def pv(m, j, g):
                pe.wait_ge(exp_done, HEADS * m + GROUP * (g + 1))
                if g == 0:
                    pe.wait_ge(v_ready, m + 1)
                    if j > 0:
                        pe.wait_ge(o_ready, m)
                for st in range(2):
                    for c in range(GROUP):
                        h = GROUP * g + c
                        mm = pe.matmul(o_ps[VW * c:VW * (c + 1), g * SEQ:(g + 1) * SEQ],
                                       v1[:, j % BUFS, st, h, :], pt[:, h % (2 * GROUP), st, :],
                                       start=(st == 0), stop=(st == 1), tile_position=(0, VW * c))
                mm.then_inc(pv_done, 1)

            def iteration(n, k):
                f = live(k)
                if f["proj"]:
                    pe.wait_ge(h_ready, n + 2)
                    if live(k - 1)["p1"]:
                        pe.wait_ge(nrow_ready, 2 * n - 1)
                    for c in range(2):
                        mm = pe.matmul(ps[:, M0, c * SEQ:(c + 1) * SEQ], w_qk[:, c * P:(c + 1) * P], hb[:, (k + 1) % BUFS, :],
                                       start=True, stop=True)
                    mm.then_inc(qk_proj, 1)
                scores(n, k, 0)
                if f["tail"]:
                    pv(n - 2, k - 2, GROUPS - 1)
                if f["p1"] or f["p2"]:
                    if f["p1"]:
                        if k >= 3:
                            pe.wait_ge(upd_ready, n - 2)
                        for st in range(2):
                            mm = pe.matmul(ps[:, M1, st * P:(st + 1) * P], hb[:, k % BUFS, st * P:(st + 1) * P], w_v[:],
                                           start=True, stop=True)
                    if f["p2"]:
                        if not f["p1"]:
                            pe.wait_ge(upd_ready, n - 2)
                        mm = transpose_negm(n - 1, k - 1, 1, M1)
                    mm.then_inc(vn_done, 1)
                if f["tail"]:
                    pe.wait_ge(o_ready, n - 1)
                    if k >= 3:
                        pe.wait_ge(a_ready, n - 2)
                        pe.wait_ge(upd_ready, n - 2)
                    if f["proj"]:
                        pe.wait_ge(qk_ready, n + 2)
                    if f["p1"] or f["p2"]:
                        pe.wait_ge(v_ready, n + 1)
                        pe.wait_ge(nrow_ready, 2 * n)
                    for tt in range(2):
                        for g in range(GROUPS):
                            mm = pe.transpose(ps[:, M0 + tt, g * P:(g + 1) * P], osb[:, g, tt * P:(tt + 1) * P], ident[:])
                    mm.then_inc(ot_done, 1)
                scores(n, k, 1)
                if f["p2"]:
                    pv(n - 1, k - 1, 0)
                if f["p1"] or f["xn"]:
                    if f["tail"]:
                        pe.wait_ge(a_ready, n - 1)
                    elif f["proj"] and k >= -1:
                        pe.wait_ge(qk_ready, n + 2)
                    if f["xn"]:
                        pe.wait_ge(xn_ready, n + 3)
                        for tt in range(2):
                            mm = pe.transpose(ps[:, M0, tt * P:(tt + 1) * P], xn[:, tt, :], ident[:])
                    if f["p1"]:
                        mm = transpose_negm(n, k, 0, M0)
                    mm.then_inc(xt_done, 1)
                scores(n, k, 2)
                if f["p2"]:
                    pv(n - 1, k - 1, 1)
                if f["tail"]:
                    pe.wait_ge(a_ready, n - 1)
                    for tt in range(2):
                        mm = pe.transpose(ps[:, M1, tt * P:(tt + 1) * P],
                                          a_tm[:, tt, :, :].rearrange("p h d -> p (h d)"), ident[:])
                    mm.then_inc(at_done, 1)
                scores(n, k, 3)
                if f["p2"]:
                    pv(n - 1, k - 1, 2)
                if f["tail"]:
                    pe.wait_ge(afm_ready, n - 1)
                    pe.matmul(ps[:, M1, 0:SEQ], w_fc[:], a_fm[:], start=True, stop=True).then_inc(fc_done, 1)

            run(pe, iteration)

        @block.vector
        def _(dve):
            def maxima(n, k, g):
                if not live(k)["p1"]:
                    return
                for h in range(GROUP * g, GROUP * (g + 1)):
                    dve.wait_ge(p1_done, HEADS * n + h + 1)
                    if h == 0 and k >= 2:
                        dve.wait_ge(vn_done, n)
                    nc.vector.tensor_reduce(negm[:, k % BUFS, h // HALF, h % HALF, :],
                                            ps[:, P1[h % 2], :].rearrange("p (t s) -> p t s", t=2),
                                            AX.X, ALU.max, negate=True).then_inc(max_done, 1)

            def iteration(n, k):
                f = live(k)
                if f["xn"]:
                    if k >= -1:
                        dve.wait_ge(xt_done, n + 2)
                    for tt in range(2):
                        t = 2 * n + 4 + tt
                        ins = nc.vector.tensor_scalar(xn[:, tt, :], x_tm[:, ds(t * D, D)], nmean[:, ds(t, 1)], rstd[:, ds(t, 1)],
                                                      ALU.subtract, ALU.mult)
                    ins.then_inc(xn_ready, 1)
                if f["proj"]:
                    dve.wait_ge(qk_proj, n + 2)
                    if k >= 0:
                        dve.wait_ge(part_ready, PARTS * (n + 1))
                    nc.vector.tensor_scalar(qk[:, 0:SEQ], ps[:, M0, 0:SEQ], bq_col[:, 0:1], None, ALU.add)
                    nc.vector.tensor_scalar(qk[:, SEQ:2 * SEQ], ps[:, M0, SEQ:2 * SEQ], bk_col[:, 0:1], None, ALU.add)\
                        .then_inc(qk_ready, 1)
                maxima(n, k, 0)
                if f["proj"]:
                    dve.wait_ge(part_ready, PARTS * (n + 1) + 1)
                    nc.vector.tensor_tensor(rest[:], qk[:], part[:, 0, :], ALU.subtract).then_inc(rest_ready, 1)
                maxima(n, k, 1)
                if f["proj"]:
                    dve.wait_ge(part_ready, PARTS * (n + 1) + 2)
                    nc.vector.tensor_tensor(rest2[:], rest[:], part[:, 1, :], ALU.subtract).then_inc(rest_ready, 1)
                if f["tail"]:
                    dve.wait_ge(ot_done, n - 1)
                    ov = ps[:, 6:8, :].rearrange("p t (h c) -> p (t h) c", c=VW)
                    nc.vector.reciprocal(rden[:].rearrange("p t h -> p (t h)"), ov[:, :, DEPTH]).then_inc(rden_ready, 1)
                    dve.wait_ge(rden_ready, n - 1)
                    if k >= 3:
                        dve.wait_ge(at_done, n - 2)
                    nc.vector.tensor_tensor(a_tm[:].rearrange("p t h d -> p (t h) d"), ov[:, :, 0:DEPTH],
                                            rden[:].rearrange("p t h -> p (t h)").unsqueeze(2).broadcast_to([P, 2 * HEADS, DEPTH]),
                                            ALU.mult).then_inc(a_ready, 1)
                maxima(n, k, 2)
                maxima(n, k, 3)

            nc.vector.memset(v1[:], 0.0).then_inc(filled, 1)
            nc.vector.memset(ks[64:ROWS_M, :, :, :], 1.0).then_inc(filled, 1)
            dve.wait_ge(filled, 2)
            nc.vector.memset(v1[:, :, :, :, DEPTH], 1.0).then_inc(filled, 1)
            run(dve, iteration)

        @block.scalar
        def _(act):
            def exps(n, k, g):
                for h in range(GROUP * g, GROUP * (g + 1)):
                    act.wait_ge(p2_done, HEADS * n + h + 1)
                    if h % GROUP == 0 and (k > 0 or g >= 2):
                        act.wait_ge(pv_done, GROUPS * n + g - 1)
                    nc.scalar.activation(pt[:, h % (2 * GROUP), :, :].rearrange("p s t -> p (s t)"), ps[:, P2[h % 2], :],
                                         ACT.Exp, scale=float(1.0 / np.sqrt(np.float32(DEPTH)))).then_inc(exp_done, 1)

            def cut(n, k, i):
                if i == 0:
                    act.wait_ge(qk_ready, n + 2)
                    if k >= 0:
                        act.wait_ge(part_out, 32 * (n + 1))
                else:
                    act.wait_ge(rest_ready, 2 * (n + 1) + i)
                nc.scalar.activation(part[:, i, :], (qk, rest, rest2)[i][:], ACT.Copy).then_inc(part_ready, 1)

            def iteration(n, k):
                f = live(k)
                if f["proj"]:
                    cut(n, k, 0)
                if f["p2"]:
                    exps(n - 1, k - 1, 0)
                if f["tail"]:
                    act.wait_ge(pv_done, GROUPS * (n - 1))
                    if k >= 3:
                        act.wait_ge(ot_done, n - 2)
                    nc.scalar.activation(osb[:].rearrange("p g t -> p (g t)"), o_ps, ACT.Copy).then_inc(o_ready, 1)
                if f["p1"] or f["p2"]:
                    act.wait_ge(vn_done, n + 1)
                if f["p1"]:
                    if k >= 2:
                        act.wait_ge(pv_done, GROUPS * (n - 1))
                    nc.scalar.activation(v1[:, k % BUFS, :, :, 0:DEPTH],
                                         ps[:, M1, 0:SEQ].rearrange("p (s h d) -> p s h d", s=2, d=DEPTH), ACT.Copy)\
                        .then_inc(v_ready, 1)
                if f["p2"]:
                    if not f["p1"]:
                        nc.scalar.sem_inc(v_ready, 1)
                    act.wait_ge(nsplit, 5 * (2 * n - 1))
                    nc.scalar.activation(nrow[:], ps[0:HALF, M1, SEQ:2 * SEQ], ACT.Copy).then_inc(nrow_ready, 1)
                if f["proj"]:
                    cut(n, k, 1)
                if f["p2"]:
                    exps(n - 1, k - 1, 1)
                if f["proj"]:
                    cut(n, k, 2)
                if f["p1"] or f["xn"]:
                    act.wait_ge(xt_done, n + 3)
                    if f["xn"]:
                        b = n + 2
                        nc.scalar.activation(hb[:, (k + 2) % BUFS, :], ps[:, M0, 0:SEQ], ACT.Identity, bias=sa[:, ds(b, 1)],
                                             scale=ca1[:, ds(b, 1)]).then_inc(h_ready, 1)
                    if f["p1"]:
                        if k > 0:
                            act.wait_ge(nsplit, 5 * 2 * n)
                        nc.scalar.activation(nrow[:], ps[0:HALF, M0, SEQ:2 * SEQ], ACT.Copy).then_inc(nrow_ready, 1)
                if f["p2"]:
                    exps(n - 1, k - 1, 2)
                if f["tail"]:
                    act.wait_ge(at_done, n - 1)
                    if k >= 3:
                        act.wait_ge(fc_done, n - 2)
                    nc.scalar.activation(a_fm[:], ps[:, M1, 0:SEQ], ACT.Identity, bias=bv_col[:, 0:1]).then_inc(afm_ready, 1)
                if f["p2"]:
                    exps(n - 1, k - 1, 3)
                if f["tail"]:
                    b = n - 2
                    act.wait_ge(fc_done, n - 1)
                    if k >= 3:
                        act.wait_ge(x_added, n - 2)
                    nc.scalar.activation(upd[:], ps[:, M1, 0:SEQ], ACT.Identity, bias=ga_bfc[:, ds(b, 1)],
                                         scale=ga[:, ds(b, 1)]).then_inc(upd_ready, 1)

            act.wait_ge(filled, 3)
            run(act, iteration)

        @block.gpsimd
        def _(pool):
            def split_rows(n, k, half):
                c = 5 * (2 * n + half)
                pool.wait_ge(nrow_ready, 2 * n + half + 1)
                if k > 0 or half > 0:
                    pool.wait_ge(nrows_out, 16 * (2 * n + half))
                nc.gpsimd.tensor_tensor(npart[:, 0, :], nrow[:], nzero[:], ALU.add).then_inc(nsplit, 1)
                pool.wait_ge(nsplit, c + 1)
                nc.gpsimd.tensor_tensor(nrest[:], nrow[:], npart[:, 0, :], ALU.subtract).then_inc(nsplit, 1)
                pool.wait_ge(nsplit, c + 2)
                nc.gpsimd.tensor_tensor(npart[:, 1, :], nrest[:], nzero[:], ALU.add).then_inc(nsplit, 1)
                pool.wait_ge(nsplit, c + 3)
                nc.gpsimd.tensor_tensor(nrest2[:], nrest[:], npart[:, 1, :], ALU.subtract).then_inc(nsplit, 1)
                pool.wait_ge(nsplit, c + 4)
                nc.gpsimd.tensor_tensor(npart[:, 2, :], nrest2[:], nzero[:], ALU.add).then_inc(nsplit, 1)

            def iteration(n, k):
                f = live(k)
                if f["p2"]:
                    split_rows(n - 1, k - 1, 1)
                if f["p1"]:
                    split_rows(n, k, 0)
                if f["tail"]:
                    b = n - 2
                    pool.wait_ge(upd_ready, n - 1)
                    cols = x_fm[:, ds(b * SEQ, SEQ)]
                    nc.gpsimd.tensor_tensor(cols, cols, upd[:], ALU.add).then_inc(x_added, 1)

            nc.gpsimd.memset(nzero[:], 0.0).then_inc(zero_filled, 1)
            pool.wait_ge(zero_filled, 1)
            run(pool, iteration)

        @block.sync
        def _(sp):
            def held(name, x):
                if isinstance(x, int):
                    return x
                r = sp.alloc_register(name)
                sp.reg_mov(r, x)
                return sp.snap(r)

            def load_stacks(buf):
                for a in range(PARTS):
                    for b in range(PARTS):
                        r = DEPTH * (PARTS * a + b)
                        sp.dma_start(qs[r:r + DEPTH, buf, :, :], bounce[buf, 0, a]).then_inc(stacked, 16)
                    r = DEPTH * PARTS * a
                    sp.dma_start(ks[r:r + DEPTH * PARTS, buf, :, :],
                                 bounce[buf, 1].rearrange("b d h t -> (b d) h t")).then_inc(stacked, 16)

            def load_rows(buf, half, out):
                sp.dma_start(nbounce[buf, half].rearrange("i h t -> h i t"), npart[:]).then_inc(nrows_out, 16)
                sp.wait_ge(nrows_out, out)
                sp.dma_start(qs[ROWS:ROWS_M, buf, HALF * half:HALF * (half + 1), :], nbounce[buf, half]).then_inc(nrows_in[half], 16)

            def iteration(n, k):
                f = live(k)
                buf = (k + 1) % BUFS
                split1 = held(f"split1_{k}", 10 * n)
                split0 = held(f"split0_{k}", 10 * n + 5)
                cut = held(f"cut_{k}", PARTS * (n + 2))
                rows1 = held(f"rows1_{k}", 32 * n)
                rows0 = held(f"rows0_{k}", 32 * n + 16)
                seen = held(f"seen_{k}", HEADS * n + 1)
                out = held(f"out_{k}", 32 * (n + 2))
                if f["p2"]:
                    sp.wait_ge(nsplit, split1)
                    load_rows((k - 1) % BUFS, 1, rows1)
                if f["proj"]:
                    sp.wait_ge(part_ready, cut)
                    for q in range(2):
                        sp.dma_start(bounce[buf, q].rearrange("a d h t -> (d h) a t"), part[:, :, q * SEQ:(q + 1) * SEQ])\
                            .then_inc(part_out, 16)
                    if f["p1"]:
                        sp.wait_ge(p1_done, seen)
                    sp.wait_ge(part_out, out)
                    load_stacks(buf)
                if f["p1"]:
                    sp.wait_ge(nsplit, split0)
                    load_rows(k % BUFS, 0, rows0)

            sp.wait_ge(filled, 3)
            run(sp, iteration)


MODS = 6


def setup(nc, T, A):
    with ExitStack() as ctx:
        def sb(name, shape, dt=F32):
            return ctx.enter_context(nc.sbuf_tensor(name, shape, dt))

        def sem(name):
            return ctx.enter_context(nc.semaphore(name))

        c_fm = sb("su_c", [P, 2, BATCH])
        cs = sb("su_cs", [P, 2, BATCH])
        wmod = sb("su_wmod", [P, 2, MODS * D])
        rot = sb("su_rot", [P, 2, PI_ALL, HEADS])
        w_in = sb("su_w", [P, 2 * D])
        b_in = sb("su_b", [1, 2 * D])
        b_rot = sb("su_brot", [1, 2 * D])
        t0 = sb("su_t0", [P, PI_ALL, HEADS])
        t1 = sb("su_t1", [P, PI_ALL, HEADS])
        u0 = sb("su_u0", [1, PI_ALL, HEADS])
        u1 = sb("su_u1", [1, PI_ALL, HEADS])
        one = sb("su_one", [1, 1])
        stats = sb("su_stats", [P, TILES, 6])
        var = sb("su_var", [P, TILES])
        dm = sb("su_dm", [P, TILES])
        sg = sb("su_sg", [P, 2 * 2, BATCH])
        ab = sb("su_ab", [P, 2 * 2, BATCH])
        ps = T["psum"]
        x_in = sem("su_x_in")
        c_in = sem("su_c_in")
        w_loaded = sem("su_w_loaded")
        silu_done = sem("su_silu_done")
        mod_done = sem("su_mod_done")
        bias_done = sem("su_bias_done")
        var_ready = sem("su_var_ready")
        std_ready = sem("su_std_ready")
        step = sem("su_step")
        rot_ready = sem("su_rot_ready")
        pool_done = sem("su_pool_done")
        block = ctx.enter_context(nc.Block())

        @block.sync
        def _(sp):
            sp.dma_start(T["x_tm"][:], A["x_tm"]).then_inc(x_in, 16)
            sp.dma_start(T["x_fm"][:], A["x_fm"]).then_inc(w_loaded, 16)
            sp.wait_ge(w_loaded, 16 * 10)
            sp.dma_start(T["w_gu"][:, WG:WU], A["wg"]).then_inc(T["ffn0_loaded"], 16)
            sp.dma_start(T["w_gu"][:, WU:WD], A["wu"]).then_inc(T["ffn0_loaded"], 16)
            for name in EARLY_LOADS:
                sp.dma_start(T[name][:], A[name]).then_inc(T["ffn0_loaded"], 16)

        @block.gpsimd
        def _(pool):
            pool.memset(one[:], 1.0).then_inc(pool_done, 1)

        @block.scalar
        def _(act):
            act.dma_start(c_fm[:], A["c_fm"]).then_inc(c_in, 16)
            act.dma_start(wmod[:], A["wmod"]).then_inc(c_in, 16)
            for dst, src in ((w_in[:], A["w_qk"]), (b_in[:], A["b_qk"]), (rot[:], A["rot"]), (T["w_v"][:], A["w_v"]),
                             (T["w_fc"][:], A["w_fc"]), (T["bv_col"][:], A["b_v"]), (T["bfc_col"][:], A["b_fc"]),
                             (T["ident"][:], A["ident"]), (T["bo_col"][:], A["b_o"])):
                act.dma_start(dst, src).then_inc(w_loaded, 16)
            act.wait_ge(c_in, 32)
            nc.scalar.activation(cs[:], c_fm[:], ACT.Silu).then_inc(silu_done, 1)
            act.wait_ge(var_ready, 1)
            nc.scalar.activation(dm[:], var[:], ACT.Sqrt).then_inc(std_ready, 1)

        @block.tensor
        def _(pe):
            pe.wait_ge(silu_done, 1)
            for l in range(2):
                for m in range(MODS):
                    at = (l * MODS + m) * BATCH
                    mm = pe.matmul(ps[:, 0, at:at + BATCH], wmod[:, l, m * D:(m + 1) * D], cs[:, l, :], start=True, stop=True)
            mm.then_inc(mod_done, 1)
            pe.wait_ge(rot_ready, 1)
            pe.wait_ge(pool_done, 1)
            for c in range(2):
                mm = pe.matmul(ps[:, 1, c:c + 1], b_rot[:, c * P:(c + 1) * P], one[:], start=True, stop=True)
            mm.then_inc(bias_done, 1)

        @block.vector
        def _(dve):
            n = 0
            dve.wait_ge(x_in, 16)
            for t in range(TILES):
                ins = nc.vector.bn_stats(stats[:, t, :], T["x_tm"][:, t * D:(t + 1) * D])
            ins.then_inc(step, 1)
            dve.wait_ge(step, 1)
            me, mo, ve, vo = (stats[:, :, i] for i in (1, 4, 2, 5))
            nc.vector.tensor_tensor(T["mean"][:], me, mo, ALU.add).then_inc(step, 1)
            nc.vector.tensor_tensor(dm[:], me, mo, ALU.subtract).then_inc(step, 1)
            nc.vector.tensor_tensor(var[:], ve, vo, ALU.add).then_inc(step, 1)
            dve.wait_ge(step, 4)
            nc.vector.tensor_scalar(T["mean"][:], T["mean"][:], 0.5, None, ALU.mult).then_inc(step, 1)
            nc.vector.scalar_tensor_tensor(dm[:], dm[:], 0.25, dm[:], ALU.mult, ALU.mult).then_inc(step, 1)
            nc.vector.tensor_scalar(var[:], var[:], 1.0 / D, LN_EPS, ALU.mult, ALU.add).then_inc(step, 1)
            dve.wait_ge(step, 7)
            nc.vector.tensor_tensor(var[:], var[:], dm[:], ALU.add).then_inc(var_ready, 1)
            dve.wait_ge(w_loaded, 16 * 10)
            for w, out, a, b, q in ((w_in, T["w_qk"], t0, t1, P), (b_in, b_rot, u0, u1, 1)):
                wv = w[:].rearrange("p (i two h) -> p i two h", two=2, h=HEADS)
                ov = out[:].rearrange("p (i two h) -> p i two h", two=2, h=HEADS)
                cos, sin = rot[0:q, 0], rot[0:q, 1]
                for o, (x, y, op) in enumerate(((cos, sin, ALU.subtract), (sin, cos, ALU.add))):
                    nc.vector.tensor_tensor(a[:], wv[:, :, 0, :], x, ALU.mult).then_inc(step, 1)
                    nc.vector.tensor_tensor(b[:], wv[:, :, 1, :], y, ALU.mult).then_inc(step, 1)
                    n += 3
                    dve.wait_ge(step, 7 + n - 1)
                    nc.vector.tensor_tensor(ov[:, :, o, :], a[:], b[:], op).then_inc(step, 1)
                    dve.wait_ge(step, 7 + n)
            nc.vector.sem_inc(rot_ready, 1)
            dve.wait_ge(mod_done, 1)
            m = ps[:, 0, 0:2 * MODS * BATCH].rearrange("p (l k b) -> p l k b", k=3, b=BATCH)
            nc.vector.tensor_copy(T["shift"][:], m[:, :, 0, :])
            nc.vector.tensor_scalar(T["scale1"][:], m[:, :, 1, :], 1.0, None, ALU.add)
            nc.vector.tensor_scalar(sg[:], m[:, :, 2, :], 0.0, 2.0, ALU.is_ge, ALU.mult).then_inc(step, 1)
            dve.wait_ge(step, 8 + n)
            nc.vector.tensor_scalar(sg[:], sg[:], -1.0, None, ALU.add).then_inc(step, 1)
            dve.wait_ge(step, 9 + n)
            nc.vector.tensor_tensor(ab[:], sg[:], m[:, :, 2, :], ALU.mult).then_inc(step, 1)
            dve.wait_ge(step, 10 + n)
            nc.vector.scalar_tensor_tensor(T["gate"][:], ab[:], 0.25, sg[:], ALU.max, ALU.mult).then_inc(step, 1)
            dve.wait_ge(step, 11 + n)
            nc.vector.tensor_scalar(T["ga_bfc"][:], T["gate"][:, 0, :], T["bfc_col"][:, 0:1], None, ALU.mult)
            nc.vector.tensor_scalar(T["ga_bo"][:], T["gate"][:, 2, :], T["bo_col"][:, 0:1], None, ALU.mult)
            dve.wait_ge(bias_done, 1)
            nc.vector.tensor_copy(T["bq_col"][:], ps[:, 1, 0:1])
            nc.vector.tensor_copy(T["bk_col"][:], ps[:, 1, 1:2])
            dve.wait_ge(std_ready, 1)
            nc.vector.reciprocal(T["rstd"][:], dm[:]).then_inc(step, 1)
            dve.wait_ge(step, 12 + n)


CHUNK = 512
CHUNKS = TOK // CHUNK
CT = CHUNK // P
CB = CHUNK // SEQ


class LayerNorm:

    def __init__(self, nc, ctx, name, T, xc, hc, nt, bank, part):
        self.nc, self.T, self.xc, self.hc, self.part = nc, T, xc, hc, part
        self.ps = T["psum"][:, bank, :]
        sb = lambda n, s: ctx.enter_context(nc.sbuf_tensor(f"{name}_{n}", s, F32))
        self.st, self.mv, self.sd, self.rs = sb("st", [P, CT, 6]), sb("mv", [P, CT, 2]), sb("sd", [P, CT]), sb("rs", [P, CT])
        self.nt = nt
        sem = lambda n: ctx.enter_context(nc.semaphore(f"{name}_{n}"))
        self.x_tm = sem("x_tm")
        self.mean = sem("mean")
        self.std = sem("std")
        self.norm = sem("norm")
        self.n_fm = sem("n_fm")
        self.h = sem("h")

    def pe_x(self, pe):
        for t in range(CT):
            mm = pe.transpose(self.ps[:, t * P:(t + 1) * P], self.xc[:, t * P:(t + 1) * P], self.T["ident"][:])
        mm.then_inc(self.x_tm, 1)

    def dve_stats(self, dve, c):
        v = self.nc.vector
        dve.wait_ge(self.x_tm, c + 1)
        for t in range(CT):
            ins = v.bn_stats(self.st[:, t, :], self.ps[:, t * P:(t + 1) * P])
        ins.then_inc(self.mean, 1)
        me, mo, ve, vo = (self.st[:, :, i] for i in (1, 4, 2, 5))
        mean, dif = self.mv[:, :, 0], self.mv[:, :, 1]
        dve.wait_ge(self.mean, 4 * c + 1)
        v.tensor_tensor(mean, me, mo, ALU.add)
        v.tensor_tensor(dif, me, mo, ALU.subtract)
        v.tensor_tensor(self.rs[:], ve, vo, ALU.add).then_inc(self.mean, 1)
        dve.wait_ge(self.mean, 4 * c + 2)
        v.tensor_scalar(mean, mean, 0.5, None, ALU.mult)
        v.scalar_tensor_tensor(dif, dif, 0.25, dif, ALU.mult, ALU.mult)
        v.tensor_scalar(self.rs[:], self.rs[:], 1.0 / D, LN_EPS, ALU.mult, ALU.add).then_inc(self.mean, 1)
        dve.wait_ge(self.mean, 4 * c + 3)
        v.tensor_tensor(self.rs[:], self.rs[:], dif, ALU.add).then_inc(self.mean, 1)

    def act_std(self, act, c):
        act.wait_ge(self.mean, 4 * c + 4)
        self.nc.scalar.activation(self.sd[:], self.rs[:], ACT.Sqrt).then_inc(self.std, 1)

    def dve_norm(self, dve, c):
        v = self.nc.vector
        dve.wait_ge(self.std, c + 1)
        v.reciprocal(self.rs[:], self.sd[:]).then_inc(self.norm, 1)
        dve.wait_ge(self.norm, 2 * c + 1)
        for t in range(CT):
            ins = v.tensor_scalar(self.nt[:, t, :], self.ps[:, t * P:(t + 1) * P], self.mv[:, t, 0:1], self.rs[:, t:t + 1],
                                  ALU.subtract, ALU.mult)
        ins.then_inc(self.norm, 1)

    def pe_n(self, pe, c):
        pe.wait_ge(self.norm, 2 * c + 2)
        for t in range(CT):
            mm = pe.transpose(self.ps[:, t * P:(t + 1) * P], self.nt[:, t, :], self.T["ident"][:])
        mm.then_inc(self.n_fm, 1)

    def act_h(self, act, c):
        act.wait_ge(self.n_fm, c + 1)
        for i in range(CB):
            b = CB * c + i
            ins = self.nc.scalar.activation(self.hc[:, i * SEQ:(i + 1) * SEQ], self.ps[:, i * SEQ:(i + 1) * SEQ], ACT.Identity,
                                            bias=self.T["shift"][:, self.part, ds(b, 1)],
                                            scale=self.T["scale1"][:, self.part, ds(b, 1)])
        ins.then_inc(self.h, 1)


def cols(t, c, size=CHUNK):
    return t[:, ds(c * size, size)]


class Steps:

    def __init__(self, eng, sem, base=0):
        self.eng, self.sem, self.base, self.n = eng, sem, base, 0

    def done(self, ins, wait=True):
        ins.then_inc(self.sem, 1)
        self.n += 1
        if wait:
            self.eng.wait_ge(self.sem, self.base + self.n)


EXPERTS, HIDDEN = 64, 88
EGROUPS, EPG = 8, 8
TOP_GROUPS = 4
ROUTED_SCALE = 2.5
EHALF = EXPERTS // 2
TAKEN = -1.0e30


def route0(nc, T, A):
    x_fm, h_fm, ps = T["x_fm"], T["h_fm"], T["psum"]
    with ExitStack() as ctx:
        def sb(name, shape, dt=F32):
            return ctx.enter_context(nc.sbuf_tensor(name, shape, dt))

        def sem(name):
            return ctx.enter_context(nc.semaphore(name))

        xc, hc = sb("r0_xc", [P, CHUNK]), sb("r0_hc", [P, CHUNK])
        ln = LayerNorm(nc, ctx, "r0_ln", T, xc, hc, sb("r0_nt", [P, CT, D]), 0, 1)
        N = TILES * EXPERTS
        lg = sb("r0_lg", [P, N])
        sfc = sb("r0_sfc", [P, N])
        w0 = sb("r0_w0", [P, N])
        w1 = sb("r0_w1", [P, N])
        G = TILES * EGROUPS
        hi, lo, th, tl = (sb(f"r0_{n}", [P, G, 4]) for n in ("hi", "lo", "th", "tl"))
        gs, rank = sb("r0_gs", [P, G]), sb("r0_rank", [P, G])
        top = sb("r0_top", [P, TILES, 8])
        den, rden = sb("r0_den", [P, TILES]), sb("r0_rden", [P, TILES])
        parts = sb("r0_parts", [P, TILES, 2, PARTS, EHALF], BF16)
        gate_w, gate_b = sb("r0_gw", [P, EXPERTS]), sb("r0_gb", [P, EXPERTS])
        less = sb("r0_less", [P, EGROUPS, EGROUPS])
        loaded = sem("r0_loaded")
        xc_ready = sem("r0_xc_ready")
        h_kept = sem("r0_h_kept")
        lg_done = sem("r0_lg_done")
        lg_kept = sem("r0_lg_kept")
        scored = sem("r0_scored")
        step = sem("r0_step")
        cut = sem("r0_cut")
        tr_done = sem("r0_tr_done")
        tr_kept = [sem(f"r0_tr_kept{g}") for g in range(2)]
        block = ctx.enter_context(nc.Block())

        @block.sync
        def _(sp):
            sp.dma_start(gate_w[:], A["gate_w"]).then_inc(loaded, 16)
            sp.dma_start(gate_b[:], A["gate_b"]).then_inc(loaded, 16)
            sp.dma_start(less[:], A["less8"]).then_inc(loaded, 16)
            routed = ROUTED_TILES * D
            sp.dma_start(T["sel"][0:PARTS * EHALF], A["sel"]).then_inc(T["ffn0_loaded"], 16)
            sp.dma_start(T["w_d"][:, 0:routed], A["wd"]).then_inc(T["ffn0_loaded"], 16)
            sp.dma_start(T["w_d"][0:SHARED_ROWS, routed:HT * D], A["sd"]).then_inc(T["ffn0_loaded"], 16)

        @block.tensor
        def _(pe):
            pe.wait_ge(loaded, 48)

            def chunk(c, first):
                pe.wait_ge(xc_ready, c + 1)
                ln.pe_x(pe)
                ln.pe_n(pe, c)
                pe.wait_ge(ln.h, c + 1)
                if not first:
                    pe.wait_ge(lg_kept, c)
                for t in range(CT):
                    mm = pe.matmul(ps[:, 1, t * EXPERTS:(t + 1) * EXPERTS], hc[:, t * P:(t + 1) * P], gate_w[:], start=True, stop=True)
                mm.then_inc(lg_done, 1)

            chunk(0, True)
            with pe.Fori(1, CHUNKS) as c:
                chunk(c, False)
            pe.wait_ge(cut, 1)
            pe.wait_ge(T["ffn0_loaded"], 16 * FFN0_LOADS)

            def turn(c, k):
                if k >= 2:
                    for g in range(2):
                        pe.wait_ge(tr_kept[g], c - 1)
                for g in range(2):
                    for t in range(CT):
                        mm = pe.matmul(ps[0:PARTS * EHALF, 2 + 2 * (k % 2) + g, t * P:(t + 1) * P],
                                       parts[:, ds(CT * c + t, 1), g, :, :].rearrange("p o i e -> p (o i e)"), T["ident_bf"][:],
                                       start=True, stop=True)
                mm.then_inc(tr_done, 1)

            turn(0, 0)
            turn(1, 1)
            with pe.Fori(1, CHUNKS // 2) as i:
                turn(2 * i, 2)
                turn(2 * i + 1, 3)

        @block.scalar
        def _(act):
            def chunk(c, first):
                if not first:
                    act.wait_ge(ln.x_tm, c)
                nc.scalar.activation(xc[:], cols(x_fm, c), ACT.Copy).then_inc(xc_ready, 1)
                ln.act_std(act, c)
                if not first:
                    act.wait_ge(lg_done, c)
                    act.wait_ge(h_kept, c)
                ln.act_h(act, c)

            chunk(0, True)
            with act.Fori(1, CHUNKS) as c:
                chunk(c, False)
            act.wait_ge(lg_kept, CHUNKS)
            nc.scalar.activation(lg[:], lg[:], ACT.Sigmoid).then_inc(scored, 1)

            def keep(c, k):
                act.wait_ge(tr_done, c + 1)
                nc.scalar.activation(T["rw"][0:PARTS * EHALF, 0, ds(c * CHUNK, CHUNK)], ps[0:PARTS * EHALF, 2 + 2 * (k % 2), :], ACT.Copy)\
                    .then_inc(tr_kept[0], 1)

            with act.Fori(0, CHUNKS // 2) as i:
                keep(2 * i, 0)
                keep(2 * i + 1, 1)

        @block.vector
        def _(dve):
            v = nc.vector
            dve.wait_ge(loaded, 48)

            def chunk(c):
                ln.dve_stats(dve, c)
                ln.dve_norm(dve, c)
                dve.wait_ge(ln.h, c + 1)
                v.tensor_copy(cols(h_fm, c), hc[:]).then_inc(h_kept, 1)
                dve.wait_ge(lg_done, c + 1)
                v.tensor_copy(lg[:, ds(c * CT * EXPERTS, CT * EXPERTS)], ps[:, 1, 0:CT * EXPERTS]).then_inc(lg_kept, 1)

            with dve.Fori(0, CHUNKS) as c:
                chunk(c)

            s = Steps(dve, step)
            dve.wait_ge(scored, 1)
            per_tile = lambda t: t[:].rearrange("p (t e) -> p t e", e=EXPERTS)
            s.done(v.tensor_tensor(per_tile(sfc), per_tile(lg), gate_b[:].unsqueeze(1).broadcast_to([P, TILES, EXPERTS]), ALU.add))
            q = sfc[:].rearrange("p (g e) -> p g e", e=EPG)
            s.done(v.tensor_tensor(hi[:], q[:, :, 0:4], q[:, :, 4:8], ALU.max), False)
            s.done(v.tensor_tensor(lo[:], q[:, :, 0:4], q[:, :, 4:8], ALU.min))
            for w in (2, 1):
                s.done(v.tensor_tensor(th[:, :, 0:w], hi[:, :, 0:w], hi[:, :, w:2 * w], ALU.min), False)
                s.done(v.tensor_tensor(tl[:, :, 0:w], lo[:, :, 0:w], lo[:, :, w:2 * w], ALU.max))
                s.done(v.tensor_tensor(hi[:, :, 0:w], hi[:, :, 0:w], hi[:, :, w:2 * w], ALU.max), False)
                s.done(v.tensor_tensor(lo[:, :, 0:w], th[:, :, 0:w], tl[:, :, 0:w], ALU.max))
            s.done(v.tensor_tensor(gs[:], hi[:, :, 0], lo[:, :, 0], ALU.add))
            own = gs[:].rearrange("p (t g) -> p t g", g=EGROUPS)
            for t4 in range(4):
                r = slice(8 * t4, 8 * t4 + 8)
                a = own[:, r, :].unsqueeze(2).broadcast_to([P, 8, EGROUPS, EGROUPS])
                b = own[:, r, :].unsqueeze(3).broadcast_to([P, 8, EGROUPS, EGROUPS])
                o0 = w0[:, 512 * t4:512 * t4 + 512].rearrange("p (t g e) -> p t g e", g=EGROUPS, e=EGROUPS)
                o1 = w1[:, 512 * t4:512 * t4 + 512].rearrange("p (t g e) -> p t g e", g=EGROUPS, e=EGROUPS)
                s.done(v.tensor_tensor(o0, a, b, ALU.is_gt), False)
                s.done(v.tensor_tensor(o1, a, b, ALU.is_equal), t4 == 3)
            s.done(v.tensor_tensor(w1[:].rearrange("p (t g) -> p t g", g=64), w1[:].rearrange("p (t g) -> p t g", g=64),
                                   less[:].rearrange("p g e -> p (g e)").unsqueeze(1).broadcast_to([P, TILES, 64]), ALU.mult))
            s.done(v.tensor_tensor(w0[:], w0[:], w1[:], ALU.add))
            s.done(v.tensor_reduce(rank[:], w0[:].rearrange("p (g e) -> p g e", e=EGROUPS), AX.X, ALU.add))
            s.done(v.tensor_scalar(rank[:], rank[:], float(TOP_GROUPS), None, ALU.is_lt))
            s.done(v.tensor_tensor(sfc[:].rearrange("p (g e) -> p g e", e=EPG), q,
                                   rank[:].unsqueeze(2).broadcast_to([P, G, EPG]), ALU.mult))
            for t in range(TILES):
                s.done(v.max(top[:, t, :], per_tile(sfc)[:, t, :]), t == TILES - 1)
            for t in range(TILES):
                s.done(v.match_replace(out=per_tile(w0)[:, t, :], in_to_replace=top[:, t, :], in_values=per_tile(sfc)[:, t, :],
                                       imm_value=TAKEN), t == TILES - 1)
            s.done(v.scalar_tensor_tensor(w1[:], w0[:], TAKEN / 2, lg[:], ALU.is_lt, ALU.mult))
            s.done(v.tensor_reduce(den[:], per_tile(w1), AX.X, ALU.add))
            s.done(v.tensor_scalar(den[:], den[:], 1e-20, None, ALU.add))
            s.done(v.reciprocal(rden[:], den[:]))
            s.done(v.tensor_tensor(per_tile(w1), per_tile(w1), rden[:].unsqueeze(2).broadcast_to([P, TILES, EXPERTS]), ALU.mult))
            s.done(v.tensor_scalar(w1[:], w1[:], ROUTED_SCALE, None, ALU.mult))
            part = lambda i: parts[:, :, :, i, :].rearrange("p t g e -> p (t g) e")
            half = lambda t: t[:].rearrange("p (t e) -> p t e", e=EHALF)
            s.done(v.tensor_copy(part(0), half(w1)))
            s.done(v.tensor_tensor(half(w0), half(w1), part(0), ALU.subtract))
            s.done(v.tensor_copy(part(1), half(w0)))
            s.done(v.tensor_tensor(half(w1), half(w0), part(1), ALU.subtract))
            v.tensor_copy(part(2), half(w1)).then_inc(cut, 1)

            def keep(c, k):
                dve.wait_ge(tr_done, c + 1)
                v.tensor_copy(T["rw"][0:PARTS * EHALF, 1, ds(c * CHUNK, CHUNK)], ps[0:PARTS * EHALF, 3 + 2 * (k % 2), :])\
                    .then_inc(tr_kept[1], 1)

            with dve.Fori(0, CHUNKS // 2) as i:
                keep(2 * i, 0)
                keep(2 * i + 1, 1)


ROUTED_TILES = EXPERTS * HIDDEN // P
SHARED_TILES, SHARED_ROWS = 2, HIDDEN
HT = ROUTED_TILES + SHARED_TILES
HALF_TILES = ROUTED_TILES // 2
LAG = 2
AHEAD = 2
HIDDEN_ALL = EXPERTS * HIDDEN + SHARED_TILES * SHARED_ROWS
KD = 2 * DEPTH
LT = SEQ // P
QKV1 = 3 * D + HEADS
DPFP_EPS = 1e-6
E1 = 9
NE1 = E1 - 1
F1 = 512
F1T = F1 // P
T1 = NE1 * F1T
LAG1 = 3
RING1 = 4
TOP1 = 2
EARLY_LOADS = ("wqkv", "wo", "wr", "ident_bf", "b_r1", "less9", "sel1")
FFN0_LOADS = len(EARLY_LOADS) + 5
ROUTER_STEPS = 16

WG, WU, WD = 0, HIDDEN_ALL, 2 * HIDDEN_ALL
WEIGHTS = 2 * HIDDEN_ALL + HT * D
FREE_G = (HIDDEN_ALL - T1 * P) // P


def w1_low(j):
    return WG + P * j


def w2_low(j):
    return WU + P * j


def w2_high(j):
    return WD + P * j


def w1_high(j):
    if j < FREE_G:
        return WG + P * (T1 + j)
    if j < 2 * FREE_G:
        return WU + P * (T1 + j - FREE_G)
    return WD + P * (T1 + j - 2 * FREE_G)


def weights_at(T, at, width, rounded=""):
    tensor, start = (T["w_gu" + rounded], at) if at < WD else (T["w_d" + rounded], at - WD)
    return tensor[:, start:start + width]


NULL_AT = WD + P * (2 * T1 - 2 * FREE_G)


def experts(nc, T, A, out):
    x_fm, h_fm, ps, rw = T["x_fm"], T["h_fm"], T["psum"], T["rw"]
    wqkv, wo, wr = (T[k] for k in ("wqkv", "wo", "wr"))
    sel = T["sel"]
    with ExitStack() as ctx:
        def sb(name, shape, dt=F32):
            return ctx.enter_context(nc.sbuf_tensor(name, shape, dt))

        def sem(name):
            return ctx.enter_context(nc.semaphore("e_" + name))

        act_g = gu = sb("e_gu", [P, 2, CHUNK])
        hm = sb("e_hm", [P, 2, CHUNK])
        h_hi, h_lo = sb("e_hhi", [P, CHUNK], F32R), sb("e_hlo", [P, CHUNK], F32R)
        ring = sb("e_ring", [P, 4 * CHUNK], F32R)
        w_ring = ring[:].rearrange("p (s i w c) -> p s i w c", i=2, w=2, c=P)
        m_lo = ring[:].rearrange("p (s c) -> p s c", c=CHUNK)
        m_hi = T["sel_buf_r"][:].rearrange("p (s c) -> p s c", c=CHUNK)
        null = weights_at(T, NULL_AT, CHUNK)
        xc = sb("e_x", [P, CHUNK])
        hc = y_fm = sb("e_h", [P, CHUNK])
        nt = sb("e_nt", [P, CT, D])
        upd = nt[:].rearrange("p t d -> p (t d)")
        y_tm = sb("e_y", [P, CT, D])
        phi = sb("e_phi", [P, 2, CT, HEADS, KD])
        psum_r, prec = sb("e_psum", [P, 2 * CT * HEADS]), sb("e_prec", [P, 2 * CT * HEADS])
        vv = sb("e_v", [P, CT, D])
        beta = sb("e_beta", [P, CT, HEADS])
        state = sb("e_state", [P, LT, HEADS, DEPTH, KD])
        prod = sb("e_prod", [P, LT, HEADS, DEPTH, KD])
        vbar = sb("e_vbar", [P, LT, D])
        u = sb("e_u", [P, LT, D])
        raw = prod[:, 0].rearrange("p h v k -> p (h v k)").rearrange("p (q a k) -> p q a k", q=2, k=KD)
        mx, sm, rs = (sb(f"e_{n}", [P, CT]) for n in ("mx", "sm", "rs"))
        pr, w0, w1 = (sb(f"e_{n}", [P, CT, E1]) for n in ("pr", "w0", "w1"))
        rank = sb("e_rank", [P, CT, E1])
        above = nt[:].rearrange("p t d -> p (t d)")[:, 0:CT * E1 * E1]
        equal = sb("e_equal", [P, CT * E1 * E1])
        parts = sb("e_parts", [P, CT, PARTS, E1], BF16)
        g1 = rw[:, 0, :]
        GB, UB, RB, ACC, SIDE = (0, 1), (2, 3), (4, 5), 6, 7
        HB, NB = GB, 2
        side = ps[:, SIDE, :]
        ln_a = LayerNorm(nc, ctx, "e_lna", T, xc, hc, nt, SIDE, 2)
        ln_b = LayerNorm(nc, ctx, "e_lnb", T, xc, hc, nt, SIDE, 3)

        wh_done = sem("wh_done")
        wl_done = sem("wl_done")
        hh_done = sem("hh_done")
        hl_done = sem("hl_done")
        gate_done = sem("gate_done")
        ur_done = sem("ur_done")
        silu_done = sem("silu_done")
        gu_done = sem("gu_done")
        hm_done = sem("hm_done")
        acc_done = sem("acc_done")
        x_new = sem("x_new")
        x_kept = sem("x_kept")
        pr_done = sem("pr_done")
        pr_kept = sem("pr_kept")
        beta_done = sem("beta_done")
        pool_step = sem("pool_step")
        u_step = sem("u_step")
        state_zero = sem("state_zero")
        phi_sum = sem("phi_sum")
        vbar_done = sem("vbar_done")
        y_done = sem("y_done")
        yt_done = sem("yt_done")
        yfm_done = sem("yfm_done")
        wo_done = sem("wo_done")
        upd_done = sem("upd_done")
        xb_done = sem("xb_done")
        xb_kept = sem("xb_kept")
        h1_kept = sem("h1_kept")
        lg1_done = sem("lg1_done")
        r_step = sem("r_step")
        shifted = sem("shifted")
        exp_done = sem("exp_done")
        cut = sem("cut")
        g1t_done = sem("g1t_done")
        g1_kept = sem("g1_kept")
        w1h_done, w1l_done, w2h_done, w2l_done = (sem(n) for n in ("w1h_done", "w1l_done", "w2h_done", "w2l_done"))
        up1_done = sem("up1_done")
        gelu_done = sem("gelu_done")
        r1_done = sem("r1_done")
        rn_done = sem("rn_done")
        nh_done = sem("nh_done")
        m_done = sem("m_done")
        mh_done, ml_done = sem("mh_done"), sem("ml_done")
        acc1_done = sem("acc1_done")
        acc1_read = sem("acc1_read")
        x_done = sem("x_done")
        stored = sem("stored")
        block = ctx.enter_context(nc.Block())

        PHI, NORM, PRODUCTS = 2, 3, 8
        KEY, OUTER, ADD, QUERY = (1, 2), (3, 6), (4, 7), (5, 8)
        POOL_STEPS = NORM + CB * PRODUCTS

        def pool_at(m, s, p):
            return POOL_STEPS * m + NORM + PRODUCTS * s + p

        V_SLOT = {21: (0, 0), 23: (0, 1), 36: (1, 0), 38: (1, 1)}
        Y_SLOT = {28: (0, 0), 34: (0, 1), 44: (1, 0)}
        Y_LAST = 3

        def live(k):
            return {"a": 0 <= k - 1 < CHUNKS, "b": 0 <= k - 2 < CHUNKS}

        SPREAD = HT + Y_LAST + 4
        def tile_of(p):
            return int(1.75 * p) if p <= SPREAD else int(1.75 * SPREAD) + p - SPREAD

        PEELED1 = 4

        def beside(q, j, jobs):
            for p in range(HT + 32):
                if tile_of(p) == T1 * q + j:
                    jobs(CHUNKS + p // HT, CHUNKS + p // HT, p % HT)

        def run(eng, block0, block1):
            for c in range(3):
                block0(c, c)
            with eng.Fori(3, CHUNKS - 1) as c:
                block0(c, 3)
            block0(CHUNKS - 1, CHUNKS - 1)
            for q in range(PEELED1):
                block1(q, q)
            with eng.Fori(PEELED1, CHUNKS) as q:
                block1(q, PEELED1)

        def rows(j):
            return P if j < ROUTED_TILES else SHARED_ROWS

        def slot(j):
            return 3 if j == HT - 1 else j % 3

        def gate_up(j):
            at = P * j if j < ROUTED_TILES else P * ROUTED_TILES + SHARED_ROWS * (j - ROUTED_TILES)
            return T["w_gu"][:].rearrange("p (w c) -> p w c", w=2)[:, :, at:at + rows(j)]

        def part(at):
            return weights_at(T, at, P, "_r")

        @block.sync
        def _(sp):
            sp.wait_ge(wl_done, HT * (CHUNKS - 1) + T1)
            sp.dma_start(weights_at(T, w1_low(0), T1 * P), A["w1"]).then_inc(T["ffn1_loaded"], 16)
            sp.dma_start(weights_at(T, w2_low(0), T1 * P), A["w2"]).then_inc(T["ffn1_loaded"], 16)
            for c in range(CHUNKS):
                sp.wait_ge(x_done, c + 1)
                sp.dma_start(cols(out, c), cols(x_fm, c)).then_inc(stored, 16)
            sp.wait_ge(stored, 16 * CHUNKS)

        @block.tensor
        def _(pe):
            pe.wait_ge(T["ffn0_loaded"], 16 * FFN0_LOADS)

            def three(out, w_hi, w_lo, x_hi, x_lo, first=True, last=True):
                pe.matmul(out, w_hi, x_hi, start=first, stop=False)
                pe.matmul(out, w_lo, x_hi, start=False, stop=False)
                return pe.matmul(out, w_hi, x_lo, start=False, stop=last)

            def down(c, j, k):
                if j == 0 and k > 0:
                    pe.wait_ge(x_new, c)
                pe.wait_ge(hm_done, HT * c + j + 1)
                mm = pe.matmul(ps[:, ACC, :], weights_at(T, WD + P * j, P)[0:rows(j), :], hm[0:rows(j), j % 2, :],
                               start=(j == 0), stop=(j == HT - 1))
                if j == HT - 1:
                    mm.then_inc(acc_done, 1)

            def tile(c, j, k):
                r, g = rows(j), HT * c + j
                if j == 0 and k > 0:
                    down(c - 1, HT - LAG, k)
                if j == 0:
                    pe.wait_ge(hl_done, c + 1)
                pe.wait_ge(wl_done, g + 1)
                if k > 0 or j >= 2:
                    pe.wait_ge(silu_done, g - 1)
                s = slot(j)
                three(ps[0:r, GB[j % 2], :], w_ring[:, s, 0, 0, 0:r], w_ring[:, s, 1, 0, 0:r], h_hi[:], h_lo[:]).then_inc(gate_done, 1)
                if j >= LAG:
                    down(c, j - LAG, k)
                elif k > 0 and j == 1:
                    down(c - 1, HT - 1, k)
                if k > 0 or j >= 2:
                    pe.wait_ge(hm_done, g - 1)
                mm = three(ps[0:r, UB[j % 2], :], w_ring[:, s, 0, 1, 0:r], w_ring[:, s, 1, 1, 0:r], h_hi[:], h_lo[:])
                if j < ROUTED_TILES:
                    mm = pe.matmul(ps[:, RB[j % 2], :], sel[0:PARTS * EHALF, j % HALF_TILES, :],
                                   rw[0:PARTS * EHALF, j // HALF_TILES, ds(c * CHUNK, CHUNK)], start=True, stop=True)
                mm.then_inc(ur_done, 1)

            def project(m, t):
                if t == 0:
                    pe.wait_ge(ln_a.h, m + 1)
                else:
                    pe.wait_ge(pr_kept, CT * m + t)
                pe.matmul(side[:, 0:QKV1], hc[:, t * P:(t + 1) * P], wqkv[:], start=True, stop=True).then_inc(pr_done, 1)

            def jobs(c, k, j):
                f = live(k)
                if f["a"]:
                    m = c - 1
                    if j == 3:
                        pe.wait_ge(x_new, m + 1)
                        if k > 1:
                            pe.wait_ge(beta_done, m)
                        if k > 2:
                            pe.wait_ge(g1_kept, m - 1)
                        ln_a.pe_x(pe)
                    if j == 6:
                        ln_a.pe_n(pe, m)
                    if 8 <= j < 8 + CT:
                        project(m, j - 8)
                if f["b"]:
                    m = c - 2
                    if j == 14:
                        if f["a"]:
                            pe.wait_ge(beta_done, c)
                        else:
                            pe.wait_ge(g1_kept, m)
                        pe.wait_ge(y_done, CT * m + CT)
                        for t in range(CT):
                            mm = pe.transpose(side[:, t * P:(t + 1) * P], y_tm[:, t, :], T["ident"][:])
                        mm.then_inc(yt_done, 1)
                    if j == 16:
                        pe.wait_ge(yfm_done, m + 1)
                        pe.matmul(side, wo[:], y_fm[:], start=True, stop=True).then_inc(wo_done, 1)
                    if j == 19:
                        pe.wait_ge(xb_done, m + 1)
                        ln_b.pe_x(pe)
                    if j == 22:
                        ln_b.pe_n(pe, m)
                    if j == 24:
                        pe.wait_ge(ln_b.h, m + 1)
                        for t in range(CT):
                            mm = pe.matmul(side[:, t * E1:(t + 1) * E1], hc[:, t * P:(t + 1) * P], wr[:], start=True, stop=True)
                        mm.then_inc(lg1_done, 1)
                    if j == 30:
                        pe.wait_ge(cut, m + 1)
                        for t in range(CT):
                            mm = pe.matmul(side[0:PARTS * E1, t * P:(t + 1) * P], parts[:, t, :, :].rearrange("p i e -> p (i e)"),
                                           T["ident_bf"][:], start=True, stop=True)
                        mm.then_inc(g1t_done, 1)

            def block0(c, k):
                for j in range(HT):
                    jobs(c, k, j)
                    tile(c, j, k)

            def spread(c, e):
                return pe.matmul(ps[:, NB if e == NE1 else RB[e % 2], :], T["sel1"][0:PARTS * E1, e, :],
                                 g1[0:PARTS * E1, ds(c * CHUNK, CHUNK)], start=True, stop=True)

            def down1(c, j, k):
                if j == 0:
                    if k > 0:
                        pe.wait_ge(acc1_read, c)
                    else:
                        pe.wait_ge(x_new, CHUNKS)
                if k == 0:
                    pe.wait_ge(w2l_done, j + 1)
                pe.wait_ge(ml_done, T1 * c + j + 1)
                s = j % RING1
                mm = three(ps[:, ACC, :], part(w2_high(j)), part(w2_low(j)), m_hi[:, s, :], m_lo[:, s, :], j == 0, j == T1 - 1)
                if j == T1 - 1:
                    mm.then_inc(acc1_done, 1)

            def up1(c, j, k):
                e, g = j // F1T, T1 * c + j
                if j == 0:
                    pe.wait_ge(hl_done, CHUNKS + c + 1)
                if k == 0:
                    pe.wait_ge(w1l_done, j + 1)
                    if j < 2:
                        pe.wait_ge(silu_done, HT * CHUNKS - 1 + j)
                if j % F1T == 0 and (k > 0 or e >= 2):
                    pe.wait_ge(m_done, g - F1T)
                if j == 0 and k > 0:
                    pe.wait_ge(nh_done, c)
                if k > 0 or j >= 2:
                    pe.wait_ge(gelu_done, g - 1)
                three(ps[:, HB[j % 2], :], part(w1_high(j)), part(w1_low(j)), h_hi[:], h_lo[:]).then_inc(up1_done, 1)

            def block1(c, k):
                for j in range(T1):
                    beside(c, j, jobs) if k < PEELED1 else None
                    if j > 0:
                        up1(c, j, k)
                    if k == 0 and j < LAG:
                        down(CHUNKS - 1, HT - LAG + j, CHUNKS)
                    elif j >= LAG1:
                        down1(c, j - LAG1, k)
                    elif k > 0:
                        down1(c - 1, T1 - LAG1 + j, k - 1)
                    if j == 0:
                        up1(c, j, k)
                    if j == (1 if k == 0 else 0):
                        if k == 0:
                            pe.wait_ge(hm_done, HT * CHUNKS)
                        spread(c, NE1).then_inc(rn_done, 1)
                        spread(c, 0).then_inc(r1_done, 1)
                    elif j > 0 and j % F1T == 0:
                        spread(c, j // F1T).then_inc(r1_done, 1)

            run(pe, block0, block1)
            for j in range(T1 - LAG1, T1):
                down1(CHUNKS - 1, j, 1)

        @block.scalar
        def _(act):
            a = nc.scalar.activation

            def h_high(n, c, wait):
                if wait:
                    wait()
                a(h_hi[:], cols(h_fm, c), ACT.Copy).then_inc(hh_done, 1)

            def weights_high(j):
                a(w_ring[:, slot(j), 0, :, 0:rows(j)], gate_up(j), ACT.Copy).then_inc(wh_done, 1)

            def w1_highs(j):
                if j == 0:
                    act.wait_ge(T["ffn1_loaded"], 32)
                if j in (0, 2 * FREE_G):
                    act.wait_ge(wl_done, HT * CHUNKS) if j == 0 else act.wait_ge(acc_done, CHUNKS)
                a(part(w1_high(j)), weights_at(T, w1_low(j), P), ACT.Copy).then_inc(w1h_done, 1)

            def jobs(c, k, j):
                f = live(k)
                if f["a"]:
                    m = c - 1
                    if j == 2:
                        act.wait_ge(x_new, m + 1)
                        a(cols(x_fm, m), xc[:], ACT.Copy).then_inc(x_kept, 1)
                    if j == 4:
                        ln_a.act_std(act, m)
                    if j == 6:
                        if k > 2:
                            act.wait_ge(h1_kept, m - 1)
                        ln_a.act_h(act, m)
                    if 8 <= j < 8 + CT:
                        t = j - 8
                        if t == 0 and k > 1:
                            act.wait_ge(y_done, CT * m)
                            act.wait_ge(pool_step, POOL_STEPS * m)
                        act.wait_ge(pr_done, CT * m + t + 1)
                        qk = side[:, 0:2 * D].rearrange("p (q h d) -> p q h d", q=2, d=DEPTH)
                        a(raw[:, :, HEADS * t:HEADS * (t + 1), 0:DEPTH], qk, ACT.Relu)
                        a(raw[:, :, HEADS * t:HEADS * (t + 1), DEPTH:KD], qk, ACT.Relu, scale=-1.0)
                        a(vv[:, t, :], side[:, 2 * D:3 * D], ACT.Copy)
                        a(beta[:, t, :], side[:, 3 * D:QKV1], ACT.Copy).then_inc(pr_kept, 1)
                        if t == CT - 1:
                            act.wait_ge(pr_kept, CT * m + CT)
                            a(beta[:], beta[:], ACT.Sigmoid).then_inc(beta_done, 1)
                if f["b"]:
                    m = c - 2
                    if j == 14:
                        act.wait_ge(yt_done, m + 1)
                        a(y_fm[:], side, ACT.Copy).then_inc(yfm_done, 1)
                    if j == 16:
                        act.wait_ge(wo_done, m + 1)
                        for i in range(CB):
                            b = CB * m + i
                            ins = a(upd[:, i * SEQ:(i + 1) * SEQ], side[:, i * SEQ:(i + 1) * SEQ], ACT.Identity,
                                    bias=T["ga_bo"][:, ds(b, 1)], scale=T["gate"][:, 2, ds(b, 1)])
                        ins.then_inc(upd_done, 1)
                    if j == 18:
                        act.wait_ge(xb_done, m + 1)
                        a(cols(x_fm, m), xc[:], ACT.Copy).then_inc(xb_kept, 1)
                    if j == 20:
                        ln_b.act_std(act, m)
                    if j == 22:
                        ln_b.act_h(act, m)
                    if j == 26:
                        act.wait_ge(shifted, m + 1)
                        a(pr[:], w0[:], ACT.Exp).then_inc(exp_done, 1)
                    if j == 30:
                        act.wait_ge(g1t_done, m + 1)
                        a(g1[0:PARTS * E1, ds(m * CHUNK, CHUNK)], side[0:PARTS * E1, :], ACT.Copy).then_inc(g1_kept, 1)

            def block0(c, k):
                for j in range(HT):
                    r, g = rows(j), HT * c + j
                    if j == 0:
                        h_high(c, c, (lambda: act.wait_ge(ur_done, HT * c)) if k > 0 else None)
                    act.wait_ge(gate_done, g + 1)
                    if k > 0 or j >= 2:
                        act.wait_ge(hm_done, g - 1)
                    a(act_g[0:r, j % 2, :], ps[0:r, GB[j % 2], :], ACT.Silu).then_inc(silu_done, 1)
                    if k < CHUNKS - 1 or j < HT - AHEAD:
                        weights_high((j + AHEAD) % HT)
                    else:
                        w1_highs(j + AHEAD - HT)
                    jobs(c, k, j)

            def hidden_high(c, j):
                act.wait_ge(m_done, T1 * c + j + 1)
                a(m_hi[:, j % RING1, :], hm[:, j % 2, :], ACT.Copy).then_inc(mh_done, 1)

            def block1(c, k):
                for j in range(T1):
                    g = T1 * c + j
                    if j == 0:
                        h_high(CHUNKS + c, c, (lambda: act.wait_ge(up1_done, g)) if k > 0 else (lambda: act.wait_ge(ur_done, HT * CHUNKS)))
                    act.wait_ge(up1_done, g + 1)
                    if k > 0 or j >= 2:
                        act.wait_ge(m_done, g - 1)
                    else:
                        act.wait_ge(hm_done, HT * CHUNKS)
                    a(gu[:, j % 2, :], ps[:, HB[j % 2], :], ACT.Gelu).then_inc(gelu_done, 1)
                    if k == 0:
                        if j + AHEAD < T1:
                            w1_highs(j + AHEAD)
                        if j == 0:
                            act.wait_ge(acc_done, CHUNKS)
                        a(part(w2_high(j)), weights_at(T, w2_low(j), P), ACT.Copy).then_inc(w2h_done, 1)
                    if j > 0:
                        hidden_high(c, j - 1)
                    elif k > 0:
                        hidden_high(c - 1, T1 - 1)
                    beside(c, j, jobs) if k < PEELED1 else None

            act.wait_ge(T["ffn0_loaded"], 16 * FFN0_LOADS)
            for j in range(AHEAD):
                weights_high(j)
            run(act, block0, block1)
            hidden_high(CHUNKS - 1, T1 - 1)

        @block.vector
        def _(dve):
            v = nc.vector

            def h_low(n, c):
                dve.wait_ge(hh_done, n + 1)
                v.tensor_tensor(h_lo[:], cols(h_fm, c), h_hi[:].bitcast(F32), ALU.subtract).then_inc(hl_done, 1)

            def weights_low(n, j):
                dve.wait_ge(wh_done, n)
                r = rows(j)
                v.tensor_tensor(w_ring[:, slot(j), 1, :, 0:r], gate_up(j), w_ring[:, slot(j), 0, :, 0:r].bitcast(F32), ALU.subtract)\
                    .then_inc(wl_done, 1)

            def low_of(low, high, high_done, low_done, j):
                dve.wait_ge(high_done, j + 1)
                v.tensor_tensor(part(low(j)), weights_at(T, low(j), P), part(high(j)).bitcast(F32), ALU.subtract).then_inc(low_done, 1)

            def product_sum(out, z):
                return v.tensor_reduce(out, prod[:, z].rearrange("p h v k -> p (h v) k"), AX.X, ALU.add)

            def y_sum(m, s, z):
                dve.wait_ge(pool_step, pool_at(m, s, QUERY[z]))
                product_sum(y_tm[:, LT * s + z, :], z).then_inc(y_done, 1)

            def router(m):
                s = Steps(dve, r_step, ROUTER_STEPS * m)
                over = lambda ap: ap.unsqueeze(2).broadcast_to([P, CT, E1])
                lg = side[:, 0:CT * E1].rearrange("p (t e) -> p t e", e=E1)
                s.done(v.tensor_tensor(w1[:], lg, T["b_r1"][:].unsqueeze(1).broadcast_to([P, CT, E1]), ALU.add))
                s.done(v.tensor_reduce(mx[:], w1[:], AX.X, ALU.max))
                v.tensor_tensor(w0[:], w1[:], over(mx[:]), ALU.subtract).then_inc(shifted, 1)
                return s

            def router_gates(m, s):
                over = lambda ap: ap.unsqueeze(2).broadcast_to([P, CT, E1])
                dve.wait_ge(exp_done, m + 1)
                s.done(v.tensor_reduce(sm[:], pr[:], AX.X, ALU.add))
                s.done(v.reciprocal(rs[:], sm[:]))
                s.done(v.tensor_tensor(pr[:], pr[:], over(rs[:]), ALU.mult))
                pa = pr[:].unsqueeze(2).broadcast_to([P, CT, E1, E1])
                pb = pr[:].unsqueeze(3).broadcast_to([P, CT, E1, E1])
                pairs = lambda ap: ap.rearrange("p (t g e) -> p t g e", g=E1, e=E1)
                s.done(v.tensor_tensor(pairs(above), pa, pb, ALU.is_gt), False)
                s.done(v.tensor_tensor(pairs(equal[:]), pa, pb, ALU.is_equal))
                per = lambda ap: ap.rearrange("p (t g) -> p t g", t=CT)
                s.done(v.tensor_tensor(per(equal[:]), per(equal[:]),
                                       T["less9"][:].rearrange("p g e -> p (g e)").unsqueeze(1).broadcast_to([P, CT, E1 * E1]), ALU.mult))
                s.done(v.tensor_tensor(above, above, equal[:], ALU.add))
                s.done(v.tensor_reduce(rank[:].rearrange("p t e -> p (t e)"), above.rearrange("p (g e) -> p g e", e=E1), AX.X, ALU.add))
                s.done(v.scalar_tensor_tensor(w0[:], rank[:], float(TOP1), pr[:], ALU.is_lt, ALU.mult))
                s.done(v.tensor_copy(parts[:, :, 0, :], w0[:]))
                s.done(v.tensor_tensor(w1[:], w0[:], parts[:, :, 0, :], ALU.subtract))
                s.done(v.tensor_copy(parts[:, :, 1, :], w1[:]))
                s.done(v.tensor_tensor(w0[:], w1[:], parts[:, :, 1, :], ALU.subtract))
                s.done(v.tensor_copy(parts[:, :, 2, :], w0[:]))
                v.sem_inc(cut, 1)
                assert s.n == ROUTER_STEPS

            held = {}

            def jobs(c, k, j):
                f = live(k)
                if f["a"]:
                    m = c - 1
                    if j == 1:
                        dve.wait_ge(acc_done, m + 1)
                        if k > 1:
                            dve.wait_ge(ln_a.x_tm, m)
                        if k > 2:
                            dve.wait_ge(xb_kept, m - 1)
                        for i in range(CB):
                            b = CB * m + i
                            ins = v.scalar_tensor_tensor(xc[:, i * SEQ:(i + 1) * SEQ], ps[:, ACC, i * SEQ:(i + 1) * SEQ],
                                                         T["gate"][:, 1, ds(b, 1)], cols(x_fm, b, SEQ), ALU.mult, ALU.add)
                        ins.then_inc(x_new, 1)
                    if j == 3:
                        ln_a.dve_stats(dve, m)
                    if j == 4:
                        ln_a.dve_norm(dve, m)
                    if j == 14:
                        dve.wait_ge(pool_step, POOL_STEPS * m + PHI)
                        v.tensor_reduce(psum_r[:], phi[:].rearrange("p q t h k -> p (q t h) k"), AX.X, ALU.add).then_inc(phi_sum, 1)
                        dve.wait_ge(phi_sum, 3 * m + 1)
                        v.tensor_scalar(psum_r[:], psum_r[:], DPFP_EPS, None, ALU.add).then_inc(phi_sum, 1)
                        dve.wait_ge(phi_sum, 3 * m + 2)
                        v.reciprocal(prec[:], psum_r[:]).then_inc(phi_sum, 1)
                    if j in V_SLOT:
                        s, z = V_SLOT[j]
                        dve.wait_ge(pool_step, pool_at(m, s, KEY[z]))
                        product_sum(vbar[:, z, :], z).then_inc(vbar_done, 1)
                    if j in Y_SLOT:
                        s, z = Y_SLOT[j]
                        if s == 0 and z == 0 and k > 1:
                            dve.wait_ge(yt_done, m)
                        y_sum(m, s, z)
                if f["b"]:
                    m = c - 2
                    if j == Y_LAST:
                        y_sum(m, CB - 1, LT - 1)
                    if j == 17:
                        dve.wait_ge(upd_done, m + 1)
                        if k > 2:
                            dve.wait_ge(ln_b.x_tm, m)
                        dve.wait_ge(x_kept, m + 2 if f["a"] else CHUNKS)
                        v.tensor_tensor(xc[:], cols(x_fm, m), upd, ALU.add).then_inc(xb_done, 1)
                    if j == 19:
                        ln_b.dve_stats(dve, m)
                    if j == 20:
                        ln_b.dve_norm(dve, m)
                    if j == 23:
                        dve.wait_ge(ln_b.h, m + 1)
                        v.tensor_copy(cols(h_fm, m), hc[:]).then_inc(h1_kept, 1)
                    if j == 25:
                        dve.wait_ge(lg1_done, m + 1)
                        held["router"] = router(m)
                    if j == 27:
                        router_gates(m, held["router"])

            def block0(c, k):
                for j in range(HT):
                    r, g = rows(j), HT * c + j
                    if j == 0:
                        h_low(c, c)
                    dve.wait_ge(silu_done, g + 1)
                    dve.wait_ge(ur_done, g + 1)
                    product = gu if j < ROUTED_TILES else hm
                    ins = v.tensor_tensor(product[0:r, j % 2, :], ps[0:r, UB[j % 2], :], act_g[0:r, j % 2, :], ALU.mult)
                    if j < ROUTED_TILES:
                        ins.then_inc(gu_done, 1)
                        dve.wait_ge(gu_done, ROUTED_TILES * c + j + 1)
                        v.tensor_tensor(hm[:, j % 2, :], ps[:, RB[j % 2], :], gu[:, j % 2, :], ALU.mult).then_inc(hm_done, 1)
                    else:
                        ins.then_inc(hm_done, 1)
                    if k < CHUNKS - 1 or j < HT - AHEAD:
                        weights_low(g + AHEAD + 1, (j + AHEAD) % HT)
                    else:
                        low_of(w1_low, w1_high, w1h_done, w1l_done, j + AHEAD - HT)
                    jobs(c, k, j)

            def hidden_low(c, j):
                dve.wait_ge(mh_done, T1 * c + j + 1)
                v.tensor_tensor(m_lo[:, j % RING1, :], hm[:, j % 2, :], m_hi[:, j % RING1, :].bitcast(F32), ALU.subtract).then_inc(ml_done, 1)

            def result(m):
                dve.wait_ge(acc1_done, m + 1)
                v.tensor_tensor(null, ps[:, ACC, :], null, ALU.add).then_inc(acc1_read, 1)
                dve.wait_ge(acc1_read, m + 1)
                for i in range(CB):
                    b = CB * m + i
                    x = cols(x_fm, b, SEQ)
                    ins = v.scalar_tensor_tensor(x, null[:, i * SEQ:(i + 1) * SEQ], T["gate"][:, 3, ds(b, 1)], x, ALU.mult, ALU.add)
                ins.then_inc(x_done, 1)

            def block1(c, k):
                for j in range(T1):
                    e, g = j // F1T, T1 * c + j
                    if j == 0:
                        h_low(CHUNKS + c, c)
                    dve.wait_ge(gelu_done, g + 1)
                    dve.wait_ge(r1_done, NE1 * c + e + 1)
                    if k > 0 or j >= 2:
                        dve.wait_ge(ml_done, g - 1)
                    if k == 0 and j < 2:
                        dve.wait_ge(acc_done, CHUNKS)
                    v.tensor_tensor(hm[:, j % 2, :], ps[:, RB[e % 2], :], gu[:, j % 2, :], ALU.mult).then_inc(m_done, 1)
                    if k == 0:
                        if j + AHEAD < T1:
                            low_of(w1_low, w1_high, w1h_done, w1l_done, j + AHEAD)
                        low_of(w2_low, w2_high, w2h_done, w2l_done, j)
                    if j > 0:
                        hidden_low(c, j - 1)
                    elif k > 0:
                        hidden_low(c - 1, T1 - 1)
                    if k > 0 and j == LAG1 - 1:
                        result(c - 1)
                    if j == 2 * LAG1:
                        dve.wait_ge(rn_done, c + 1)
                        v.tensor_tensor(null, ps[:, NB, :], cols(h_fm, c), ALU.mult).then_inc(nh_done, 1)
                    beside(c, j, jobs) if k < PEELED1 else None

            for j in range(AHEAD):
                weights_low(j + 1, j)
            run(dve, block0, block1)
            hidden_low(CHUNKS - 1, T1 - 1)
            result(CHUNKS - 1)

        @block.gpsimd
        def _(pool):
            tt = nc.gpsimd.tensor_tensor
            nc.gpsimd.memset(state[:], 0.0).then_inc(state_zero, 1)
            pool.wait_ge(state_zero, 1)
            wide = lambda ap: ap.unsqueeze(3).broadcast_to([P, HEADS, DEPTH, KD])
            tall = lambda ap: ap.unsqueeze(2).broadcast_to([P, HEADS, DEPTH, KD])
            heads = lambda ap: ap.rearrange("p (h v) -> p h v", v=DEPTH)

            def chunk(m, first):
                base = POOL_STEPS * m
                pool.wait_ge(pr_kept, CT * m + CT)
                r, o = raw.rearrange("p q a k -> p (q a) k"), phi[:].rearrange("p q t h k -> p (q t h) k")
                tt(o[:, :, 1:KD], r[:, :, 1:KD], r[:, :, 0:KD - 1], ALU.mult).then_inc(pool_step, 1)
                tt(o[:, :, 0], r[:, :, 0], r[:, :, KD - 1], ALU.mult).then_inc(pool_step, 1)
                pool.wait_ge(phi_sum, 3 * m + 3)
                tt(o, o, prec[:].unsqueeze(2).broadcast_to([P, 2 * CT * HEADS, KD]), ALU.mult).then_inc(pool_step, 1)
                pool.wait_ge(pool_step, base + NORM)
                pool.wait_ge(beta_done, m + 1)
                for s in range(CB):
                    at = base + NORM + PRODUCTS * s
                    for z in range(LT):
                        if not (first and s == 0):
                            pool.wait_ge(y_done, CT * m + LT * s - LT + z + 1)
                        tt(prod[:, z], state[:, z], tall(phi[:, 1, LT * s + z]), ALU.mult).then_inc(pool_step, 1)
                    for z in range(LT):
                        t = LT * s + z
                        uz, key = u[:, z, :], phi[:, 1, t]
                        pool.wait_ge(vbar_done, CT * m + t + 1)
                        tt(uz, vv[:, t, :], vbar[:, z, :], ALU.subtract).then_inc(u_step, 1)
                        pool.wait_ge(u_step, 2 * (CT * m + t) + 1)
                        tt(heads(uz), heads(uz), beta[:, t, :].unsqueeze(2).broadcast_to([P, HEADS, DEPTH]), ALU.mult).then_inc(u_step, 1)
                        pool.wait_ge(u_step, 2 * (CT * m + t) + 2)
                        tt(prod[:, z], wide(heads(uz)), tall(key), ALU.mult).then_inc(pool_step, 1)
                        pool.wait_ge(pool_step, at + OUTER[z])
                        tt(state[:, z], state[:, z], prod[:, z], ALU.add).then_inc(pool_step, 1)
                        pool.wait_ge(pool_step, at + ADD[z])
                        tt(prod[:, z], state[:, z], tall(phi[:, 0, t]), ALU.mult).then_inc(pool_step, 1)
                    pool.wait_ge(pool_step, at + PRODUCTS)

            chunk(0, True)
            with pool.Fori(1, CHUNKS) as m:
                chunk(m, False)


PI_ALL = 2 * DEPTH // 2
NAMES = ("x_fm", "x_tm", "c_fm", "wmod", "w_qk", "b_qk", "w_v", "b_v", "w_fc", "b_fc", "b_o", "ident", "rot", "ident_bf",
         "gate_w", "gate_b", "less8", "wg", "wu", "wd", "sd", "wqkv", "wo", "sel", "wr", "b_r1", "less9", "sel1", "w1", "w2")


def adaln_two_blocks(nc, *args):
    A, out = dict(zip(NAMES, args[:-1])), args[-1]
    with ExitStack() as ctx:
        T = {}

        def sb(name, shape, dt=F32, scope=ctx):
            T[name] = scope.enter_context(nc.sbuf_tensor(name, shape, dt))

        def second_name(name, shape):
            T[name + "_r"] = nc.alloc_sbuf_tensor_at(name + "_r", shape, F32R, offset=nc.sbuf_base - 4 * shape[1])

        for name, shape in dict(x_fm=[P, TOK], h_fm=[P, TOK], ident=[P, P], bq_col=[P, 1], bk_col=[P, 1], bv_col=[P, 1],
                                bfc_col=[P, 1], bo_col=[P, 1], shift=[P, 4, BATCH], scale1=[P, 4, BATCH], gate=[P, 4, BATCH],
                                ga_bfc=[P, BATCH], ga_bo=[P, BATCH], wqkv=[P, QKV1], wo=[P, D], wr=[P, E1], b_r1=[P, E1],
                                less9=[P, E1, E1]).items():
            sb(name, shape)
        sb("ident_bf", [P, P], BF16)
        sb("sel1", [PARTS * E1, E1, P], BF16)
        T["x_tm"] = T["h_fm"]
        T["psum"] = ctx.enter_context(nc.psum_tensor("psum", [P, 8, BANK], F32))
        for name in ("ffn0_loaded", "ffn1_loaded"):
            T[name] = ctx.enter_context(nc.semaphore(name))
        sb("w_gu", [P, WD])
        second_name("w_gu", [P, WD])
        with ExitStack() as first:
            for name, shape in dict(mean=[P, TILES], rstd=[P, TILES], w_qk=[P, 2 * D], w_v=[P, D], w_fc=[P, D]).items():
                sb(name, shape, scope=first)
            setup(nc, T, A)
            attention(nc, T, T["x_fm"], T["x_tm"],
                      (T["scale1"][:, 0, :], T["shift"][:, 0, :], T["gate"][:, 0, :], T["ga_bfc"][:, :]))
        sb("w_d", [P, WEIGHTS - WD])
        second_name("w_d", [P, WEIGHTS - WD])
        sb("sel_buf", [P, RING1 * CHUNK])
        second_name("sel_buf", [P, RING1 * CHUNK])
        T["sel"] = T["sel_buf"][:, 0:HALF_TILES * P // 2].bitcast(BF16).rearrange("p (t r) -> p t r", r=P)
        sb("rw", [P, 2, TOK], BF16)
        route0(nc, T, A)
        experts(nc, T, A, out)


def layout(i):
    bf16 = mybir.dt.np(BF16)
    f = np.ascontiguousarray
    x = i["L0_attn_x"].reshape(TOK, D)
    w, b = i["L0_attn_w_qkv"], i["L0_attn_b_qkv"]
    a = {}
    a["x_fm"] = f(x.T)
    a["x_tm"] = f(x.reshape(TILES, P, D).transpose(1, 0, 2).reshape(P, TOK))
    a["c_fm"] = f(np.stack([i["L0_c"], i["L1_c"]]).transpose(2, 0, 1))
    a["wmod"] = f(np.stack([i["L0_wmod"], i["L1_wmod"]]).transpose(1, 0, 2))
    a["w_qk"] = f(w[:, :2 * D].reshape(D, 2, HEADS, DEPTH).transpose(0, 1, 3, 2).reshape(D, 2 * D))
    a["b_qk"] = f(b[:2 * D].reshape(2, HEADS, DEPTH).transpose(0, 2, 1).reshape(1, 2 * D))
    a["w_v"] = f(w[:, 2 * D:])
    a["b_v"] = f(b[2 * D:].reshape(D, 1))
    a["w_fc"] = i["L0_attn_w_fc"]
    a["b_fc"] = f(i["L0_attn_b_fc"].reshape(D, 1))
    a["b_o"] = f(i["L1_attn_bo"].reshape(D, 1))
    a["ident"] = np.eye(P, dtype=np.float32)
    inv = (1.0 / 10000.0 ** (np.arange(0, DEPTH, 2, dtype=np.float32) / DEPTH)).astype(np.float32)
    ang = (np.arange(HEADS, dtype=np.float32)[:, None] * inv[None, :]).astype(np.float32).T
    a["rot"] = f(np.broadcast_to(np.stack([np.tile(np.cos(ang), (2, 1)), np.tile(np.sin(ang), (2, 1))]), (P, 2, PI_ALL, HEADS)))
    a["ident_bf"] = np.eye(P).astype(bf16)
    a["gate_w"] = f(i["L0_ffn_gate_w"].T)
    a["gate_b"] = f(np.broadcast_to(i["L0_ffn_gate_bias"], (P, EXPERTS)))
    a["less8"] = f(np.broadcast_to(np.tril(np.ones((8, 8), np.float32), -1), (P, 8, 8)))
    for name, w, s in (("wg", "Wg", "Sg"), ("wu", "Wu", "Su")):
        rows = np.concatenate([i["L0_ffn_" + w].reshape(EXPERTS * HIDDEN, D), i["L0_ffn_" + s]])
        a[name] = f(rows.T)
    a["wd"] = f(i["L0_ffn_Wd"].transpose(0, 2, 1).reshape(ROUTED_TILES, P, D).transpose(1, 0, 2).reshape(P, ROUTED_TILES * D))
    a["sd"] = f(i["L0_ffn_Sd"].T.reshape(SHARED_TILES, SHARED_ROWS, D).transpose(1, 0, 2).reshape(SHARED_ROWS, SHARED_TILES * D))
    a["wqkv"] = f(np.concatenate([i["L1_attn_W" + n] for n in "qkvb"], axis=1))
    a["wo"] = i["L1_attn_Wo"]
    owner = (np.arange(HALF_TILES * P) // HIDDEN).reshape(HALF_TILES, P)
    one_hot = (owner[None] == np.arange(EHALF)[:, None, None])
    a["sel"] = f(np.tile(one_hot, (PARTS, 1, 1)).astype(bf16))
    a["wr"] = i["L1_ffn_router_w"]
    a["b_r1"] = f(np.broadcast_to(i["L1_ffn_router_b"], (P, E1)))
    a["less9"] = f(np.broadcast_to(np.tril(np.ones((E1, E1), np.float32), -1), (P, E1, E1)))
    a["sel1"] = f(np.tile(np.broadcast_to(np.eye(E1)[:, :, None], (E1, E1, P)), (PARTS, 1, 1)).astype(bf16))
    a["w1"] = f(i["L1_ffn_w1"].reshape(NE1, D, F1T, P).transpose(1, 0, 2, 3).reshape(D, T1 * P))
    a["w2"] = f(i["L1_ffn_w2"].reshape(NE1, F1T, P, D).transpose(2, 0, 1, 3).reshape(P, T1 * D))
    return a


def kernel(**inputs):
    import concourse.bacc as bacc
    from concourse.bass_utils import run_bass_kernel_spmd

    nc = bacc.Bacc("TRN2", target_bir_lowering=False, num_devices=1)
    placed = layout({name: np.asarray(a) for name, a in inputs.items()})
    arrays = {f"in_{name}": np.ascontiguousarray(placed[name]) for name in NAMES}
    args = [nc.dram_tensor(f"in_{name}", arrays[f"in_{name}"].shape, mybir.dt.from_np(arrays[f"in_{name}"].dtype),
                           kind="ExternalInput").ap() for name in NAMES]
    args.append(nc.dram_tensor("out", (D, TOK), F32, kind="ExternalOutput").ap())
    adaln_two_blocks(nc, *args)
    r = run_bass_kernel_spmd(nc, [arrays], core_ids=[0])
    return np.ascontiguousarray(np.asarray(r.results[0]["out"]).T).reshape(BATCH, SEQ, D)
```

```python
from contextlib import ExitStack

import numpy as np

import concourse.bass as bass
from concourse import mybir

F32 = mybir.dt.float32
BF16 = mybir.dt.bfloat16
F32R = mybir.dt.float32r
ALU = mybir.AluOpType
ACT = mybir.ActivationFunctionType
AX = mybir.AxisListType

P = 128
D = 128
BATCH, SEQ = 16, 256
TOK = BATCH * SEQ
TILES = TOK // P
HEADS, DEPTH = 16, 8
LN_EPS = 1e-5
BANK = 512


def ds(start, size):
    return bass.ds(start, size)


PARTS = 3
PAIRS = PARTS * PARTS
ROWS = PAIRS * DEPTH
ROWS_M = ROWS + PARTS
HALF = HEADS // 2
GROUP = 4
GROUPS = HEADS // GROUP
BUFS = 3
PEELED = 5
STACK_DMAS = PARTS * PARTS + PARTS
VW = 32


def attention(nc, T, x_fm, x_tm, mod):
    ident = T["ident"]
    w_qk, w_v, w_fc, bq_col, bk_col, bv_col = (T[k] for k in ("w_qk", "w_v", "w_fc", "bq_col", "bk_col", "bv_col"))
    ca1, sa, ga, ga_bfc = mod
    rstd, nmean = T["rstd"], T["mean"]
    with ExitStack() as ctx:
        def sb(name, shape, dt=F32):
            return ctx.enter_context(nc.sbuf_tensor(name, shape, dt))

        def sem(name):
            return ctx.enter_context(nc.semaphore(name))

        xn = sb("at_xn", [P, 2, D])
        hb = sb("at_h", [P, BUFS, SEQ])
        qk = sb("at_qk", [P, 2 * SEQ])
        rest = sb("at_rest", [P, 2 * SEQ])
        rest2 = sb("at_rest2", [P, 2 * SEQ])
        part = sb("at_part", [P, PARTS, 2 * SEQ], BF16)
        qs = sb("at_qs", [P, BUFS, HEADS, SEQ], BF16)
        ks = sb("at_ks", [P, BUFS, HEADS, SEQ], BF16)
        v1 = sb("at_v", [P, BUFS, 2, HEADS, VW])
        negm = sb("at_negm", [P, BUFS, 2, HALF, 2])
        nrow = sb("at_nrow", [HALF, SEQ])
        nrest = sb("at_nrest", [HALF, SEQ])
        nrest2 = sb("at_nrest2", [HALF, SEQ])
        nzero = sb("at_nzero", [HALF, SEQ])
        npart = sb("at_npart", [HALF, PARTS, SEQ], BF16)
        pt = sb("at_p", [P, 2 * GROUP, 2, SEQ])
        osb = sb("at_o", [P, GROUPS, SEQ])
        rden = sb("at_rden", [P, 2, HEADS])
        a_tm = sb("at_a", [P, 2, HEADS, DEPTH])
        a_fm = sb("at_afm", [P, SEQ])
        upd = sb("at_upd", [P, SEQ])
        bounce = nc.dram_tensor("qk_parts", [BUFS, 2, PARTS, DEPTH, HEADS, SEQ], BF16, kind="Internal").ap()
        nbounce = nc.dram_tensor("max_parts", [BUFS, 2, PARTS, HALF, SEQ], BF16, kind="Internal").ap()
        ps = T["psum"]
        P1, P2, OB, M0, M1 = [0, 1], [2, 3], (4, 5), 6, 7
        o_ps = ps[:, 4:6, :].rearrange("p a c -> p (a c)")

        filled = sem("at_filled")
        zero_filled = sem("at_zero_filled")
        xn_ready = sem("at_xn_ready")
        xt_done = sem("at_xt_done")
        h_ready = sem("at_h_ready")
        qk_proj = sem("at_qk_proj")
        qk_ready = sem("at_qk_ready")
        part_ready = sem("at_part_ready")
        rest_ready = sem("at_rest_ready")
        part_out = sem("at_part_out")
        stacked = sem("at_stacked")
        p1_done = sem("at_p1_done")
        max_done = sem("at_max_done")
        nrow_ready = sem("at_nrow_ready")
        nsplit = sem("at_nsplit")
        nrows_out = sem("at_nrows_out")
        nrows_in = [sem(f"at_nrows_in{i}") for i in range(2)]
        vn_done = sem("at_vn_done")
        v_ready = sem("at_v_ready")
        p2_done = sem("at_p2_done")
        exp_done = sem("at_exp_done")
        pv_done = sem("at_pv_done")
        o_ready = sem("at_o_ready")
        ot_done = sem("at_ot_done")
        rden_ready = sem("at_rden_ready")
        a_ready = sem("at_a_ready")
        at_done = sem("at_at_done")
        afm_ready = sem("at_afm_ready")
        fc_done = sem("at_fc_done")
        upd_ready = sem("at_upd_ready")
        x_added = sem("at_x_added")
        block = ctx.enter_context(nc.Block())

        def live(k):
            return {
                "xn": 0 <= k + 2 < BATCH, "proj": 0 <= k + 1 < BATCH, "p1": 0 <= k < BATCH,
                "p2": 0 <= k - 1 < BATCH, "tail": 0 <= k - 2 < BATCH,
            }

        def heads(g, part=None):
            first = GROUP * g + (GROUP // 2 if part == 1 else 0)
            return range(first, first + (GROUP if part is None else GROUP // 2))

        def run(eng, iteration):
            for n in range(-2, PEELED):
                iteration(n, n)
            with eng.Fori(0, (BATCH - 2 - PEELED) // BUFS) as i:
                for k in range(PEELED, PEELED + BUFS):
                    iteration(BUFS * i + k, k)
            for n in range(BATCH - 2, BATCH + 2):
                iteration(n, n)

        @block.tensor
        def _(pe):
            def transpose_negm(n, k, half, bank):
                pe.wait_ge(max_done, HEADS * n + HALF * (half + 1))
                for tt in range(2):
                    mm = pe.transpose(ps[0:HALF, bank, SEQ + tt * P:SEQ + (tt + 1) * P], negm[:, k % BUFS, half, :, tt], ident[:])
                return mm

            def scores(n, k, g, part=None):
                f = live(k)
                for h in heads(g, part):
                    if f["p1"]:
                        if h == 0:
                            pe.wait_ge(stacked, 16 * STACK_DMAS * (n + 1))
                        if k > 0 or h >= 2:
                            pe.wait_ge(max_done, HEADS * n + h - 1)
                        for tt in range(2):
                            mm = pe.matmul(ps[:, P1[h % 2], tt * SEQ:(tt + 1) * SEQ],
                                           qs[0:ROWS, k % BUFS, h, tt * P:(tt + 1) * P], ks[0:ROWS, k % BUFS, h, :],
                                           start=True, stop=True)
                        mm.then_inc(p1_done, 1)
                    if f["p2"]:
                        m, j = n - 1, k - 1
                        if h % HALF == 0:
                            pe.wait_ge(nrows_in[h // HALF], 16 * (m + 1))
                        if j > 0 or h >= 2:
                            pe.wait_ge(exp_done, HEADS * m + h - 1)
                        for st in range(2):
                            mm = pe.matmul(ps[:, P2[h % 2], st * SEQ:(st + 1) * SEQ],
                                           ks[0:ROWS_M, j % BUFS, h, st * P:(st + 1) * P], qs[0:ROWS_M, j % BUFS, h, :],
                                           start=True, stop=True)
                        mm.then_inc(p2_done, 1)

            def pv(m, j, g):
                pe.wait_ge(exp_done, HEADS * m + GROUP * (g + 1))
                if g == 0:
                    pe.wait_ge(v_ready, m + 1)
                    if j > 0:
                        pe.wait_ge(o_ready, m)
                for st in range(2):
                    for c in range(GROUP):
                        h = GROUP * g + c
                        mm = pe.matmul(o_ps[VW * c:VW * (c + 1), g * SEQ:(g + 1) * SEQ],
                                       v1[:, j % BUFS, st, h, :], pt[:, h % (2 * GROUP), st, :],
                                       start=(st == 0), stop=(st == 1), tile_position=(0, VW * c))
                mm.then_inc(pv_done, 1)

            def iteration(n, k):
                f = live(k)
                if f["proj"]:
                    pe.wait_ge(h_ready, n + 2)
                    if live(k - 1)["p1"]:
                        pe.wait_ge(nrow_ready, 2 * n - 1)
                    for c in range(2):
                        mm = pe.matmul(ps[:, M0, c * SEQ:(c + 1) * SEQ], w_qk[:, c * P:(c + 1) * P], hb[:, (k + 1) % BUFS, :],
                                       start=True, stop=True)
                    mm.then_inc(qk_proj, 1)
                scores(n, k, 0, 0)
                if f["p1"] or f["p2"]:
                    if f["p1"]:
                        if k >= 3:
                            pe.wait_ge(upd_ready, n - 2)
                        for st in range(2):
                            mm = pe.matmul(ps[:, M1, st * P:(st + 1) * P], hb[:, k % BUFS, st * P:(st + 1) * P], w_v[:],
                                           start=True, stop=True)
                    if f["p2"]:
                        if not f["p1"]:
                            pe.wait_ge(upd_ready, n - 2)
                        mm = transpose_negm(n - 1, k - 1, 1, M1)
                    mm.then_inc(vn_done, 1)
                if f["tail"]:
                    pv(n - 2, k - 2, GROUPS - 1)
                scores(n, k, 0, 1)
                if f["tail"]:
                    pe.wait_ge(o_ready, n - 1)
                    if k >= 3:
                        pe.wait_ge(a_ready, n - 2)
                        pe.wait_ge(upd_ready, n - 2)
                    if f["proj"]:
                        pe.wait_ge(qk_ready, n + 2)
                    if f["p1"] or f["p2"]:
                        pe.wait_ge(v_ready, n + 1)
                        pe.wait_ge(nrow_ready, 2 * n)
                    for tt in range(2):
                        for g in range(GROUPS):
                            mm = pe.transpose(ps[:, M0 + tt, g * P:(g + 1) * P], osb[:, g, tt * P:(tt + 1) * P], ident[:])
                    mm.then_inc(ot_done, 1)
                scores(n, k, 1)
                if f["p2"]:
                    pv(n - 1, k - 1, 0)
                scores(n, k, 2, 0)
                if f["p1"] or f["xn"]:
                    if f["tail"]:
                        pe.wait_ge(a_ready, n - 1)
                    elif f["proj"] and k >= -1:
                        pe.wait_ge(qk_ready, n + 2)
                    if f["xn"]:
                        pe.wait_ge(xn_ready, n + 3)
                        for tt in range(2):
                            mm = pe.transpose(ps[:, M0, tt * P:(tt + 1) * P], xn[:, tt, :], ident[:])
                    if f["p1"]:
                        mm = transpose_negm(n, k, 0, M0)
                    mm.then_inc(xt_done, 1)
                scores(n, k, 2, 1)
                if f["p2"]:
                    pv(n - 1, k - 1, 1)
                if f["tail"]:
                    pe.wait_ge(a_ready, n - 1)
                    for tt in range(2):
                        mm = pe.transpose(ps[:, M1, tt * P:(tt + 1) * P],
                                          a_tm[:, tt, :, :].rearrange("p h d -> p (h d)"), ident[:])
                    mm.then_inc(at_done, 1)
                scores(n, k, 3)
                if f["p2"]:
                    pv(n - 1, k - 1, 2)
                if f["tail"]:
                    pe.wait_ge(afm_ready, n - 1)
                    pe.matmul(ps[:, M1, 0:SEQ], w_fc[:], a_fm[:], start=True, stop=True).then_inc(fc_done, 1)

            run(pe, iteration)

        @block.vector
        def _(dve):
            def maxima(n, k, g):
                if not live(k)["p1"]:
                    return
                for h in range(GROUP * g, GROUP * (g + 1)):
                    dve.wait_ge(p1_done, HEADS * n + h + 1)
                    if h == 0 and k >= 2:
                        dve.wait_ge(vn_done, n)
                    nc.vector.tensor_reduce(negm[:, k % BUFS, h // HALF, h % HALF, :],
                                            ps[:, P1[h % 2], :].rearrange("p (t s) -> p t s", t=2),
                                            AX.X, ALU.max, negate=True).then_inc(max_done, 1)

            def iteration(n, k):
                f = live(k)
                if f["xn"]:
                    if k >= -1:
                        dve.wait_ge(xt_done, n + 2)
                    for tt in range(2):
                        t = 2 * n + 4 + tt
                        ins = nc.vector.tensor_scalar(xn[:, tt, :], x_tm[:, ds(t * D, D)], nmean[:, ds(t, 1)], rstd[:, ds(t, 1)],
                                                      ALU.subtract, ALU.mult)
                    ins.then_inc(xn_ready, 1)
                if f["proj"]:
                    dve.wait_ge(qk_proj, n + 2)
                    if k >= 0:
                        dve.wait_ge(part_ready, PARTS * (n + 1))
                    nc.vector.tensor_scalar(qk[:, 0:SEQ], ps[:, M0, 0:SEQ], bq_col[:, 0:1], None, ALU.add)
                    nc.vector.tensor_scalar(qk[:, SEQ:2 * SEQ], ps[:, M0, SEQ:2 * SEQ], bk_col[:, 0:1], None, ALU.add)\
                        .then_inc(qk_ready, 1)
                maxima(n, k, 0)
                if f["proj"]:
                    dve.wait_ge(part_ready, PARTS * (n + 1) + 1)
                    nc.vector.tensor_tensor(rest[:], qk[:], part[:, 0, :], ALU.subtract).then_inc(rest_ready, 1)
                maxima(n, k, 1)
                if f["proj"]:
                    dve.wait_ge(part_ready, PARTS * (n + 1) + 2)
                    nc.vector.tensor_tensor(rest2[:], rest[:], part[:, 1, :], ALU.subtract).then_inc(rest_ready, 1)
                if f["tail"]:
                    dve.wait_ge(ot_done, n - 1)
                    ov = ps[:, 6:8, :].rearrange("p t (h c) -> p (t h) c", c=VW)
                    nc.vector.reciprocal(rden[:].rearrange("p t h -> p (t h)"), ov[:, :, DEPTH]).then_inc(rden_ready, 1)
                    dve.wait_ge(rden_ready, n - 1)
                    if k >= 3:
                        dve.wait_ge(at_done, n - 2)
                    nc.vector.tensor_tensor(a_tm[:].rearrange("p t h d -> p (t h) d"), ov[:, :, 0:DEPTH],
                                            rden[:].rearrange("p t h -> p (t h)").unsqueeze(2).broadcast_to([P, 2 * HEADS, DEPTH]),
                                            ALU.mult).then_inc(a_ready, 1)
                maxima(n, k, 2)
                maxima(n, k, 3)

            nc.vector.memset(v1[:], 0.0).then_inc(filled, 1)
            nc.vector.memset(ks[64:ROWS_M, :, :, :], 1.0).then_inc(filled, 1)
            dve.wait_ge(filled, 2)
            nc.vector.memset(v1[:, :, :, :, DEPTH], 1.0).then_inc(filled, 1)
            run(dve, iteration)

        @block.scalar
        def _(act):
            def exps(n, k, g, part=None):
                for h in heads(g, part):
                    act.wait_ge(p2_done, HEADS * n + h + 1)
                    if h % GROUP == 0 and (k > 0 or g >= 2):
                        act.wait_ge(pv_done, GROUPS * n + g - 1)
                    nc.scalar.activation(pt[:, h % (2 * GROUP), :, :].rearrange("p s t -> p (s t)"), ps[:, P2[h % 2], :],
                                         ACT.Exp, scale=float(1.0 / np.sqrt(np.float32(DEPTH)))).then_inc(exp_done, 1)

            def cut(n, k, i):
                if i == 0:
                    act.wait_ge(qk_ready, n + 2)
                    if k >= 0:
                        act.wait_ge(part_out, 32 * (n + 1))
                else:
                    act.wait_ge(rest_ready, 2 * (n + 1) + i)
                nc.scalar.activation(part[:, i, :], (qk, rest, rest2)[i][:], ACT.Copy).then_inc(part_ready, 1)

            def iteration(n, k):
                f = live(k)
                if f["proj"]:
                    cut(n, k, 0)
                if f["p2"]:
                    exps(n - 1, k - 1, 0, 0)
                if f["p1"] or f["p2"]:
                    act.wait_ge(vn_done, n + 1)
                if f["p1"]:
                    if k >= 3:
                        act.wait_ge(pv_done, GROUPS * (n - 2))
                    nc.scalar.activation(v1[:, k % BUFS, :, :, 0:DEPTH],
                                         ps[:, M1, 0:SEQ].rearrange("p (s h d) -> p s h d", s=2, d=DEPTH), ACT.Copy)\
                        .then_inc(v_ready, 1)
                if f["p2"]:
                    if not f["p1"]:
                        nc.scalar.sem_inc(v_ready, 1)
                    act.wait_ge(nsplit, 5 * (2 * n - 1))
                    nc.scalar.activation(nrow[:], ps[0:HALF, M1, SEQ:2 * SEQ], ACT.Copy).then_inc(nrow_ready, 1)
                if f["tail"]:
                    act.wait_ge(pv_done, GROUPS * (n - 1))
                    if k >= 3:
                        act.wait_ge(ot_done, n - 2)
                    nc.scalar.activation(osb[:].rearrange("p g t -> p (g t)"), o_ps, ACT.Copy).then_inc(o_ready, 1)
                if f["p2"]:
                    exps(n - 1, k - 1, 0, 1)
                if f["proj"]:
                    cut(n, k, 1)
                if f["p2"]:
                    exps(n - 1, k - 1, 1)
                if f["proj"]:
                    cut(n, k, 2)
                if f["p2"]:
                    exps(n - 1, k - 1, 2, 0)
                if f["p1"] or f["xn"]:
                    act.wait_ge(xt_done, n + 3)
                    if f["xn"]:
                        b = n + 2
                        nc.scalar.activation(hb[:, (k + 2) % BUFS, :], ps[:, M0, 0:SEQ], ACT.Identity, bias=sa[:, ds(b, 1)],
                                             scale=ca1[:, ds(b, 1)]).then_inc(h_ready, 1)
                    if f["p1"]:
                        if k > 0:
                            act.wait_ge(nsplit, 5 * 2 * n)
                        nc.scalar.activation(nrow[:], ps[0:HALF, M0, SEQ:2 * SEQ], ACT.Copy).then_inc(nrow_ready, 1)
                if f["p2"]:
                    exps(n - 1, k - 1, 2, 1)
                if f["tail"]:
                    act.wait_ge(at_done, n - 1)
                    if k >= 3:
                        act.wait_ge(fc_done, n - 2)
                    nc.scalar.activation(a_fm[:], ps[:, M1, 0:SEQ], ACT.Identity, bias=bv_col[:, 0:1]).then_inc(afm_ready, 1)
                if f["p2"]:
                    exps(n - 1, k - 1, 3)
                if f["tail"]:
                    b = n - 2
                    act.wait_ge(fc_done, n - 1)
                    if k >= 3:
                        act.wait_ge(x_added, n - 2)
                    nc.scalar.activation(upd[:], ps[:, M1, 0:SEQ], ACT.Identity, bias=ga_bfc[:, ds(b, 1)],
                                         scale=ga[:, ds(b, 1)]).then_inc(upd_ready, 1)

            act.wait_ge(filled, 3)
            run(act, iteration)

        @block.gpsimd
        def _(pool):
            def split_rows(n, k, half):
                c = 5 * (2 * n + half)
                pool.wait_ge(nrow_ready, 2 * n + half + 1)
                if k > 0 or half > 0:
                    pool.wait_ge(nrows_out, 16 * (2 * n + half))
                nc.gpsimd.tensor_tensor(npart[:, 0, :], nrow[:], nzero[:], ALU.add).then_inc(nsplit, 1)
                pool.wait_ge(nsplit, c + 1)
                nc.gpsimd.tensor_tensor(nrest[:], nrow[:], npart[:, 0, :], ALU.subtract).then_inc(nsplit, 1)
                pool.wait_ge(nsplit, c + 2)
                nc.gpsimd.tensor_tensor(npart[:, 1, :], nrest[:], nzero[:], ALU.add).then_inc(nsplit, 1)
                pool.wait_ge(nsplit, c + 3)
                nc.gpsimd.tensor_tensor(nrest2[:], nrest[:], npart[:, 1, :], ALU.subtract).then_inc(nsplit, 1)
                pool.wait_ge(nsplit, c + 4)
                nc.gpsimd.tensor_tensor(npart[:, 2, :], nrest2[:], nzero[:], ALU.add).then_inc(nsplit, 1)

            def iteration(n, k):
                f = live(k)
                if f["p2"]:
                    split_rows(n - 1, k - 1, 1)
                if f["p1"]:
                    split_rows(n, k, 0)
                if f["tail"]:
                    b = n - 2
                    pool.wait_ge(upd_ready, n - 1)
                    cols = x_fm[:, ds(b * SEQ, SEQ)]
                    nc.gpsimd.tensor_tensor(cols, cols, upd[:], ALU.add).then_inc(x_added, 1)

            nc.gpsimd.memset(nzero[:], 0.0).then_inc(zero_filled, 1)
            pool.wait_ge(zero_filled, 1)
            run(pool, iteration)

        @block.sync
        def _(sp):
            def held(name, x):
                if isinstance(x, int):
                    return x
                r = sp.alloc_register(name)
                sp.reg_mov(r, x)
                return sp.snap(r)

            def load_stacks(buf, between):
                for a in range(PARTS):
                    for b in range(PARTS):
                        r = DEPTH * (PARTS * a + b)
                        sp.dma_start(qs[r:r + DEPTH, buf, :, :], bounce[buf, 0, a]).then_inc(stacked, 16)
                    r = DEPTH * PARTS * a
                    sp.dma_start(ks[r:r + DEPTH * PARTS, buf, :, :],
                                 bounce[buf, 1].rearrange("b d h t -> (b d) h t")).then_inc(stacked, 16)
                    between[a]()

            def store_rows(buf, half, split):
                sp.wait_ge(nsplit, split)
                sp.dma_start(nbounce[buf, half].rearrange("i h t -> h i t"), npart[:]).then_inc(nrows_out, 16)

            def load_rows(buf, half, out):
                sp.wait_ge(nrows_out, out)
                sp.dma_start(qs[ROWS:ROWS_M, buf, HALF * half:HALF * (half + 1), :], nbounce[buf, half]).then_inc(nrows_in[half], 16)

            def iteration(n, k):
                f = live(k)
                buf = (k + 1) % BUFS
                split1 = held(f"split1_{k}", 10 * n)
                split0 = held(f"split0_{k}", 10 * n + 5)
                cut = held(f"cut_{k}", PARTS * (n + 2))
                rows1 = held(f"rows1_{k}", 32 * n)
                rows0 = held(f"rows0_{k}", 32 * n + 16)
                seen = held(f"seen_{k}", HEADS * n + 1)
                out = held(f"out_{k}", 32 * (n + 2))
                if f["p2"]:
                    store_rows((k - 1) % BUFS, 1, split1)
                    load_rows((k - 1) % BUFS, 1, rows1)
                if f["proj"]:
                    sp.wait_ge(part_ready, cut)
                    for q in range(2):
                        sp.dma_start(bounce[buf, q].rearrange("a d h t -> (d h) a t"), part[:, :, q * SEQ:(q + 1) * SEQ])\
                            .then_inc(part_out, 16)
                    if f["p1"]:
                        sp.wait_ge(p1_done, seen)
                    sp.wait_ge(part_out, out)
                    nothing = lambda: None
                    if f["p1"]:
                        load_stacks(buf, (nothing, lambda: store_rows(k % BUFS, 0, split0), lambda: load_rows(k % BUFS, 0, rows0)))
                    else:
                        load_stacks(buf, (nothing, nothing, nothing))
                elif f["p1"]:
                    store_rows(k % BUFS, 0, split0)
                    load_rows(k % BUFS, 0, rows0)

            sp.wait_ge(filled, 3)
            run(sp, iteration)


MODS = 6


def setup(nc, T, A):
    with ExitStack() as ctx:
        def sb(name, shape, dt=F32):
            return ctx.enter_context(nc.sbuf_tensor(name, shape, dt))

        def sem(name):
            return ctx.enter_context(nc.semaphore(name))

        c_fm = sb("su_c", [P, 2, BATCH])
        cs = sb("su_cs", [P, 2, BATCH])
        wmod = sb("su_wmod", [P, 2, MODS * D])
        rot = sb("su_rot", [P, 2, PI_ALL, HEADS])
        w_in = sb("su_w", [P, 2 * D])
        b_in = sb("su_b", [1, 2 * D])
        b_rot = sb("su_brot", [1, 2 * D])
        t0 = sb("su_t0", [P, PI_ALL, HEADS])
        t1 = sb("su_t1", [P, PI_ALL, HEADS])
        u0 = sb("su_u0", [1, PI_ALL, HEADS])
        u1 = sb("su_u1", [1, PI_ALL, HEADS])
        one = sb("su_one", [1, 1])
        stats = sb("su_stats", [P, TILES, 6])
        var = sb("su_var", [P, TILES])
        dm = sb("su_dm", [P, TILES])
        sg = sb("su_sg", [P, 2 * 2, BATCH])
        ab = sb("su_ab", [P, 2 * 2, BATCH])
        ps = T["psum"]
        x_in = sem("su_x_in")
        c_in = sem("su_c_in")
        w_loaded = sem("su_w_loaded")
        silu_done = sem("su_silu_done")
        mod_done = sem("su_mod_done")
        bias_done = sem("su_bias_done")
        var_ready = sem("su_var_ready")
        std_ready = sem("su_std_ready")
        step = sem("su_step")
        rot_ready = sem("su_rot_ready")
        pool_done = sem("su_pool_done")
        block = ctx.enter_context(nc.Block())

        @block.sync
        def _(sp):
            sp.dma_start(T["x_tm"][:], A["x_tm"]).then_inc(x_in, 16)
            sp.dma_start(T["x_fm"][:], A["x_fm"]).then_inc(w_loaded, 16)
            sp.wait_ge(w_loaded, 16 * 10)
            sp.dma_start(T["w_gu"][:, WG:WU], A["wg"]).then_inc(T["ffn0_loaded"], 16)
            sp.dma_start(T["w_gu"][:, WU:WD], A["wu"]).then_inc(T["ffn0_loaded"], 16)
            for name in EARLY_LOADS:
                sp.dma_start(T[name][:], A[name]).then_inc(T["ffn0_loaded"], 16)

        @block.gpsimd
        def _(pool):
            pool.memset(one[:], 1.0).then_inc(pool_done, 1)

        @block.scalar
        def _(act):
            act.dma_start(c_fm[:], A["c_fm"]).then_inc(c_in, 16)
            act.dma_start(wmod[:], A["wmod"]).then_inc(c_in, 16)
            for dst, src in ((w_in[:], A["w_qk"]), (b_in[:], A["b_qk"]), (rot[:], A["rot"]), (T["w_v"][:], A["w_v"]),
                             (T["w_fc"][:], A["w_fc"]), (T["bv_col"][:], A["b_v"]), (T["bfc_col"][:], A["b_fc"]),
                             (T["ident"][:], A["ident"]), (T["bo_col"][:], A["b_o"])):
                act.dma_start(dst, src).then_inc(w_loaded, 16)
            act.wait_ge(c_in, 32)
            nc.scalar.activation(cs[:], c_fm[:], ACT.Silu).then_inc(silu_done, 1)
            act.wait_ge(var_ready, 1)
            nc.scalar.activation(dm[:], var[:], ACT.Sqrt).then_inc(std_ready, 1)

        @block.tensor
        def _(pe):
            pe.wait_ge(silu_done, 1)
            for l in range(2):
                for m in range(MODS):
                    at = (l * MODS + m) * BATCH
                    mm = pe.matmul(ps[:, 0, at:at + BATCH], wmod[:, l, m * D:(m + 1) * D], cs[:, l, :], start=True, stop=True)
            mm.then_inc(mod_done, 1)
            pe.wait_ge(rot_ready, 1)
            pe.wait_ge(pool_done, 1)
            for c in range(2):
                mm = pe.matmul(ps[:, 1, c:c + 1], b_rot[:, c * P:(c + 1) * P], one[:], start=True, stop=True)
            mm.then_inc(bias_done, 1)

        @block.vector
        def _(dve):
            n = 0
            dve.wait_ge(x_in, 16)
            for t in range(TILES):
                ins = nc.vector.bn_stats(stats[:, t, :], T["x_tm"][:, t * D:(t + 1) * D])
            ins.then_inc(step, 1)
            dve.wait_ge(step, 1)
            me, mo, ve, vo = (stats[:, :, i] for i in (1, 4, 2, 5))
            nc.vector.tensor_tensor(T["mean"][:], me, mo, ALU.add).then_inc(step, 1)
            nc.vector.tensor_tensor(dm[:], me, mo, ALU.subtract).then_inc(step, 1)
            nc.vector.tensor_tensor(var[:], ve, vo, ALU.add).then_inc(step, 1)
            dve.wait_ge(step, 4)
            nc.vector.tensor_scalar(T["mean"][:], T["mean"][:], 0.5, None, ALU.mult).then_inc(step, 1)
            nc.vector.scalar_tensor_tensor(dm[:], dm[:], 0.25, dm[:], ALU.mult, ALU.mult).then_inc(step, 1)
            nc.vector.tensor_scalar(var[:], var[:], 1.0 / D, LN_EPS, ALU.mult, ALU.add).then_inc(step, 1)
            dve.wait_ge(step, 7)
            nc.vector.tensor_tensor(var[:], var[:], dm[:], ALU.add).then_inc(var_ready, 1)
            dve.wait_ge(w_loaded, 16 * 10)
            for w, out, a, b, q in ((w_in, T["w_qk"], t0, t1, P), (b_in, b_rot, u0, u1, 1)):
                wv = w[:].rearrange("p (i two h) -> p i two h", two=2, h=HEADS)
                ov = out[:].rearrange("p (i two h) -> p i two h", two=2, h=HEADS)
                cos, sin = rot[0:q, 0], rot[0:q, 1]
                for o, (x, y, op) in enumerate(((cos, sin, ALU.subtract), (sin, cos, ALU.add))):
                    nc.vector.tensor_tensor(a[:], wv[:, :, 0, :], x, ALU.mult).then_inc(step, 1)
                    nc.vector.tensor_tensor(b[:], wv[:, :, 1, :], y, ALU.mult).then_inc(step, 1)
                    n += 3
                    dve.wait_ge(step, 7 + n - 1)
                    nc.vector.tensor_tensor(ov[:, :, o, :], a[:], b[:], op).then_inc(step, 1)
                    dve.wait_ge(step, 7 + n)
            nc.vector.sem_inc(rot_ready, 1)
            dve.wait_ge(mod_done, 1)
            m = ps[:, 0, 0:2 * MODS * BATCH].rearrange("p (l k b) -> p l k b", k=3, b=BATCH)
            nc.vector.tensor_copy(T["shift"][:], m[:, :, 0, :])
            nc.vector.tensor_scalar(T["scale1"][:], m[:, :, 1, :], 1.0, None, ALU.add)
            nc.vector.tensor_scalar(sg[:], m[:, :, 2, :], 0.0, 2.0, ALU.is_ge, ALU.mult).then_inc(step, 1)
            dve.wait_ge(step, 8 + n)
            nc.vector.tensor_scalar(sg[:], sg[:], -1.0, None, ALU.add).then_inc(step, 1)
            dve.wait_ge(step, 9 + n)
            nc.vector.tensor_tensor(ab[:], sg[:], m[:, :, 2, :], ALU.mult).then_inc(step, 1)
            dve.wait_ge(step, 10 + n)
            nc.vector.scalar_tensor_tensor(T["gate"][:], ab[:], 0.25, sg[:], ALU.max, ALU.mult).then_inc(step, 1)
            dve.wait_ge(step, 11 + n)
            nc.vector.tensor_scalar(T["ga_bfc"][:], T["gate"][:, 0, :], T["bfc_col"][:, 0:1], None, ALU.mult)
            nc.vector.tensor_scalar(T["ga_bo"][:], T["gate"][:, 2, :], T["bo_col"][:, 0:1], None, ALU.mult)
            dve.wait_ge(bias_done, 1)
            nc.vector.tensor_copy(T["bq_col"][:], ps[:, 1, 0:1])
            nc.vector.tensor_copy(T["bk_col"][:], ps[:, 1, 1:2])
            dve.wait_ge(std_ready, 1)
            nc.vector.reciprocal(T["rstd"][:], dm[:]).then_inc(step, 1)
            dve.wait_ge(step, 12 + n)


CHUNK = 512
CHUNKS = TOK // CHUNK
CT = CHUNK // P
CB = CHUNK // SEQ


class LayerNorm:

    def __init__(self, nc, ctx, name, T, xc, hc, nt, bank, part):
        self.nc, self.T, self.xc, self.hc, self.part = nc, T, xc, hc, part
        self.ps = T["psum"][:, bank, :]
        sb = lambda n, s: ctx.enter_context(nc.sbuf_tensor(f"{name}_{n}", s, F32))
        self.st, self.mv, self.sd, self.rs = sb("st", [P, CT, 6]), sb("mv", [P, CT, 2]), sb("sd", [P, CT]), sb("rs", [P, CT])
        self.nt = nt
        sem = lambda n: ctx.enter_context(nc.semaphore(f"{name}_{n}"))
        self.x_tm = sem("x_tm")
        self.mean = sem("mean")
        self.std = sem("std")
        self.norm = sem("norm")
        self.n_fm = sem("n_fm")
        self.h = sem("h")

    def pe_x(self, pe):
        for t in range(CT):
            mm = pe.transpose(self.ps[:, t * P:(t + 1) * P], self.xc[:, t * P:(t + 1) * P], self.T["ident"][:])
        mm.then_inc(self.x_tm, 1)

    def dve_stats(self, dve, c):
        v = self.nc.vector
        dve.wait_ge(self.x_tm, c + 1)
        for t in range(CT):
            ins = v.bn_stats(self.st[:, t, :], self.ps[:, t * P:(t + 1) * P])
        ins.then_inc(self.mean, 1)
        me, mo, ve, vo = (self.st[:, :, i] for i in (1, 4, 2, 5))
        mean, dif = self.mv[:, :, 0], self.mv[:, :, 1]
        dve.wait_ge(self.mean, 4 * c + 1)
        v.tensor_tensor(mean, me, mo, ALU.add)
        v.tensor_tensor(dif, me, mo, ALU.subtract)
        v.tensor_tensor(self.rs[:], ve, vo, ALU.add).then_inc(self.mean, 1)
        dve.wait_ge(self.mean, 4 * c + 2)
        v.tensor_scalar(mean, mean, 0.5, None, ALU.mult)
        v.scalar_tensor_tensor(dif, dif, 0.25, dif, ALU.mult, ALU.mult)
        v.tensor_scalar(self.rs[:], self.rs[:], 1.0 / D, LN_EPS, ALU.mult, ALU.add).then_inc(self.mean, 1)
        dve.wait_ge(self.mean, 4 * c + 3)
        v.tensor_tensor(self.rs[:], self.rs[:], dif, ALU.add).then_inc(self.mean, 1)

    def act_std(self, act, c):
        act.wait_ge(self.mean, 4 * c + 4)
        self.nc.scalar.activation(self.sd[:], self.rs[:], ACT.Sqrt).then_inc(self.std, 1)

    def dve_norm(self, dve, c):
        v = self.nc.vector
        dve.wait_ge(self.std, c + 1)
        v.reciprocal(self.rs[:], self.sd[:]).then_inc(self.norm, 1)
        dve.wait_ge(self.norm, 2 * c + 1)
        for t in range(CT):
            ins = v.tensor_scalar(self.nt[:, t, :], self.ps[:, t * P:(t + 1) * P], self.mv[:, t, 0:1], self.rs[:, t:t + 1],
                                  ALU.subtract, ALU.mult)
        ins.then_inc(self.norm, 1)

    def pe_n(self, pe, c):
        pe.wait_ge(self.norm, 2 * c + 2)
        for t in range(CT):
            mm = pe.transpose(self.ps[:, t * P:(t + 1) * P], self.nt[:, t, :], self.T["ident"][:])
        mm.then_inc(self.n_fm, 1)

    def act_h(self, act, c, chunk=None):
        act.wait_ge(self.n_fm, c + 1)
        for i in range(CB):
            b = CB * (c if chunk is None else chunk) + i
            ins = self.nc.scalar.activation(self.hc[:, i * SEQ:(i + 1) * SEQ], self.ps[:, i * SEQ:(i + 1) * SEQ], ACT.Identity,
                                            bias=self.T["shift"][:, self.part, ds(b, 1)],
                                            scale=self.T["scale1"][:, self.part, ds(b, 1)])
        ins.then_inc(self.h, 1)


def cols(t, c, size=CHUNK):
    return t[:, ds(c * size, size)]


class Steps:

    def __init__(self, eng, sem, base=0):
        self.eng, self.sem, self.base, self.n = eng, sem, base, 0

    def done(self, ins, wait=True):
        ins.then_inc(self.sem, 1)
        self.n += 1
        if wait:
            self.eng.wait_ge(self.sem, self.base + self.n)


EXPERTS, HIDDEN = 64, 88
EGROUPS, EPG = 8, 8
TOP_GROUPS = 4
ROUTED_SCALE = 2.5
EHALF = EXPERTS // 2
TAKEN = -1.0e30


def route0(nc, T, A):
    x_fm, h_fm, ps = T["x_fm"], T["h_fm"], T["psum"]
    with ExitStack() as ctx:
        def sb(name, shape, dt=F32):
            return ctx.enter_context(nc.sbuf_tensor(name, shape, dt))

        def sem(name):
            return ctx.enter_context(nc.semaphore(name))

        xc, hc = sb("r0_xc", [P, 2, CHUNK]), sb("r0_hc", [P, 2, CHUNK])
        ln = [LayerNorm(nc, ctx, f"r0_ln{i}", T, xc[:, i, :], hc[:, i, :], sb(f"r0_nt{i}", [P, CT, D]), i, 1) for i in range(2)]
        LB = 6
        N = TILES * EXPERTS
        lg = sb("r0_lg", [P, N])
        sfc = sb("r0_sfc", [P, N])
        w0 = sb("r0_w0", [P, N])
        w1 = sb("r0_w1", [P, N])
        G = TILES * EGROUPS
        hi, lo, th, tl = (sb(f"r0_{n}", [P, G, 4]) for n in ("hi", "lo", "th", "tl"))
        gs, rank = sb("r0_gs", [P, G]), sb("r0_rank", [P, G])
        top = sb("r0_top", [P, TILES, 8])
        den, rden = sb("r0_den", [P, TILES]), sb("r0_rden", [P, TILES])
        parts = sb("r0_parts", [P, TILES, 2, PARTS, EHALF], BF16)
        gate_w, gate_b = sb("r0_gw", [P, EXPERTS]), sb("r0_gb", [P, EXPERTS])
        less = sb("r0_less", [P, EGROUPS, EGROUPS])
        loaded = sem("r0_loaded")
        xc_ready = sem("r0_xc_ready")
        h_kept = sem("r0_h_kept")
        lg_done = sem("r0_lg_done")
        lg_kept = sem("r0_lg_kept")
        scored = sem("r0_scored")
        step = sem("r0_step")
        cut = sem("r0_cut")
        tr_done = sem("r0_tr_done")
        tr_kept = [sem(f"r0_tr_kept{g}") for g in range(2)]
        block = ctx.enter_context(nc.Block())

        def has(k):
            return 0 <= k < CHUNKS

        pair = {}

        def nth(c, k):
            return c // 2 if isinstance(c, int) else pair["i"] + (k - 4) // 2

        def run(eng, step_):
            for c in range(4):
                step_(c, c)
            with eng.Fori(2, CHUNKS // 2) as i:
                pair["i"] = i
                for k in (4, 5):
                    step_(2 * i + k - 4, k)
            for c in range(CHUNKS, CHUNKS + 2):
                step_(c, c)

        @block.sync
        def _(sp):
            sp.dma_start(gate_w[:], A["gate_w"]).then_inc(loaded, 16)
            sp.dma_start(gate_b[:], A["gate_b"]).then_inc(loaded, 16)
            sp.dma_start(less[:], A["less8"]).then_inc(loaded, 16)
            routed = ROUTED_TILES * D
            sp.dma_start(T["sel"][0:PARTS * EHALF], A["sel"]).then_inc(T["ffn0_loaded"], 16)
            sp.dma_start(T["w_d"][:, 0:routed], A["wd"]).then_inc(T["ffn0_loaded"], 16)
            sp.dma_start(T["w_d"][0:SHARED_ROWS, routed:HT * D], A["sd"]).then_inc(T["ffn0_loaded"], 16)

        @block.tensor
        def _(pe):
            pe.wait_ge(loaded, 48)

            def step_(c, k):
                if has(k):
                    pe.wait_ge(xc_ready, c + 1)
                    ln[k % 2].pe_x(pe)
                if has(k - 1):
                    ln[(k - 1) % 2].pe_n(pe, nth(c - 1, k - 1))
                if has(k - 2):
                    l = ln[k % 2]
                    pe.wait_ge(l.h, nth(c - 2, k - 2) + 1)
                    if k - 2 >= 2:
                        pe.wait_ge(lg_kept, c - 3)
                    for t in range(CT):
                        mm = pe.matmul(ps[:, LB + k % 2, t * EXPERTS:(t + 1) * EXPERTS], l.hc[:, t * P:(t + 1) * P], gate_w[:],
                                       start=True, stop=True)
                    mm.then_inc(lg_done, 1)

            run(pe, step_)
            pe.wait_ge(cut, 1)
            pe.wait_ge(T["ffn0_loaded"], 16 * FFN0_LOADS)

            def turn(c, k):
                if k >= 2:
                    for g in range(2):
                        pe.wait_ge(tr_kept[g], c - 1)
                for g in range(2):
                    for t in range(CT):
                        mm = pe.matmul(ps[0:PARTS * EHALF, 2 + 2 * (k % 2) + g, t * P:(t + 1) * P],
                                       parts[:, ds(CT * c + t, 1), g, :, :].rearrange("p o i e -> p (o i e)"), T["ident_bf"][:],
                                       start=True, stop=True)
                mm.then_inc(tr_done, 1)

            turn(0, 0)
            turn(1, 1)
            with pe.Fori(1, CHUNKS // 2) as i:
                turn(2 * i, 2)
                turn(2 * i + 1, 3)

        @block.scalar
        def _(act):
            def step_(c, k):
                if has(k):
                    if k >= 2:
                        act.wait_ge(ln[k % 2].x_tm, nth(c, k))
                    nc.scalar.activation(xc[:, k % 2, :], cols(x_fm, c), ACT.Copy).then_inc(xc_ready, 1)
                if has(k - 1):
                    if k - 1 >= 2:
                        act.wait_ge(lg_done, c - 2)
                        act.wait_ge(h_kept, c - 2)
                    ln[(k - 1) % 2].act_h(act, nth(c - 1, k - 1), c - 1)
                if has(k):
                    ln[k % 2].act_std(act, nth(c, k))

            run(act, step_)
            act.wait_ge(lg_kept, CHUNKS)
            nc.scalar.activation(lg[:], lg[:], ACT.Sigmoid).then_inc(scored, 1)

            def keep(c, k):
                act.wait_ge(tr_done, c + 1)
                nc.scalar.activation(T["rw"][0:PARTS * EHALF, 0, ds(c * CHUNK, CHUNK)], ps[0:PARTS * EHALF, 2 + 2 * (k % 2), :], ACT.Copy)\
                    .then_inc(tr_kept[0], 1)

            with act.Fori(0, CHUNKS // 2) as i:
                keep(2 * i, 0)
                keep(2 * i + 1, 1)

        @block.vector
        def _(dve):
            v = nc.vector
            dve.wait_ge(loaded, 48)

            def step_(c, k):
                if has(k - 1):
                    ln[(k - 1) % 2].dve_norm(dve, nth(c - 1, k - 1))
                if has(k):
                    ln[k % 2].dve_stats(dve, nth(c, k))
                if has(k - 2):
                    dve.wait_ge(ln[k % 2].h, nth(c - 2, k - 2) + 1)
                    v.tensor_copy(cols(h_fm, c - 2), hc[:, k % 2, :]).then_inc(h_kept, 1)
                    dve.wait_ge(lg_done, c - 1)
                    v.tensor_copy(lg[:, ds((c - 2) * CT * EXPERTS, CT * EXPERTS)], ps[:, LB + k % 2, 0:CT * EXPERTS]).then_inc(lg_kept, 1)

            run(dve, step_)

            s = Steps(dve, step)
            dve.wait_ge(scored, 1)
            per_tile = lambda t: t[:].rearrange("p (t e) -> p t e", e=EXPERTS)
            s.done(v.tensor_tensor(per_tile(sfc), per_tile(lg), gate_b[:].unsqueeze(1).broadcast_to([P, TILES, EXPERTS]), ALU.add))
            q = sfc[:].rearrange("p (g e) -> p g e", e=EPG)
            s.done(v.tensor_tensor(hi[:], q[:, :, 0:4], q[:, :, 4:8], ALU.max), False)
            s.done(v.tensor_tensor(lo[:], q[:, :, 0:4], q[:, :, 4:8], ALU.min))
            for w in (2, 1):
                s.done(v.tensor_tensor(th[:, :, 0:w], hi[:, :, 0:w], hi[:, :, w:2 * w], ALU.min), False)
                s.done(v.tensor_tensor(tl[:, :, 0:w], lo[:, :, 0:w], lo[:, :, w:2 * w], ALU.max))
                s.done(v.tensor_tensor(hi[:, :, 0:w], hi[:, :, 0:w], hi[:, :, w:2 * w], ALU.max), False)
                s.done(v.tensor_tensor(lo[:, :, 0:w], th[:, :, 0:w], tl[:, :, 0:w], ALU.max))
            s.done(v.tensor_tensor(gs[:], hi[:, :, 0], lo[:, :, 0], ALU.add))
            own = gs[:].rearrange("p (t g) -> p t g", g=EGROUPS)
            for t4 in range(4):
                r = slice(8 * t4, 8 * t4 + 8)
                a = own[:, r, :].unsqueeze(2).broadcast_to([P, 8, EGROUPS, EGROUPS])
                b = own[:, r, :].unsqueeze(3).broadcast_to([P, 8, EGROUPS, EGROUPS])
                o0 = w0[:, 512 * t4:512 * t4 + 512].rearrange("p (t g e) -> p t g e", g=EGROUPS, e=EGROUPS)
                o1 = w1[:, 512 * t4:512 * t4 + 512].rearrange("p (t g e) -> p t g e", g=EGROUPS, e=EGROUPS)
                s.done(v.tensor_tensor(o0, a, b, ALU.is_gt), False)
                s.done(v.tensor_tensor(o1, a, b, ALU.is_equal), t4 == 3)
            s.done(v.tensor_tensor(w1[:].rearrange("p (t g) -> p t g", g=64), w1[:].rearrange("p (t g) -> p t g", g=64),
                                   less[:].rearrange("p g e -> p (g e)").unsqueeze(1).broadcast_to([P, TILES, 64]), ALU.mult))
            s.done(v.tensor_tensor(w0[:], w0[:], w1[:], ALU.add))
            s.done(v.tensor_reduce(rank[:], w0[:].rearrange("p (g e) -> p g e", e=EGROUPS), AX.X, ALU.add))
            s.done(v.tensor_scalar(rank[:], rank[:], float(TOP_GROUPS), None, ALU.is_lt))
            s.done(v.tensor_tensor(sfc[:].rearrange("p (g e) -> p g e", e=EPG), q,
                                   rank[:].unsqueeze(2).broadcast_to([P, G, EPG]), ALU.mult))
            for t in range(TILES):
                s.done(v.max(top[:, t, :], per_tile(sfc)[:, t, :]), t == TILES - 1)
            for t in range(TILES):
                s.done(v.match_replace(out=per_tile(w0)[:, t, :], in_to_replace=top[:, t, :], in_values=per_tile(sfc)[:, t, :],
                                       imm_value=TAKEN), t == TILES - 1)
            s.done(v.scalar_tensor_tensor(w1[:], w0[:], TAKEN / 2, lg[:], ALU.is_lt, ALU.mult))
            s.done(v.tensor_reduce(den[:], per_tile(w1), AX.X, ALU.add))
            s.done(v.tensor_scalar(den[:], den[:], 1e-20, None, ALU.add))
            s.done(v.reciprocal(rden[:], den[:]))
            s.done(v.tensor_tensor(per_tile(w1), per_tile(w1), rden[:].unsqueeze(2).broadcast_to([P, TILES, EXPERTS]), ALU.mult))
            s.done(v.tensor_scalar(w1[:], w1[:], ROUTED_SCALE, None, ALU.mult))
            part = lambda i: parts[:, :, :, i, :].rearrange("p t g e -> p (t g) e")
            half = lambda t: t[:].rearrange("p (t e) -> p t e", e=EHALF)
            s.done(v.tensor_copy(part(0), half(w1)))
            s.done(v.tensor_tensor(half(w0), half(w1), part(0), ALU.subtract))
            s.done(v.tensor_copy(part(1), half(w0)))
            s.done(v.tensor_tensor(half(w1), half(w0), part(1), ALU.subtract))
            v.tensor_copy(part(2), half(w1)).then_inc(cut, 1)

            def keep(c, k):
                dve.wait_ge(tr_done, c + 1)
                v.tensor_copy(T["rw"][0:PARTS * EHALF, 1, ds(c * CHUNK, CHUNK)], ps[0:PARTS * EHALF, 3 + 2 * (k % 2), :])\
                    .then_inc(tr_kept[1], 1)

            with dve.Fori(0, CHUNKS // 2) as i:
                keep(2 * i, 0)
                keep(2 * i + 1, 1)


ROUTED_TILES = EXPERTS * HIDDEN // P
SHARED_TILES, SHARED_ROWS = 2, HIDDEN
HT = ROUTED_TILES + SHARED_TILES
HALF_TILES = ROUTED_TILES // 2
LAG = 3
AHEAD = 3
HIDDEN_ALL = EXPERTS * HIDDEN + SHARED_TILES * SHARED_ROWS
KD = 2 * DEPTH
LT = SEQ // P
QKV1 = 3 * D + HEADS
DPFP_EPS = 1e-6
E1 = 9
NE1 = E1 - 1
F1 = 512
F1T = F1 // P
T1 = NE1 * F1T
LAG1 = 3
RING1 = 4
SEL = HALF_TILES * P // 2
TOP1 = 2
EARLY_LOADS = ("wqkv", "wo", "wr", "ident_bf", "b_r1", "less9", "sel1")
FFN0_LOADS = len(EARLY_LOADS) + 5
ROUTER_STEPS = 16

WG, WU, WD = 0, HIDDEN_ALL, 2 * HIDDEN_ALL
WEIGHTS = 2 * HIDDEN_ALL + HT * D
FREE_G = (HIDDEN_ALL - T1 * P) // P


def w1_low(j):
    return WG + P * j


def w2_low(j):
    return WU + P * j


def w2_high(j):
    return WD + P * j


def w1_high(j):
    if j < FREE_G:
        return WG + P * (T1 + j)
    if j < 2 * FREE_G:
        return WU + P * (T1 + j - FREE_G)
    return WD + P * (T1 + j - 2 * FREE_G)


def weights_at(T, at, width, rounded=""):
    tensor, start = (T["w_gu" + rounded], at) if at < WD else (T["w_d" + rounded], at - WD)
    return tensor[:, start:start + width]


NULL_AT = WD + P * (2 * T1 - 2 * FREE_G)


def experts(nc, T, A, out):
    x_fm, h_fm, ps, rw = T["x_fm"], T["h_fm"], T["psum"], T["rw"]
    wqkv, wo, wr = (T[k] for k in ("wqkv", "wo", "wr"))
    sel = T["sel"]
    with ExitStack() as ctx:
        def sb(name, shape, dt=F32):
            return ctx.enter_context(nc.sbuf_tensor(name, shape, dt))

        def sem(name):
            return ctx.enter_context(nc.semaphore("e_" + name))

        act_g = gu = sb("e_gu", [P, 2, CHUNK])
        hm = sb("e_hm", [P, 4, CHUNK])
        h_hi, h_lo = sb("e_hhi", [P, CHUNK], F32R), sb("e_hlo", [P, CHUNK], F32R)
        ring = sb("e_ring", [P, 4 * CHUNK], F32R)
        w_slots = [ring[:, s * CHUNK:(s + 1) * CHUNK] for s in range(4)] + [T["sel_buf_r"][:, SEL:SEL + CHUNK]]
        m_lo = ring[:].rearrange("p (s c) -> p s c", c=CHUNK)
        m_hi = T["sel_buf_r"][:].rearrange("p (s c) -> p s c", c=CHUNK)
        null = weights_at(T, NULL_AT, CHUNK)
        xc = sb("e_x", [P, CHUNK])
        hc = y_fm = sb("e_h", [P, CHUNK])
        nt = sb("e_nt", [P, CT, D])
        upd = nt[:].rearrange("p t d -> p (t d)")
        y_tm = sb("e_y", [P, CT, D])
        phi = sb("e_phi", [P, 2, CT, HEADS, KD])
        psum_r = prec = sb("e_prec", [P, 2 * CT * HEADS])
        vv = sb("e_v", [P, CT, D])
        beta = sb("e_beta", [P, CT, HEADS])
        state = sb("e_state", [P, LT, HEADS, DEPTH, KD])
        prod = sb("e_prod", [P, LT, HEADS, DEPTH, KD])
        vbar = sb("e_vbar", [P, LT, D])
        u = vbar
        raw = prod[:, 0].rearrange("p h v k -> p (h v k)").rearrange("p (q a k) -> p q a k", q=2, k=KD)
        mx, sm, rs = (sb(f"e_{n}", [P, CT]) for n in ("mx", "sm", "rs"))
        pr, w0, w1 = (sb(f"e_{n}", [P, CT, E1]) for n in ("pr", "w0", "w1"))
        rank = w1
        above = nt[:].rearrange("p t d -> p (t d)")[:, 0:CT * E1 * E1]
        equal = xc[:, 0:CT * E1 * E1]
        parts = sb("e_parts", [P, CT, PARTS, E1], BF16)
        g1 = rw[:, 0, :]
        GB, UB, RB, ACC, SIDE = (0, 1), (2, 3), (4, 5), 6, 7
        HB, NB = GB, 2
        side = ps[:, SIDE, :]
        ln_a = LayerNorm(nc, ctx, "e_lna", T, xc, hc, nt, SIDE, 2)
        ln_b = LayerNorm(nc, ctx, "e_lnb", T, xc, hc, nt, SIDE, 3)

        wh_done = sem("wh_done")
        wl_done = sem("wl_done")
        hh_done = sem("hh_done")
        hl_done = sem("hl_done")
        gate_done = sem("gate_done")
        ur_done = sem("ur_done")
        silu_done = sem("silu_done")
        gu_done = sem("gu_done")
        hm_done = sem("hm_done")
        acc_done = sem("acc_done")
        x_new = sem("x_new")
        x_kept = sem("x_kept")
        pr_done = sem("pr_done")
        pr_kept = sem("pr_kept")
        beta_done = sem("beta_done")
        pool_step = sem("pool_step")
        u_step = sem("u_step")
        state_zero = sem("state_zero")
        phi_sum = sem("phi_sum")
        vbar_done = sem("vbar_done")
        y_done = sem("y_done")
        yt_done = sem("yt_done")
        yfm_done = sem("yfm_done")
        wo_done = sem("wo_done")
        upd_done = sem("upd_done")
        xb_done = sem("xb_done")
        xb_kept = sem("xb_kept")
        h1_kept = sem("h1_kept")
        lg1_done = sem("lg1_done")
        r_step = sem("r_step")
        shifted = sem("shifted")
        exp_done = sem("exp_done")
        cut = sem("cut")
        g1t_done = sem("g1t_done")
        g1_kept = sem("g1_kept")
        w1h_done, w1l_done, w2h_done, w2l_done = (sem(n) for n in ("w1h_done", "w1l_done", "w2h_done", "w2l_done"))
        up1_done = sem("up1_done")
        gelu_done = sem("gelu_done")
        r1_done = sem("r1_done")
        rn_done = sem("rn_done")
        nh_done = sem("nh_done")
        m_done = sem("m_done")
        mh_done, ml_done = sem("mh_done"), sem("ml_done")
        acc1_done = sem("acc1_done")
        acc1_read = sem("acc1_read")
        x_done = sem("x_done")
        stored = sem("stored")
        block = ctx.enter_context(nc.Block())

        PHI, NORM, PRODUCTS = 2, 3, 8
        KEY, OUTER, ADD, QUERY = (1, 2), (3, 6), (4, 7), (5, 8)
        POOL_STEPS = NORM + CB * PRODUCTS

        def pool_at(m, s, p):
            return POOL_STEPS * m + NORM + PRODUCTS * s + p

        V_SLOT = {22: (0, 0, 0), 23: (0, 0, 1), 25: (0, 1, 0), 26: (0, 1, 1),
                  38: (1, 0, 0), 39: (1, 0, 1), 41: (1, 1, 0), 42: (1, 1, 1)}
        Y_SLOT = {29: (0, 0, 0), 30: (0, 0, 1), 33: (0, 1, 0), 35: (0, 1, 1)}
        Y_LAST = {0: (1, 0, 0), 2: (1, 0, 1), 8: (1, 1, 0), 10: (1, 1, 1)}

        X_SLOT = 1

        def live(k):
            return {"a": 0 <= k - 1 < CHUNKS, "b": 0 <= k - 2 < CHUNKS}

        SPREAD = HT + 10
        def tile_of(p):
            return int(1.65 * p) if p <= SPREAD else int(1.65 * SPREAD) + p - SPREAD

        PEELED1 = 4
        assert tile_of(HT + 43) < T1 * PEELED1

        def beside(q, j, jobs):
            for p in range(2 * HT):
                if tile_of(p) == T1 * q + j:
                    jobs(CHUNKS + p // HT, CHUNKS + p // HT, p % HT)

        def run(eng, block0, block1):
            for c in range(3):
                block0(c, c)
            with eng.Fori(3, CHUNKS - 1) as c:
                block0(c, 3)
            block0(CHUNKS - 1, CHUNKS - 1)
            for q in range(PEELED1):
                block1(q, q)
            with eng.Fori(PEELED1, CHUNKS) as q:
                block1(q, PEELED1)

        W2_FIRST = 2
        def w2_tiles(j):
            i = j - W2_FIRST
            return [] if i < 0 else list(range(2 * i, min(2 * i + 2, j + 1))) if 2 * i < j + 1 else [j]

        def rows(j):
            return P if j < ROUTED_TILES else SHARED_ROWS

        def slot(j):
            return 3 if j == HT - 1 else j % 3

        def w_slot(j, i, w=slice(0, 2)):
            s = j % 4 if j < HT - 10 else (j - (HT - 10)) % 5
            return w_slots[s].rearrange("p (i w c) -> p i w c", i=2, w=2)[:, i, w, 0:rows(j)]

        def gate_up(j):
            at = P * j if j < ROUTED_TILES else P * ROUTED_TILES + SHARED_ROWS * (j - ROUTED_TILES)
            return T["w_gu"][:].rearrange("p (w c) -> p w c", w=2)[:, :, at:at + rows(j)]

        def part(at):
            return weights_at(T, at, P, "_r")

        @block.sync
        def _(sp):
            sp.wait_ge(wl_done, HT * (CHUNKS - 1) + T1)
            sp.dma_start(weights_at(T, w1_low(0), T1 * P), A["w1"]).then_inc(T["ffn1_loaded"], 16)
            sp.dma_start(weights_at(T, w2_low(0), T1 * P), A["w2"]).then_inc(T["ffn1_loaded"], 16)
            for c in range(CHUNKS):
                sp.wait_ge(x_done, c + 1)
                sp.dma_start(cols(out, c), cols(x_fm, c)).then_inc(stored, 16)
            sp.wait_ge(stored, 16 * CHUNKS)

        @block.tensor
        def _(pe):
            pe.wait_ge(T["ffn0_loaded"], 16 * FFN0_LOADS)

            def three(out, w_hi, w_lo, x_hi, x_lo, first=True, last=True):
                pe.matmul(out, w_hi, x_hi, start=first, stop=False)
                pe.matmul(out, w_lo, x_hi, start=False, stop=False)
                return pe.matmul(out, w_hi, x_lo, start=False, stop=last)

            def down(c, j, k):
                if j == 0 and k > 0:
                    pe.wait_ge(x_new, c)
                pe.wait_ge(hm_done, HT * c + j + 1)
                mm = pe.matmul(ps[:, ACC, :], weights_at(T, WD + P * j, P)[0:rows(j), :], hm[0:rows(j), slot(j), :],
                               start=(j == 0), stop=(j == HT - 1))
                if j == HT - 1:
                    mm.then_inc(acc_done, 1)

            def tile(c, j, k):
                r, g = rows(j), HT * c + j
                if j == 0 and k > 0:
                    down(c - 1, HT - 3, k)
                    down(c - 1, HT - 2, k)
                if j == 0:
                    pe.wait_ge(hl_done, c + 1)
                pe.wait_ge(wl_done, g + 1)
                if k > 0 or j >= 2:
                    pe.wait_ge(silu_done, g - 1)
                three(ps[0:r, GB[j % 2], :], w_slot(j, 0, 0), w_slot(j, 1, 0), h_hi[:], h_lo[:]).then_inc(gate_done, 1)
                if j >= LAG:
                    down(c, j - LAG, k)
                elif k > 0 and j == 1:
                    down(c - 1, HT - 1, k)
                if k > 0 or j >= 2:
                    pe.wait_ge(hm_done, g - 1)
                mm = three(ps[0:r, UB[j % 2], :], w_slot(j, 0, 1), w_slot(j, 1, 1), h_hi[:], h_lo[:])
                if j < ROUTED_TILES:
                    mm = pe.matmul(ps[:, RB[j % 2], :], sel[0:PARTS * EHALF, j % HALF_TILES, :],
                                   rw[0:PARTS * EHALF, j // HALF_TILES, ds(c * CHUNK, CHUNK)], start=True, stop=True)
                mm.then_inc(ur_done, 1)

            def project(m, t):
                if t == 0:
                    pe.wait_ge(ln_a.h, m + 1)
                else:
                    pe.wait_ge(pr_kept, CT * m + t)
                pe.matmul(side[:, 0:QKV1], hc[:, t * P:(t + 1) * P], wqkv[:], start=True, stop=True).then_inc(pr_done, 1)

            def jobs(c, k, j):
                f = live(k)
                if f["a"]:
                    m = c - 1
                    if j == 4:
                        pe.wait_ge(x_new, m + 1)
                        if k > 1:
                            pe.wait_ge(beta_done, m)
                        if k > 2:
                            pe.wait_ge(g1_kept, m - 1)
                        ln_a.pe_x(pe)
                    if j == 10:
                        ln_a.pe_n(pe, m)
                    if 12 <= j < 12 + CT:
                        project(m, j - 12)
                if f["b"]:
                    m = c - 2
                    if j == 17:
                        if f["a"]:
                            pe.wait_ge(beta_done, c)
                        else:
                            pe.wait_ge(g1_kept, m)
                        pe.wait_ge(y_done, 2 * (CT * m + CT))
                        for t in range(CT):
                            mm = pe.transpose(side[:, t * P:(t + 1) * P], y_tm[:, t, :], T["ident"][:])
                        mm.then_inc(yt_done, 1)
                    if j == 19:
                        pe.wait_ge(yfm_done, m + 1)
                        pe.matmul(side, wo[:], y_fm[:], start=True, stop=True).then_inc(wo_done, 1)
                    if j == 24:
                        pe.wait_ge(xb_done, m + 1)
                        ln_b.pe_x(pe)
                    if j == 31:
                        ln_b.pe_n(pe, m)
                    if j == 33:
                        pe.wait_ge(ln_b.h, m + 1)
                        for t in range(CT):
                            mm = pe.matmul(side[:, t * E1:(t + 1) * E1], hc[:, t * P:(t + 1) * P], wr[:], start=True, stop=True)
                        mm.then_inc(lg1_done, 1)
                    if j == 43:
                        pe.wait_ge(cut, m + 1)
                        for t in range(CT):
                            mm = pe.matmul(side[0:PARTS * E1, t * P:(t + 1) * P], parts[:, t, :, :].rearrange("p i e -> p (i e)"),
                                           T["ident_bf"][:], start=True, stop=True)
                        mm.then_inc(g1t_done, 1)

            def block0(c, k):
                for j in range(HT):
                    jobs(c, k, j)
                    tile(c, j, k)

            def spread(c, e):
                return pe.matmul(ps[:, NB if e == NE1 else RB[e % 2], :], T["sel1"][0:PARTS * E1, e, :],
                                 g1[0:PARTS * E1, ds(c * CHUNK, CHUNK)], start=True, stop=True)

            def down1(c, j, k):
                if j == 0:
                    if k > 0:
                        pe.wait_ge(acc1_read, c)
                    else:
                        pe.wait_ge(x_new, CHUNKS)
                if k == 0:
                    pe.wait_ge(w2l_done, j + 1)
                pe.wait_ge(ml_done, T1 * c + j + 1)
                s = j % RING1
                mm = three(ps[:, ACC, :], part(w2_high(j)), part(w2_low(j)), m_hi[:, s, :], m_lo[:, s, :], j == 0, j == T1 - 1)
                if j == T1 - 1:
                    mm.then_inc(acc1_done, 1)

            def up1(c, j, k):
                e, g = j // F1T, T1 * c + j
                if j == 0:
                    pe.wait_ge(hl_done, CHUNKS + c + 1)
                if k == 0:
                    pe.wait_ge(w1l_done, j + 1)
                    if j < 2:
                        pe.wait_ge(silu_done, HT * CHUNKS - 1 + j)
                if j % F1T == 0 and (k > 0 or e >= 2):
                    pe.wait_ge(m_done, g - F1T)
                if j == 0 and k > 0:
                    pe.wait_ge(nh_done, c)
                if k > 0 or j >= 2:
                    pe.wait_ge(gelu_done, g - 1)
                three(ps[:, HB[j % 2], :], part(w1_high(j)), part(w1_low(j)), h_hi[:], h_lo[:]).then_inc(up1_done, 1)

            def block1(c, k):
                for j in range(T1):
                    beside(c, j, jobs) if k < PEELED1 else None
                    if k == 0 and j == 0:
                        down(CHUNKS - 1, HT - 3, CHUNKS)
                        down(CHUNKS - 1, HT - 2, CHUNKS)
                    if k == 0 and j == 1:
                        down(CHUNKS - 1, HT - 1, CHUNKS)
                    if j > 0:
                        up1(c, j, k)
                    if k == 0 and j < LAG1:
                        pass
                    elif j >= LAG1:
                        down1(c, j - LAG1, k)
                    elif k > 0:
                        down1(c - 1, T1 - LAG1 + j, k - 1)
                    if j == 0:
                        up1(c, j, k)
                    if j == (1 if k == 0 else 0):
                        if k == 0:
                            pe.wait_ge(hm_done, HT * CHUNKS)
                        spread(c, NE1).then_inc(rn_done, 1)
                        spread(c, 0).then_inc(r1_done, 1)
                    elif j > 0 and j % F1T == 0:
                        spread(c, j // F1T).then_inc(r1_done, 1)

            run(pe, block0, block1)
            for j in range(T1 - LAG1, T1):
                down1(CHUNKS - 1, j, 1)

        @block.scalar
        def _(act):
            a = nc.scalar.activation

            def h_high(n, c):
                a(h_hi[:], cols(h_fm, c), ACT.Copy).then_inc(hh_done, 1)

            def weights_high(j):
                a(w_slot(j, 0), gate_up(j), ACT.Copy).then_inc(wh_done, 1)

            def w1_highs(j):
                if j == 0:
                    act.wait_ge(T["ffn1_loaded"], 32)
                if j in (0, 2 * FREE_G):
                    act.wait_ge(wl_done, HT * CHUNKS) if j == 0 else act.wait_ge(acc_done, CHUNKS)
                a(part(w1_high(j)), weights_at(T, w1_low(j), P), ACT.Copy).then_inc(w1h_done, 1)

            def jobs(c, k, j):
                f = live(k)
                if f["a"]:
                    m = c - 1
                    if j == 3:
                        act.wait_ge(x_new, m + 1)
                        a(cols(x_fm, m), xc[:], ACT.Copy).then_inc(x_kept, 1)
                    if j == 6:
                        ln_a.act_std(act, m)
                    if j == 10:
                        if k > 2:
                            act.wait_ge(h1_kept, m - 1)
                        ln_a.act_h(act, m)
                    if 12 <= j < 12 + CT:
                        t = j - 12
                        if t == 0 and k > 1:
                            act.wait_ge(y_done, 2 * CT * m)
                            act.wait_ge(pool_step, POOL_STEPS * m)
                        act.wait_ge(pr_done, CT * m + t + 1)
                        qk = side[:, 0:2 * D].rearrange("p (q h d) -> p q h d", q=2, d=DEPTH)
                        a(raw[:, :, HEADS * t:HEADS * (t + 1), 0:DEPTH], qk, ACT.Relu)
                        a(raw[:, :, HEADS * t:HEADS * (t + 1), DEPTH:KD], qk, ACT.Relu, scale=-1.0)
                        a(vv[:, t, :], side[:, 2 * D:3 * D], ACT.Copy)
                        a(beta[:, t, :], side[:, 3 * D:QKV1], ACT.Copy).then_inc(pr_kept, 1)
                        if t == CT - 1:
                            act.wait_ge(pr_kept, CT * m + CT)
                            a(beta[:], beta[:], ACT.Sigmoid).then_inc(beta_done, 1)
                if f["b"]:
                    m = c - 2
                    if j == 17:
                        act.wait_ge(yt_done, m + 1)
                        a(y_fm[:], side, ACT.Copy).then_inc(yfm_done, 1)
                    if j == 19:
                        act.wait_ge(wo_done, m + 1)
                        for i in range(CB):
                            b = CB * m + i
                            ins = a(upd[:, i * SEQ:(i + 1) * SEQ], side[:, i * SEQ:(i + 1) * SEQ], ACT.Identity,
                                    bias=T["ga_bo"][:, ds(b, 1)], scale=T["gate"][:, 2, ds(b, 1)])
                        ins.then_inc(upd_done, 1)
                    if j == 23:
                        act.wait_ge(xb_done, m + 1)
                        a(cols(x_fm, m), xc[:], ACT.Copy).then_inc(xb_kept, 1)
                    if j == 26:
                        ln_b.act_std(act, m)
                    if j == 31:
                        ln_b.act_h(act, m)
                    if j == 35:
                        act.wait_ge(shifted, m + 1)
                        a(pr[:], w0[:], ACT.Exp).then_inc(exp_done, 1)
                    if j == 43:
                        act.wait_ge(g1t_done, m + 1)
                        a(g1[0:PARTS * E1, ds(m * CHUNK, CHUNK)], side[0:PARTS * E1, :], ACT.Copy).then_inc(g1_kept, 1)

            def block0(c, k):
                for j in range(HT):
                    r, g = rows(j), HT * c + j
                    act.wait_ge(gate_done, g + 1)
                    if k > 0 or j >= 2:
                        act.wait_ge(hm_done, g - 1)
                    a(act_g[0:r, j % 2, :], ps[0:r, GB[j % 2], :], ACT.Silu).then_inc(silu_done, 1)
                    if j == HT - 1:
                        act.wait_ge(ur_done, HT * (c + 1))
                        h_high(c + 1, c + 1 if k < CHUNKS - 1 else 0)
                    if k < CHUNKS - 1 or j < HT - AHEAD:
                        weights_high((j + AHEAD) % HT)
                    else:
                        w1_highs(j + AHEAD - HT)
                    jobs(c, k, j)

            def hidden_high(c, j):
                act.wait_ge(m_done, T1 * c + j + 1)
                a(m_hi[:, j % RING1, :], hm[:, j % 2, :], ACT.Copy).then_inc(mh_done, 1)

            def block1(c, k):
                for j in range(T1):
                    g = T1 * c + j
                    if j == 0 and k > 0:
                        act.wait_ge(up1_done, g)
                        h_high(CHUNKS + c, c)
                    act.wait_ge(up1_done, g + 1)
                    if k > 0 or j >= 2:
                        act.wait_ge(m_done, g - 1)
                    else:
                        act.wait_ge(hm_done, HT * CHUNKS)
                    a(gu[:, j % 2, :], ps[:, HB[j % 2], :], ACT.Gelu).then_inc(gelu_done, 1)
                    if k == 0:
                        if j + AHEAD < T1:
                            w1_highs(j + AHEAD)
                        if j == W2_FIRST:
                            act.wait_ge(acc_done, CHUNKS)
                        for i in w2_tiles(j):
                            a(part(w2_high(i)), weights_at(T, w2_low(i), P), ACT.Copy).then_inc(w2h_done, 1)
                    if j > 0:
                        hidden_high(c, j - 1)
                    elif k > 0:
                        hidden_high(c - 1, T1 - 1)
                    beside(c, j, jobs) if k < PEELED1 else None

            act.wait_ge(T["ffn0_loaded"], 16 * FFN0_LOADS)
            for j in range(AHEAD):
                weights_high(j)
            h_high(0, 0)
            run(act, block0, block1)
            hidden_high(CHUNKS - 1, T1 - 1)

        @block.vector
        def _(dve):
            v = nc.vector

            def h_low(n, c):
                dve.wait_ge(hh_done, n + 1)
                v.tensor_tensor(h_lo[:], cols(h_fm, c), h_hi[:].bitcast(F32), ALU.subtract).then_inc(hl_done, 1)

            def weights_low(n, j):
                dve.wait_ge(wh_done, n)
                v.tensor_tensor(w_slot(j, 1), gate_up(j), w_slot(j, 0).bitcast(F32), ALU.subtract).then_inc(wl_done, 1)

            def low_of(low, high, high_done, low_done, j):
                dve.wait_ge(high_done, j + 1)
                v.tensor_tensor(part(low(j)), weights_at(T, low(j), P), part(high(j)).bitcast(F32), ALU.subtract).then_inc(low_done, 1)

            def product_sum(out, z, half):
                at = slice(half * D // 2, (half + 1) * D // 2)
                return v.tensor_reduce(out[:, at], prod[:, z].rearrange("p h v k -> p (h v) k")[:, at], AX.X, ALU.add)

            def y_sum(m, s, z, half):
                dve.wait_ge(pool_step, pool_at(m, s, QUERY[z]))
                product_sum(y_tm[:, LT * s + z, :], z, half).then_inc(y_done, 1)

            def router(m):
                s = Steps(dve, r_step, ROUTER_STEPS * m)
                over = lambda ap: ap.unsqueeze(2).broadcast_to([P, CT, E1])
                lg = side[:, 0:CT * E1].rearrange("p (t e) -> p t e", e=E1)
                s.done(v.tensor_tensor(w1[:], lg, T["b_r1"][:].unsqueeze(1).broadcast_to([P, CT, E1]), ALU.add))
                s.done(v.tensor_reduce(mx[:], w1[:], AX.X, ALU.max))
                v.tensor_tensor(w0[:], w1[:], over(mx[:]), ALU.subtract).then_inc(shifted, 1)
                return s

            def router_gates(m, s):
                over = lambda ap: ap.unsqueeze(2).broadcast_to([P, CT, E1])
                dve.wait_ge(exp_done, m + 1)
                s.done(v.tensor_reduce(sm[:], pr[:], AX.X, ALU.add))
                s.done(v.reciprocal(rs[:], sm[:]))
                s.done(v.tensor_tensor(pr[:], pr[:], over(rs[:]), ALU.mult))
                pa = pr[:].unsqueeze(2).broadcast_to([P, CT, E1, E1])
                pb = pr[:].unsqueeze(3).broadcast_to([P, CT, E1, E1])
                pairs = lambda ap: ap.rearrange("p (t g e) -> p t g e", g=E1, e=E1)
                s.done(v.tensor_tensor(pairs(above), pa, pb, ALU.is_gt), False)
                s.done(v.tensor_tensor(pairs(equal), pa, pb, ALU.is_equal))
                per = lambda ap: ap.rearrange("p (t g) -> p t g", t=CT)
                s.done(v.tensor_tensor(per(equal), per(equal),
                                       T["less9"][:].rearrange("p g e -> p (g e)").unsqueeze(1).broadcast_to([P, CT, E1 * E1]), ALU.mult))

            def router_rank(s):
                s.done(v.tensor_tensor(above, above, equal, ALU.add))
                s.done(v.tensor_reduce(rank[:].rearrange("p t e -> p (t e)"), above.rearrange("p (g e) -> p g e", e=E1), AX.X, ALU.add))

            def router_cut(s):
                s.done(v.scalar_tensor_tensor(w0[:], rank[:], float(TOP1), pr[:], ALU.is_lt, ALU.mult))
                s.done(v.tensor_copy(parts[:, :, 0, :], w0[:]))
                s.done(v.tensor_tensor(w1[:], w0[:], parts[:, :, 0, :], ALU.subtract))
                s.done(v.tensor_copy(parts[:, :, 1, :], w1[:]))
                s.done(v.tensor_tensor(w0[:], w1[:], parts[:, :, 1, :], ALU.subtract))
                s.done(v.tensor_copy(parts[:, :, 2, :], w0[:]))
                v.sem_inc(cut, 1)
                assert s.n == ROUTER_STEPS

            held = {}

            def jobs(c, k, j):
                f = live(k)
                if f["a"]:
                    m = c - 1
                    if j == X_SLOT:
                        dve.wait_ge(acc_done, m + 1)
                        if k > 1:
                            dve.wait_ge(ln_a.x_tm, m)
                        if k > 2:
                            dve.wait_ge(xb_kept, m - 1)
                        for i in range(CB):
                            b = CB * m + i
                            ins = v.scalar_tensor_tensor(xc[:, i * SEQ:(i + 1) * SEQ], ps[:, ACC, i * SEQ:(i + 1) * SEQ],
                                                         T["gate"][:, 1, ds(b, 1)], cols(x_fm, b, SEQ), ALU.mult, ALU.add)
                        ins.then_inc(x_new, 1)
                    if j == 4:
                        ln_a.dve_stats(dve, m)
                    if j == 7:
                        ln_a.dve_norm(dve, m)
                    if j in (18, 19):
                        dve.wait_ge(pool_step, POOL_STEPS * m + PHI)
                        at = slice((j - 18) * CT * HEADS, (j - 17) * CT * HEADS)
                        v.tensor_reduce(psum_r[:, at], phi[:].rearrange("p q t h k -> p (q t h) k")[:, at], AX.X, ALU.add).then_inc(phi_sum, 1)
                    if j == 19:
                        dve.wait_ge(phi_sum, 4 * m + 2)
                        v.tensor_scalar(psum_r[:], psum_r[:], DPFP_EPS, None, ALU.add).then_inc(phi_sum, 1)
                        dve.wait_ge(phi_sum, 4 * m + 3)
                        v.reciprocal(prec[:], psum_r[:]).then_inc(phi_sum, 1)
                    if j in V_SLOT:
                        s, z, half = V_SLOT[j]
                        dve.wait_ge(pool_step, pool_at(m, s, KEY[z]))
                        product_sum(vbar[:, z, :], z, half).then_inc(vbar_done, 1)
                    if j in Y_SLOT:
                        if j == min(Y_SLOT) and k > 1:
                            dve.wait_ge(yt_done, m)
                        y_sum(m, *Y_SLOT[j])
                if f["b"]:
                    m = c - 2
                    if j in Y_LAST:
                        y_sum(m, *Y_LAST[j])
                    if j == 21:
                        dve.wait_ge(upd_done, m + 1)
                        if k > 2:
                            dve.wait_ge(ln_b.x_tm, m)
                        dve.wait_ge(x_kept, m + 2 if f["a"] else CHUNKS)
                        v.tensor_tensor(xc[:], cols(x_fm, m), upd, ALU.add).then_inc(xb_done, 1)
                    if j == 24:
                        ln_b.dve_stats(dve, m)
                    if j == 27:
                        ln_b.dve_norm(dve, m)
                    if j == 32:
                        dve.wait_ge(ln_b.h, m + 1)
                        v.tensor_copy(cols(h_fm, m), hc[:]).then_inc(h1_kept, 1)
                    if j == 34:
                        dve.wait_ge(lg1_done, m + 1)
                        held["router"] = router(m)
                    if j == 36:
                        router_gates(m, held["router"])
                    if j == 37:
                        router_rank(held["router"])
                    if j == 40:
                        router_cut(held["router"])

            def block0(c, k):
                for j in range(HT):
                    r, g = rows(j), HT * c + j
                    if j == X_SLOT:
                        jobs(c, k, j)
                    dve.wait_ge(silu_done, g + 1)
                    dve.wait_ge(ur_done, g + 1)
                    product = gu[0:r, j % 2, :] if j < ROUTED_TILES else hm[0:r, slot(j), :]
                    ins = v.tensor_tensor(product, ps[0:r, UB[j % 2], :], act_g[0:r, j % 2, :], ALU.mult)
                    if j < ROUTED_TILES:
                        ins.then_inc(gu_done, 1)
                        dve.wait_ge(gu_done, ROUTED_TILES * c + j + 1)
                        v.tensor_tensor(hm[:, slot(j), :], ps[:, RB[j % 2], :], gu[:, j % 2, :], ALU.mult).then_inc(hm_done, 1)
                    else:
                        ins.then_inc(hm_done, 1)
                    if j == HT - 1:
                        h_low(c + 1, c + 1 if k < CHUNKS - 1 else 0)
                    if k < CHUNKS - 1 or j < HT - AHEAD:
                        weights_low(g + AHEAD + 1, (j + AHEAD) % HT)
                    else:
                        low_of(w1_low, w1_high, w1h_done, w1l_done, j + AHEAD - HT)
                    if j != X_SLOT:
                        jobs(c, k, j)

            def hidden_low(c, j):
                dve.wait_ge(mh_done, T1 * c + j + 1)
                v.tensor_tensor(m_lo[:, j % RING1, :], hm[:, j % 2, :], m_hi[:, j % RING1, :].bitcast(F32), ALU.subtract).then_inc(ml_done, 1)

            def result(m):
                dve.wait_ge(acc1_done, m + 1)
                v.tensor_tensor(null, ps[:, ACC, :], null, ALU.add).then_inc(acc1_read, 1)
                dve.wait_ge(acc1_read, m + 1)
                for i in range(CB):
                    b = CB * m + i
                    x = cols(x_fm, b, SEQ)
                    ins = v.scalar_tensor_tensor(x, null[:, i * SEQ:(i + 1) * SEQ], T["gate"][:, 3, ds(b, 1)], x, ALU.mult, ALU.add)
                ins.then_inc(x_done, 1)

            def block1(c, k):
                for j in range(T1):
                    e, g = j // F1T, T1 * c + j
                    if j == 0 and k > 0:
                        h_low(CHUNKS + c, c)
                    dve.wait_ge(gelu_done, g + 1)
                    dve.wait_ge(r1_done, NE1 * c + e + 1)
                    if k > 0 or j >= 2:
                        dve.wait_ge(ml_done, g - 1)
                    v.tensor_tensor(hm[:, j % 2, :], ps[:, RB[e % 2], :], gu[:, j % 2, :], ALU.mult).then_inc(m_done, 1)
                    if k == 0:
                        if j + AHEAD < T1:
                            low_of(w1_low, w1_high, w1h_done, w1l_done, j + AHEAD)
                        for i in w2_tiles(j):
                            low_of(w2_low, w2_high, w2h_done, w2l_done, i)
                    if j > 0:
                        hidden_low(c, j - 1)
                    elif k > 0:
                        hidden_low(c - 1, T1 - 1)
                    if k > 0 and j == LAG1 - 1:
                        result(c - 1)
                    if j == 2 * LAG1:
                        dve.wait_ge(rn_done, c + 1)
                        v.tensor_tensor(null, ps[:, NB, :], cols(h_fm, c), ALU.mult).then_inc(nh_done, 1)
                    beside(c, j, jobs) if k < PEELED1 else None

            for j in range(AHEAD):
                weights_low(j + 1, j)
            h_low(0, 0)
            run(dve, block0, block1)
            hidden_low(CHUNKS - 1, T1 - 1)
            result(CHUNKS - 1)

        @block.gpsimd
        def _(pool):
            tt = nc.gpsimd.tensor_tensor
            nc.gpsimd.memset(state[:], 0.0).then_inc(state_zero, 1)
            pool.wait_ge(state_zero, 1)
            wide = lambda ap: ap.unsqueeze(3).broadcast_to([P, HEADS, DEPTH, KD])
            tall = lambda ap: ap.unsqueeze(2).broadcast_to([P, HEADS, DEPTH, KD])
            heads = lambda ap: ap.rearrange("p (h v) -> p h v", v=DEPTH)

            def chunk(m, first):
                base = POOL_STEPS * m
                pool.wait_ge(pr_kept, CT * m + CT)
                r, o = raw.rearrange("p q a k -> p (q a) k"), phi[:].rearrange("p q t h k -> p (q t h) k")
                tt(o[:, :, 1:KD], r[:, :, 1:KD], r[:, :, 0:KD - 1], ALU.mult).then_inc(pool_step, 1)
                tt(o[:, :, 0], r[:, :, 0], r[:, :, KD - 1], ALU.mult).then_inc(pool_step, 1)
                pool.wait_ge(phi_sum, 4 * m + 4)
                tt(o, o, prec[:].unsqueeze(2).broadcast_to([P, 2 * CT * HEADS, KD]), ALU.mult).then_inc(pool_step, 1)
                pool.wait_ge(pool_step, base + NORM)
                pool.wait_ge(beta_done, m + 1)
                for s in range(CB):
                    at = base + NORM + PRODUCTS * s
                    for z in range(LT):
                        if not (first and s == 0):
                            pool.wait_ge(y_done, 2 * (CT * m + LT * s - LT + z + 1))
                        tt(prod[:, z], state[:, z], tall(phi[:, 1, LT * s + z]), ALU.mult).then_inc(pool_step, 1)
                    for z in range(LT):
                        t = LT * s + z
                        uz, key = u[:, z, :], phi[:, 1, t]
                        pool.wait_ge(vbar_done, 2 * (CT * m + t + 1))
                        tt(uz, vv[:, t, :], vbar[:, z, :], ALU.subtract).then_inc(u_step, 1)
                        pool.wait_ge(u_step, 2 * (CT * m + t) + 1)
                        tt(heads(uz), heads(uz), beta[:, t, :].unsqueeze(2).broadcast_to([P, HEADS, DEPTH]), ALU.mult).then_inc(u_step, 1)
                        pool.wait_ge(u_step, 2 * (CT * m + t) + 2)
                        tt(prod[:, z], wide(heads(uz)), tall(key), ALU.mult).then_inc(pool_step, 1)
                        pool.wait_ge(pool_step, at + OUTER[z])
                        tt(state[:, z], state[:, z], prod[:, z], ALU.add).then_inc(pool_step, 1)
                        pool.wait_ge(pool_step, at + ADD[z])
                        tt(prod[:, z], state[:, z], tall(phi[:, 0, t]), ALU.mult).then_inc(pool_step, 1)
                    pool.wait_ge(pool_step, at + PRODUCTS)

            chunk(0, True)
            with pool.Fori(1, CHUNKS) as m:
                chunk(m, False)


PI_ALL = 2 * DEPTH // 2
NAMES = ("x_fm", "x_tm", "c_fm", "wmod", "w_qk", "b_qk", "w_v", "b_v", "w_fc", "b_fc", "b_o", "ident", "rot", "ident_bf",
         "gate_w", "gate_b", "less8", "wg", "wu", "wd", "sd", "wqkv", "wo", "sel", "wr", "b_r1", "less9", "sel1", "w1", "w2")


def adaln_two_blocks(nc, *args):
    A, out = dict(zip(NAMES, args[:-1])), args[-1]
    with ExitStack() as ctx:
        T = {}

        def sb(name, shape, dt=F32, scope=ctx):
            T[name] = scope.enter_context(nc.sbuf_tensor(name, shape, dt))

        def second_name(name, shape):
            T[name + "_r"] = nc.alloc_sbuf_tensor_at(name + "_r", shape, F32R, offset=nc.sbuf_base - 4 * shape[1])

        for name, shape in dict(x_fm=[P, TOK], h_fm=[P, TOK], ident=[P, P], bq_col=[P, 1], bk_col=[P, 1], bv_col=[P, 1],
                                bfc_col=[P, 1], bo_col=[P, 1], shift=[P, 4, BATCH], scale1=[P, 4, BATCH], gate=[P, 4, BATCH],
                                ga_bfc=[P, BATCH], ga_bo=[P, BATCH], wqkv=[P, QKV1], wo=[P, D], wr=[P, E1], b_r1=[P, E1],
                                less9=[P, E1, E1]).items():
            sb(name, shape)
        sb("ident_bf", [P, P], BF16)
        sb("sel1", [PARTS * E1, E1, P], BF16)
        T["x_tm"] = T["h_fm"]
        T["psum"] = ctx.enter_context(nc.psum_tensor("psum", [P, 8, BANK], F32))
        for name in ("ffn0_loaded", "ffn1_loaded"):
            T[name] = ctx.enter_context(nc.semaphore(name))
        sb("w_gu", [P, WD])
        second_name("w_gu", [P, WD])
        with ExitStack() as first:
            for name, shape in dict(mean=[P, TILES], rstd=[P, TILES], w_qk=[P, 2 * D], w_v=[P, D], w_fc=[P, D]).items():
                sb(name, shape, scope=first)
            setup(nc, T, A)
            attention(nc, T, T["x_fm"], T["x_tm"],
                      (T["scale1"][:, 0, :], T["shift"][:, 0, :], T["gate"][:, 0, :], T["ga_bfc"][:, :]))
        sb("w_d", [P, WEIGHTS - WD])
        second_name("w_d", [P, WEIGHTS - WD])
        sb("sel_buf", [P, RING1 * CHUNK])
        second_name("sel_buf", [P, RING1 * CHUNK])
        T["sel"] = T["sel_buf"][:, 0:SEL].bitcast(BF16).rearrange("p (t r) -> p t r", r=P)
        sb("rw", [P, 2, TOK], BF16)
        route0(nc, T, A)
        experts(nc, T, A, out)


def layout(i):
    bf16 = mybir.dt.np(BF16)
    f = np.ascontiguousarray
    x = i["L0_attn_x"].reshape(TOK, D)
    w, b = i["L0_attn_w_qkv"], i["L0_attn_b_qkv"]
    a = {}
    a["x_fm"] = f(x.T)
    a["x_tm"] = f(x.reshape(TILES, P, D).transpose(1, 0, 2).reshape(P, TOK))
    a["c_fm"] = f(np.stack([i["L0_c"], i["L1_c"]]).transpose(2, 0, 1))
    a["wmod"] = f(np.stack([i["L0_wmod"], i["L1_wmod"]]).transpose(1, 0, 2))
    a["w_qk"] = f(w[:, :2 * D].reshape(D, 2, HEADS, DEPTH).transpose(0, 1, 3, 2).reshape(D, 2 * D))
    a["b_qk"] = f(b[:2 * D].reshape(2, HEADS, DEPTH).transpose(0, 2, 1).reshape(1, 2 * D))
    a["w_v"] = f(w[:, 2 * D:])
    a["b_v"] = f(b[2 * D:].reshape(D, 1))
    a["w_fc"] = i["L0_attn_w_fc"]
    a["b_fc"] = f(i["L0_attn_b_fc"].reshape(D, 1))
    a["b_o"] = f(i["L1_attn_bo"].reshape(D, 1))
    a["ident"] = np.eye(P, dtype=np.float32)
    inv = (1.0 / 10000.0 ** (np.arange(0, DEPTH, 2, dtype=np.float32) / DEPTH)).astype(np.float32)
    ang = (np.arange(HEADS, dtype=np.float32)[:, None] * inv[None, :]).astype(np.float32).T
    a["rot"] = f(np.broadcast_to(np.stack([np.tile(np.cos(ang), (2, 1)), np.tile(np.sin(ang), (2, 1))]), (P, 2, PI_ALL, HEADS)))
    a["ident_bf"] = np.eye(P).astype(bf16)
    a["gate_w"] = f(i["L0_ffn_gate_w"].T)
    a["gate_b"] = f(np.broadcast_to(i["L0_ffn_gate_bias"], (P, EXPERTS)))
    a["less8"] = f(np.broadcast_to(np.tril(np.ones((8, 8), np.float32), -1), (P, 8, 8)))
    for name, w, s in (("wg", "Wg", "Sg"), ("wu", "Wu", "Su")):
        rows = np.concatenate([i["L0_ffn_" + w].reshape(EXPERTS * HIDDEN, D), i["L0_ffn_" + s]])
        a[name] = f(rows.T)
    a["wd"] = f(i["L0_ffn_Wd"].transpose(0, 2, 1).reshape(ROUTED_TILES, P, D).transpose(1, 0, 2).reshape(P, ROUTED_TILES * D))
    a["sd"] = f(i["L0_ffn_Sd"].T.reshape(SHARED_TILES, SHARED_ROWS, D).transpose(1, 0, 2).reshape(SHARED_ROWS, SHARED_TILES * D))
    a["wqkv"] = f(np.concatenate([i["L1_attn_W" + n] for n in "qkvb"], axis=1))
    a["wo"] = i["L1_attn_Wo"]
    owner = (np.arange(HALF_TILES * P) // HIDDEN).reshape(HALF_TILES, P)
    one_hot = (owner[None] == np.arange(EHALF)[:, None, None])
    a["sel"] = f(np.tile(one_hot, (PARTS, 1, 1)).astype(bf16))
    a["wr"] = i["L1_ffn_router_w"]
    a["b_r1"] = f(np.broadcast_to(i["L1_ffn_router_b"], (P, E1)))
    a["less9"] = f(np.broadcast_to(np.tril(np.ones((E1, E1), np.float32), -1), (P, E1, E1)))
    a["sel1"] = f(np.tile(np.broadcast_to(np.eye(E1)[:, :, None], (E1, E1, P)), (PARTS, 1, 1)).astype(bf16))
    a["w1"] = f(i["L1_ffn_w1"].reshape(NE1, D, F1T, P).transpose(1, 0, 2, 3).reshape(D, T1 * P))
    a["w2"] = f(i["L1_ffn_w2"].reshape(NE1, F1T, P, D).transpose(2, 0, 1, 3).reshape(P, T1 * D))
    return a


def kernel(**inputs):
    import concourse.bacc as bacc
    from concourse.bass_utils import run_bass_kernel_spmd

    nc = bacc.Bacc("TRN2", target_bir_lowering=False, num_devices=1)
    placed = layout({name: np.asarray(a) for name, a in inputs.items()})
    arrays = {f"in_{name}": np.ascontiguousarray(placed[name]) for name in NAMES}
    args = [nc.dram_tensor(f"in_{name}", arrays[f"in_{name}"].shape, mybir.dt.from_np(arrays[f"in_{name}"].dtype),
                           kind="ExternalInput").ap() for name in NAMES]
    args.append(nc.dram_tensor("out", (D, TOK), F32, kind="ExternalOutput").ap())
    adaln_two_blocks(nc, *args)
    r = run_bass_kernel_spmd(nc, [arrays], core_ids=[0])
    return np.ascontiguousarray(np.asarray(r.results[0]["out"]).T).reshape(BATCH, SEQ, D)
```
